# Optimizing a Trainium2 kernel written in Bass

```python
import numpy as np
import jax
import jax.numpy as jnp

def _softmax(x, axis=-1):
    return jax.nn.softmax(x, axis=axis)

def _gelu(x):
    return jax.nn.gelu(x, approximate=True)

def _silu(x):
    return jax.nn.silu(x)

def _sigmoid(x):
    return jax.nn.sigmoid(x)

def _layernorm(x, axis=-1, eps=1e-05):
    m = jnp.mean(x, axis=axis, keepdims=True)
    v = jnp.var(x, axis=axis, keepdims=True)
    return (x - m) / jnp.sqrt(v + eps)

def _scatter_add(tgt, idx, src, axis=0):
    return tgt.at[idx].add(src)

def _segment_sum(src, seg, n):
    return jax.ops.segment_sum(src, seg, n)
kernel_name = 'mk_gnn_preln_d4_gnn_r32_d0700b'

def setup_inputs(seed: int=0):
    np.random.seed(seed)
    _w = jnp.asarray

    def _rec_inputs():
        import jax
        import jax.numpy as jnp
        _gk = jax.random.key(seed)
        x = -0.0006008 + 1.001 * jax.random.normal(jax.random.fold_in(_gk, 1), (3125, 256), jnp.float32)
        _s = jax.random.randint(jax.random.fold_in(_gk, 2), (25000,), 0, 3125, jnp.int32)
        _d = jax.random.randint(jax.random.fold_in(_gk, 3), (25000,), 0, 3125, jnp.int32)
        _loop = jnp.arange(3125, dtype=jnp.int32)
        src = jnp.concatenate([_s, _d, _loop])
        dst = jnp.concatenate([_d, _s, _loop])
        _o = jnp.argsort(dst, stable=True)
        src = src[_o]
        dst = dst[_o]
        edge_attr_96 = -4.21973e-05 + 0.999841 * jax.random.normal(jax.random.fold_in(_gk, 13), (53125, 96), jnp.float32)
        edge_weight1 = 0.000937891 + 0.999965 * jax.random.normal(jax.random.fold_in(_gk, 15), (53125, 1), jnp.float32)
        return (x, src, dst, edge_attr_96, edge_weight1)
    x, src, dst, edge_attr_96, edge_weight1 = _rec_inputs()

    def _L0_gnn_setup():
        import jax, jax.numpy as jnp
        import numpy as np
        N_NODES = 10000
        N_EDGES = 10000
        IN_DIM = 256
        OUT_DIM = 256
        LN_EPS = 1e-05
        key = jax.random.key(seed)
        ks = jax.random.split(key, 4)
        x = jax.random.normal(ks[0], (N_NODES, IN_DIM), dtype=jnp.float32)
        edge_index = jax.random.randint(ks[1], (2, N_EDGES), 0, N_NODES, dtype=jnp.int64)
        W_msg = jax.random.normal(ks[2], (2 * IN_DIM, OUT_DIM), dtype=jnp.float32) / np.sqrt(2 * IN_DIM)
        b_msg = jnp.zeros((OUT_DIM,), dtype=jnp.float32)
        W_upd = jax.random.normal(ks[3], (IN_DIM + OUT_DIM, OUT_DIM), dtype=jnp.float32) / np.sqrt(IN_DIM + OUT_DIM)
        b_upd = jnp.zeros((OUT_DIM,), dtype=jnp.float32)
        gamma = jnp.ones((OUT_DIM,), dtype=jnp.float32)
        beta = jnp.zeros((OUT_DIM,), dtype=jnp.float32)
        return {'x': x, 'edge_index': edge_index, 'W_msg': W_msg, 'b_msg': b_msg, 'W_upd': W_upd, 'b_upd': b_upd, 'gamma': gamma, 'beta': beta}
    _L0_gnn_all = _L0_gnn_setup()
    _L0_gnn_in = {k: v for k, v in _L0_gnn_all.items() if k in ('W_msg', 'b_msg', 'W_upd', 'b_upd', 'gamma', 'beta')}
    del _L0_gnn_all

    def _L1_gnn_setup():
        import jax, jax.numpy as jnp
        import numpy as np
        N_NODES = 50000
        N_EDGES = 25000
        EDGE_F = 96
        NODE_F = 256
        GLOB_F = 64
        HIDDEN = 1024
        N_GRAPHS = 8
        MLP_IN = NODE_F + 3 * EDGE_F + GLOB_F
        key = jax.random.key(seed)
        ks = jax.random.split(key, 9)
        x = jax.random.normal(ks[0], (N_NODES, NODE_F), dtype=jnp.float32)
        edge_attr = jax.random.normal(ks[1], (N_EDGES, EDGE_F), dtype=jnp.float32)
        u = jax.random.normal(ks[2], (N_GRAPHS, GLOB_F), dtype=jnp.float32)
        W1 = jax.random.normal(ks[3], (MLP_IN, HIDDEN), dtype=jnp.float32) * (1.0 / np.sqrt(MLP_IN))
        b1 = jax.random.normal(ks[4], (HIDDEN,), dtype=jnp.float32) * 0.01
        W2 = jax.random.normal(ks[5], (HIDDEN, NODE_F), dtype=jnp.float32) * (1.0 / np.sqrt(HIDDEN))
        b2 = jax.random.normal(ks[6], (NODE_F,), dtype=jnp.float32) * 0.01
        edge_index = jax.random.randint(ks[7], (2, N_EDGES), 0, N_NODES, dtype=jnp.int64 if jax.config.jax_enable_x64 else jnp.int32)
        batch = jnp.sort(jax.random.randint(ks[8], (N_NODES,), 0, N_GRAPHS, dtype=jnp.int32))
        return {'x': x, 'edge_attr': edge_attr, 'u': u, 'W1': W1, 'b1': b1, 'W2': W2, 'b2': b2, 'edge_index': edge_index, 'batch': batch}
    _L1_gnn_all = _L1_gnn_setup()
    _L1_gnn_in = {k: v for k, v in _L1_gnn_all.items() if k in ('u', 'W1', 'b1', 'W2', 'b2')}
    del _L1_gnn_all

    def _L2_gnn_setup():
        import jax, jax.numpy as jnp
        import numpy as np
        N = 50000
        E = 25000
        IN = 256
        POS = 16
        H = 4
        D = 64
        D4 = D // 4

        def _xavier(key, shape):
            fan_out, fan_in = (shape[0], shape[1])
            lim = np.sqrt(6.0 / (fan_in + fan_out)).astype(np.float32)
            return jax.random.uniform(key, shape, jnp.float32, -lim, lim)
        key = jax.random.key(seed)
        ks = jax.random.split(key, 10)
        feat = jax.random.normal(ks[0], (N, IN), jnp.float32)
        src = jax.random.randint(ks[1], (E,), 0, N, jnp.int32)
        dst = jax.random.randint(ks[2], (E,), 0, N, jnp.int32)
        cd = IN - POS
        Wc = _xavier(ks[3], (H * D, cd))
        Wp = _xavier(ks[4], (H * D4, POS))
        attn_src = _xavier(ks[5], (H, D)).reshape(1, H, D)
        attn_dst = _xavier(ks[6], (H, D)).reshape(1, H, D)
        pos_attn_src = _xavier(ks[7], (H, D4)).reshape(1, H, D4)
        pos_attn_dst = _xavier(ks[8], (H, D4)).reshape(1, H, D4)
        att_comb = jnp.full((H, 2), 0.5, jnp.float32)
        return {'feat': feat, 'src': src, 'dst': dst, 'Wc': Wc, 'Wp': Wp, 'attn_src': attn_src, 'attn_dst': attn_dst, 'pos_attn_src': pos_attn_src, 'pos_attn_dst': pos_attn_dst, 'att_comb': att_comb}
    _L2_gnn_all = _L2_gnn_setup()
    _L2_gnn_in = {k: v for k, v in _L2_gnn_all.items() if k in ('Wc', 'Wp', 'attn_src', 'attn_dst', 'pos_attn_src', 'pos_attn_dst', 'att_comb')}
    del _L2_gnn_all

    def _L3_gnn_setup():
        import jax, jax.numpy as jnp
        import numpy as np
        N_NODES = 50000
        N_EDGES = 25000
        D_IN = 256
        D_OUT = 256
        key = jax.random.key(seed)
        ks = jax.random.split(key, 8)
        feat = jax.random.normal(ks[0], (N_NODES, D_IN), dtype=jnp.float32)
        weight = jax.random.normal(ks[1], (N_EDGES, 1), dtype=jnp.float32)
        src = jax.random.randint(ks[2], (N_EDGES,), 0, N_NODES, dtype=jnp.int32)
        dst = jax.random.randint(ks[3], (N_EDGES,), 0, N_NODES, dtype=jnp.int32)
        W_pool = jax.random.normal(ks[4], (D_IN, D_IN), dtype=jnp.float32) * 0.05
        b_pool = jnp.zeros((D_IN,), dtype=jnp.float32)
        W_self = jax.random.normal(ks[5], (D_OUT, D_IN), dtype=jnp.float32) * 0.05
        b_self = jnp.zeros((D_OUT,), dtype=jnp.float32)
        W_neigh = jax.random.normal(ks[6], (D_OUT, D_IN), dtype=jnp.float32) * 0.05
        b_neigh = jnp.zeros((D_OUT,), dtype=jnp.float32)
        return {'feat': feat, 'weight': weight, 'src': src, 'dst': dst, 'W_pool': W_pool, 'b_pool': b_pool, 'W_self': W_self, 'b_self': b_self, 'W_neigh': W_neigh, 'b_neigh': b_neigh}
    _L3_gnn_all = _L3_gnn_setup()
    _L3_gnn_in = {k: v for k, v in _L3_gnn_all.items() if k in ('W_pool', 'b_pool', 'W_self', 'b_self', 'W_neigh', 'b_neigh')}
    del _L3_gnn_all
    return {'x': x, 'src': src, 'dst': dst, 'edge_attr_96': edge_attr_96, 'edge_weight1': edge_weight1, 'L0_gnn_W_msg': _L0_gnn_in['W_msg'], 'L0_gnn_b_msg': _L0_gnn_in['b_msg'], 'L0_gnn_W_upd': _L0_gnn_in['W_upd'], 'L0_gnn_b_upd': _L0_gnn_in['b_upd'], 'L0_gnn_gamma': _L0_gnn_in['gamma'], 'L0_gnn_beta': _L0_gnn_in['beta'], 'L1_gnn_u': _L1_gnn_in['u'], 'L1_gnn_W1': _L1_gnn_in['W1'], 'L1_gnn_b1': _L1_gnn_in['b1'], 'L1_gnn_W2': _L1_gnn_in['W2'], 'L1_gnn_b2': _L1_gnn_in['b2'], 'L2_gnn_Wc': _L2_gnn_in['Wc'], 'L2_gnn_Wp': _L2_gnn_in['Wp'], 'L2_gnn_attn_src': _L2_gnn_in['attn_src'], 'L2_gnn_attn_dst': _L2_gnn_in['attn_dst'], 'L2_gnn_pos_attn_src': _L2_gnn_in['pos_attn_src'], 'L2_gnn_pos_attn_dst': _L2_gnn_in['pos_attn_dst'], 'L2_gnn_att_comb': _L2_gnn_in['att_comb'], 'L3_gnn_W_pool': _L3_gnn_in['W_pool'], 'L3_gnn_b_pool': _L3_gnn_in['b_pool'], 'L3_gnn_W_self': _L3_gnn_in['W_self'], 'L3_gnn_b_self': _L3_gnn_in['b_self'], 'L3_gnn_W_neigh': _L3_gnn_in['W_neigh'], 'L3_gnn_b_neigh': _L3_gnn_in['b_neigh']}

def reference(x, src, dst, edge_attr_96, edge_weight1, L0_gnn_W_msg, L0_gnn_b_msg, L0_gnn_W_upd, L0_gnn_b_upd, L0_gnn_gamma, L0_gnn_beta, L1_gnn_u, L1_gnn_W1, L1_gnn_b1, L1_gnn_W2, L1_gnn_b2, L2_gnn_Wc, L2_gnn_Wp, L2_gnn_attn_src, L2_gnn_attn_dst, L2_gnn_pos_attn_src, L2_gnn_pos_attn_dst, L2_gnn_att_comb, L3_gnn_W_pool, L3_gnn_b_pool, L3_gnn_W_self, L3_gnn_b_self, L3_gnn_W_neigh, L3_gnn_b_neigh):
    import jax
    import jax.numpy as jnp

    def _L0_gnn_ref(x, edge_index, W_msg, b_msg, W_upd, b_upd, gamma, beta):
        import jax, jax.numpy as jnp
        import numpy as np
        N_NODES = 10000
        N_EDGES = 10000
        IN_DIM = 256
        OUT_DIM = 256
        LN_EPS = 1e-05
        row, col = (edge_index[0], edge_index[1])
        msg_in = jnp.concatenate([x[row], x[col]], axis=-1)
        messages = jax.nn.relu(msg_in @ W_msg + b_msg)
        aggregated = jax.ops.segment_sum(messages, col, num_segments=x.shape[0])
        h = jax.nn.relu(jnp.concatenate([x, aggregated], axis=-1) @ W_upd + b_upd)
        mu = jnp.mean(h, axis=-1, keepdims=True)
        var = jnp.mean(jnp.square(h - mu), axis=-1, keepdims=True)
        return (h - mu) * jax.lax.rsqrt(var + LN_EPS) * gamma + beta

    def _L1_gnn_ref(x, edge_attr, u, W1, b1, W2, b2, edge_index, batch):
        import jax, jax.numpy as jnp
        import numpy as np
        N_NODES = 50000
        N_EDGES = 25000
        EDGE_F = 96
        NODE_F = 256
        GLOB_F = 64
        HIDDEN = 1024
        N_GRAPHS = 8
        MLP_IN = NODE_F + 3 * EDGE_F + GLOB_F
        col = edge_index[1]
        n = x.shape[0]
        out1 = jax.ops.segment_sum(edge_attr, col, num_segments=n)
        cnt = jax.ops.segment_sum(jnp.ones((edge_attr.shape[0], 1), edge_attr.dtype), col, num_segments=n)
        out2 = jax.ops.segment_max(edge_attr, col, num_segments=n)
        out2 = jnp.where(cnt > 0, out2, jnp.zeros_like(out2))
        out3 = out1 / jnp.maximum(cnt, 1.0)
        h = jnp.concatenate([x, out1, out2, out3, u[batch]], axis=1)
        h = jax.nn.relu(h @ W1 + b1) @ W2 + b2
        return h + x

    def _L2_gnn_ref(feat, src, dst, Wc, Wp, attn_src, attn_dst, pos_attn_src, pos_attn_dst, att_comb):
        import jax, jax.numpy as jnp
        import numpy as np
        N = 50000
        E = 25000
        IN = 256
        POS = 16
        H = 4
        D = 64
        D4 = D // 4

        def _xavier(key, shape):
            fan_out, fan_in = (shape[0], shape[1])
            lim = np.sqrt(6.0 / (fan_in + fan_out)).astype(np.float32)
            return jax.random.uniform(key, shape, jnp.float32, -lim, lim)
        n = feat.shape[0]
        content = feat[:, :IN - POS]
        pos = feat[:, IN - POS:]
        hc = (content @ Wc.T).reshape(n, H, D)
        hp = (pos @ Wp.T).reshape(n, H, D4)
        s_c = jnp.einsum('nhd,hd->nh', hc, attn_src[0])
        d_c = jnp.einsum('nhd,hd->nh', hc, attn_dst[0])
        s_p = jnp.einsum('nhd,hd->nh', hp, pos_attn_src[0])
        d_p = jnp.einsum('nhd,hd->nh', hp, pos_attn_dst[0])
        content_e = s_c[src] + d_c[dst]
        pos_e = s_p[src] + d_p[dst]
        e = content_e * att_comb[:, 0] + pos_e * att_comb[:, 1]
        e = jax.nn.leaky_relu(e, negative_slope=0.2)
        m = jax.ops.segment_max(e, dst, num_segments=n)
        m = jax.lax.stop_gradient(jnp.where(jnp.isfinite(m), m, 0.0))
        ee = jnp.exp(e - m[dst])
        denom = jax.ops.segment_sum(ee, dst, num_segments=n)
        a = ee / denom[dst]
        msg = hc[src] * a[..., None]
        ft = jax.ops.segment_sum(msg, dst, num_segments=n)
        h = ft.reshape(n, H * D)
        h = h + feat
        return h

    def _L3_gnn_ref(feat, weight, src, dst, W_pool, b_pool, W_self, b_self, W_neigh, b_neigh):
        import jax, jax.numpy as jnp
        import numpy as np
        N_NODES = 50000
        N_EDGES = 25000
        D_IN = 256
        D_OUT = 256
        n = feat.shape[0]
        h = jax.nn.relu(feat @ W_pool.T + b_pool)
        m = h[src] * weight
        neigh = jax.ops.segment_max(m, dst, num_segments=n)
        deg = jax.ops.segment_sum(jnp.ones((src.shape[0],), feat.dtype), dst, num_segments=n)
        neigh = jnp.where((deg > 0)[:, None], neigh, jnp.zeros((), feat.dtype))
        return feat @ W_self.T + b_self + (neigh @ W_neigh.T + b_neigh)
    edge_index = jnp.stack([src, dst])
    batch0 = jnp.zeros((3125,), jnp.int32)
    h = jnp.maximum(_layernorm(x, axis=-1), 0.0)
    x = x + _L0_gnn_ref(h, edge_index, L0_gnn_W_msg, L0_gnn_b_msg, L0_gnn_W_upd, L0_gnn_b_upd, L0_gnn_gamma, L0_gnn_beta)
    h = jnp.maximum(_layernorm(x, axis=-1), 0.0)
    x = x + _L1_gnn_ref(h, edge_attr_96, L1_gnn_u, L1_gnn_W1, L1_gnn_b1, L1_gnn_W2, L1_gnn_b2, edge_index, batch0)
    h = jnp.maximum(_layernorm(x, axis=-1), 0.0)
    x = x + _L2_gnn_ref(h, src, dst, L2_gnn_Wc, L2_gnn_Wp, L2_gnn_attn_src, L2_gnn_attn_dst, L2_gnn_pos_attn_src, L2_gnn_pos_attn_dst, L2_gnn_att_comb)
    h = jnp.maximum(_layernorm(x, axis=-1), 0.0)
    x = x + _L3_gnn_ref(h, edge_weight1, src, dst, L3_gnn_W_pool, L3_gnn_b_pool, L3_gnn_W_self, L3_gnn_b_self, L3_gnn_W_neigh, L3_gnn_b_neigh)
    return x

_drawn_inputs = setup_inputs


def setup_inputs(seed=0):
    import zlib

    import numpy as np

    out = dict(_drawn_inputs(seed))
    spreads = {'L0_gnn_b_msg': (0.0, 0.1),
     'L0_gnn_b_upd': (0.0, 0.416),
     'L0_gnn_gamma': (1.0, 0.2),
     'L0_gnn_beta': (0.0, 0.1),
     'L2_gnn_att_comb': (0.5, 0.6),
     'L3_gnn_b_pool': (0.0, 0.1),
     'L3_gnn_b_self': (0.0, 0.267),
     'L3_gnn_b_neigh': (0.0, 0.281)}
    factors = {'L1_gnn_b1': 21.353,
     'L1_gnn_b2': 8.0,
     'L2_gnn_Wp': 8.0,
     'L2_gnn_attn_src': 8.0,
     'L2_gnn_attn_dst': 54.152,
     'L2_gnn_pos_attn_src': 8.0,
     'L2_gnn_pos_attn_dst': 8.0}
    for name, (base, spread) in spreads.items():
        noise = np.random.default_rng([zlib.crc32(name.encode()), seed]).standard_normal(out[name].shape)
        drawn = base * np.exp(spread * noise) if base else spread * noise
        out[name] = jnp.asarray(drawn.astype(out[name].dtype))
    for name, factor in factors.items():
        out[name] = (out[name] * factor).astype(out[name].dtype)
    return out
```

```python
from contextlib import ExitStack

import concourse.bass as bass
from concourse import mybir

F32 = mybir.dt.float32
BF16 = mybir.dt.bfloat16
I32 = mybir.dt.int32
ALU = mybir.AluOpType
ACT = mybir.ActivationFunctionType

P = 128
N = 3125
E = 53125
D = 256
NT = 125
NB = N // NT
WN = N + P
TG = 4
GE = TG * P
SLOTS = 4
T = -(-E // (GE * SLOTS)) * TG * SLOTS
NG = T // TG
NI = NG // SLOTS
RQ = 4
RT = T // RQ
FULL = E // P
REST = E - FULL * P
AF = 96
U = 64
HID = 1024
H = 4
HD = 64
POS = 16
CD = D - POS
CREDIT = SLOTS + TG
FLT = 3.3895313892515355e38
EPS = 1e-5
BANK = 512
CH = 500
CHUNKS = [(c, min(CH, N - c)) for c in range(0, N, CH)]


def ready(i, s):
    return i * SLOTS + (s + 1 + CREDIT)


def freed(i, s, buffers):
    return i * SLOTS + (s + 1 + CREDIT - buffers)


def tiles_before(i, s, t):
    return i * (SLOTS * TG) + (s * TG + t + CREDIT)


def hold(eng, sem, value, least=1):
    value = value if isinstance(value, int) else eng.to_reg(value)
    eng.wait_ge(sem, least)
    eng.wait_ge(sem, value)


def pipelined(eng, stages):
    for g in range(-max(ahead for _, ahead in stages), 0):
        for stage, ahead in stages:
            if g + ahead >= 0:
                stage(0, g + ahead)
    with eng.Fori(0, NI - 1) as i:
        for s in range(SLOTS):
            for stage, ahead in stages:
                k = s + ahead
                stage(i + 1 if k >= SLOTS else i, k % SLOTS)
    for s in range(SLOTS):
        for stage, ahead in stages:
            if s + ahead < SLOTS:
                stage(NI - 1, s + ahead)


class Kernel:

    def __init__(self, nc, ctx, a, out):
        self.nc, self.ctx, self.a, self.out = nc, ctx, a, out
        self.before = {}
        sem = self.sem
        self.index_in = [sem(f"index_in{s}") for s in range(SLOTS)]
        self.rows_in = [sem(f"rows_in{s}") for s in range(SLOTS)]
        self.line_in = [sem(f"line_in{s}") for s in range(SLOTS)]
        self.window_in = [sem(f"window_in{s}") for s in range(SLOTS)]

    def sem(self, name):
        return self.ctx.enter_context(self.nc.semaphore(name))

    def sb(self, name, shape, dt=F32, ctx=None):
        return (ctx or self.ctx).enter_context(self.nc.sbuf_tensor(name, shape, dt))

    def ps(self, name, shape, ctx):
        size = 1
        for n in shape[1:]:
            size *= n
        banks = ctx.enter_context(self.nc.psum_tensor(name, [shape[0], -(-size // BANK) * BANK], F32))
        flat = banks[:, 0:size]
        if len(shape) == 3:
            return flat.rearrange("p (a b) -> p a b", a=shape[1])
        if len(shape) == 4:
            return flat.rearrange("p (a b c) -> p a b c", a=shape[1], b=shape[2])
        return flat

    def landed(self, semaphores, i, s, transfers=1):
        sem = semaphores[s]
        return sem, i * (16 * transfers) + (self.before.get(sem.name, 0) + 16 * transfers)

    def pass_over(self, semaphores, transfers=1, more=()):
        for s, sem in enumerate(semaphores):
            self.before[sem.name] = self.before.get(sem.name, 0) + 16 * (transfers * NI + (s in more))

    def bases(self, engine, i, s):
        _, values = self.nc.values_load_multi_w_load_instructions(
            self.base[0:1, bass.ds(i * (SLOTS * TG) + s * TG, TG)], engines=[engine], min_val=0, max_val=N - 1,
            skip_runtime_bounds_check_because="destinations are node numbers")
        return values

    def prepare(self):
        nc, a, sb = self.nc, self.a, self.sb
        lines_made = 0
        self.x = sb("x", [NT, NB, D])
        self.hT = sb("hT", [P, 2, N])
        self.h = sb("h", [NT, NB, D])
        self.source = sb("source", [P, T], I32)
        self.place = sb("place", [P, T])
        self.place_end = sb("place_end", [P, T])
        self.weight = sb("weight", [P, T])
        self.base = sb("base", [1, T], I32)
        self.columns = sb("columns", [P, P])
        self.partition = sb("partition", [P, 1])
        self.ident = sb("ident", [P, P])
        self.ones = sb("ones", [P, P])
        self.aggT = sb("aggT", [P, 2, WN])
        self.place_line = nc.dram_tensor("place_line", [T * P], BF16).ap()
        self.mask_line = nc.dram_tensor("mask_line", [T * P], BF16).ap()
        loads, constants, chain = self.sem("prep_loads"), self.sem("prep_constants"), self.sem("prep_chain")
        clears, pe, stores = self.sem("prep_clears"), self.sem("prep_transposed"), self.sem("prep_stores")
        with ExitStack() as ctx:
            def tmp(name, shape, dt=F32):
                return self.sb(name, shape, dt, ctx)
            raw = {k: tmp(k, [RT, RQ, P], I32) for k in ("src_rows", "dst_rows")}
            w_rows = tmp("w_rows", [RT, RQ, P])
            before, after = tmp("before", [RT, RQ], I32), tmp("after", [RT, RQ], I32)
            src_f, dst_f, other = tmp("src_f", [RT, RQ, P]), tmp("dst_f", [RT, RQ, P]), tmp("other", [RT, RQ, P])
            before_f, after_f = tmp("before_f", [RT, RQ]), tmp("after_f", [RT, RQ])
            rel, rel_end, flag = tmp("rel", [RT, RQ, P]), tmp("rel_end", [RT, RQ, P]), tmp("flag", [RT, RQ, P])
            mask = tmp("mask", [RT, RQ, P], BF16)
            rel16 = tmp("rel16", [RT, RQ, P], BF16)
            psT = [self.ps(f"prep_ps{k}", [P, T], ctx) for k in range(4)]
            whole = (RQ - 1) * RT
            transfers = []
            for tile, flat in ((raw["src_rows"], a["src"]), (raw["dst_rows"], a["dst"]),
                               (w_rows, a["edge_weight1"].rearrange("e o -> (e o)"))):
                transfers += [
                    (tile[:, 0:RQ - 1, :], flat[0:whole * P].rearrange("(q r c) -> r q c", r=RT, c=P)),
                    (tile[0:FULL - whole, RQ - 1, :], flat[whole * P:FULL * P].rearrange("(r c) -> r c", c=P)),
                    (tile[FULL - whole:FULL - whole + 1, RQ - 1, 0:REST],
                     flat[FULL * P:E].rearrange("(r c) -> r c", r=1))]
            dst = a["dst"]
            ends = dst[P:FULL * P].rearrange("(j c) -> j c", c=P)[:, P - 1:P]
            firsts = dst[P:FULL * P].rearrange("(j c) -> j c", c=P)[:, 0:1]
            transfers += [(before[1:2, 0:1], dst[P - 1:P].rearrange("(r c) -> r c", r=1)),
                          (before[2:RT, 0:1], ends[0:RT - 2, :])]
            transfers += [(before[:, q:q + 1], ends[q * RT - 2:(q + 1) * RT - 2, :]) for q in range(1, RQ - 1)]
            transfers += [(before[0:FULL + 1 - whole, RQ - 1:RQ], ends[whole - 2:FULL - 1, :])]
            transfers += [(after[:, q:q + 1], firsts[q * RT:(q + 1) * RT, :]) for q in range(RQ - 1)]
            transfers += [(after[0:FULL - 1 - whole, RQ - 1:RQ], firsts[whole:FULL - 1, :]),
                          (after[FULL - 1 - whole:FULL - whole, RQ - 1:RQ],
                           dst[FULL * P:FULL * P + 1].rearrange("(r c) -> r c", r=1))]
            transfers += [(self.base[0:1, 0:FULL], dst[0:FULL * P].rearrange("(j c) -> c j", c=P)[0:1, :]),
                          (self.base[0:1, FULL:FULL + 1], dst[FULL * P:FULL * P + 1].rearrange("(r c) -> r c", r=1)),
                          (self.x[:, :, :], a["x"].rearrange("(b p) d -> p b d", p=NT))]
            with nc.Block() as block:
                @block.gpsimd
                def _(pool):
                    nc.gpsimd.iota(self.columns[:], pattern=[[1, P]], base=0, channel_multiplier=0,
                                   allow_small_or_imprecise_dtypes=True).then_inc(constants, 1)
                    nc.gpsimd.iota(self.partition[:], pattern=[[0, 1]], base=0, channel_multiplier=1,
                                   allow_small_or_imprecise_dtypes=True).then_inc(constants, 1)

                @block.vector
                def _(dve):
                    nonlocal lines_made
                    steps = 0

                    def link(ins):
                        nonlocal steps
                        steps += 1
                        ins.then_inc(chain, 1)
                        dve.wait_ge(chain, steps)
                    nc.vector.memset(raw["src_rows"][:], 0).then_inc(clears, 1)
                    nc.vector.memset(raw["dst_rows"][:], -1).then_inc(clears, 1)
                    nc.vector.memset(w_rows[:], 0.0).then_inc(clears, 1)
                    nc.vector.memset(before[:], -1).then_inc(clears, 1)
                    nc.vector.memset(after[:], -1).then_inc(clears, 1)
                    nc.vector.memset(self.ones[:], 1.0)
                    dve.wait_ge(constants, 2)
                    link(nc.vector.tensor_scalar(self.ident[:], self.columns[:], self.partition[:, 0:1], None,
                                                 ALU.is_equal))
                    dve.wait_ge(loads, 16 * len(transfers))
                    link(nc.vector.tensor_copy(src_f[:], raw["src_rows"][:]))
                    link(nc.vector.tensor_copy(dst_f[:], raw["dst_rows"][:]))
                    link(nc.vector.tensor_copy(before_f[:], before[:]))
                    link(nc.vector.tensor_copy(after_f[:], after[:]))
                    link(nc.vector.tensor_tensor(rel[:], dst_f[:], dst_f[:, :, 0:1].to_broadcast([RT, RQ, P]),
                                                 ALU.subtract))
                    link(nc.vector.tensor_copy(other[:, :, 0:P - 1], dst_f[:, :, 1:P]))
                    link(nc.vector.tensor_copy(other[:, :, P - 1:P], after_f[:].unsqueeze(2)))
                    link(nc.vector.tensor_tensor(flag[:], dst_f[:], other[:], ALU.not_equal))
                    link(nc.vector.scalar_tensor_tensor(out=rel_end[:], in0=rel[:], scalar=1.0, in1=flag[:],
                                                        op0=ALU.add, op1=ALU.mult))
                    link(nc.vector.tensor_scalar(rel_end[:], rel_end[:], -1.0, None, ALU.add))
                    link(nc.vector.tensor_copy(other[:, :, 1:P], dst_f[:, :, 0:P - 1]))
                    link(nc.vector.tensor_copy(other[:, :, 0:1], before_f[:].unsqueeze(2)))
                    link(nc.vector.tensor_tensor(flag[:], dst_f[:], other[:], ALU.not_equal))
                    link(nc.vector.tensor_scalar(other[:], flag[:], -FLT, FLT, ALU.mult, ALU.add))
                    link(nc.vector.scalar_tensor_tensor(out=mask[:], in0=flag[:], scalar=-FLT, in1=other[:],
                                                        op0=ALU.mult, op1=ALU.add))
                    link(nc.vector.tensor_copy(rel16[:], rel[:]))
                    lines_made = steps
                    for k, dst in enumerate((self.source, self.place, self.place_end, self.weight)):
                        dve.wait_ge(pe, k + 1)
                        nc.vector.tensor_copy(dst[:], psT[k][:])

                @block.tensor
                def _(t):
                    t.wait_ge(chain, lines_made)
                    for k, rows in enumerate((src_f, rel, rel_end, w_rows)):
                        for q in range(RQ):
                            last = nc.tensor.transpose(psT[k][:, q * RT:(q + 1) * RT], rows[:, q, :],
                                                       self.ident[0:RT, 0:RT])
                        last.then_inc(pe, 1)

                @block.sync
                def _(sp):
                    sp.wait_ge(clears, 5)
                    for tile, src in transfers:
                        sp.dma_start(tile, src, allow_slow_non_contiguous=True).then_inc(loads, 16)
                    sp.wait_ge(chain, lines_made)
                    sp.dma_start(self.mask_line.rearrange("(q r c) -> r q c", r=RT, c=P), mask[:]).then_inc(stores, 16)
                    sp.dma_start(self.place_line.rearrange("(q r c) -> r q c", r=RT, c=P), rel16[:]).then_inc(stores, 16)
                    sp.wait_ge(stores, 32)

    def normalize(self, name):
        nc = self.nc
        chain, root, rstd, made = (self.sem(f"{name}_{k}") for k in ("stats", "root", "rstd", "h"))
        turned, kept = self.sem(f"{name}_turned"), self.sem(f"{name}_kept")
        with ExitStack() as ctx:
            st = self.sb(f"{name}_st", [NT, NB, 6], ctx=ctx)
            mv = self.sb(f"{name}_mv", [NT, NB, 2], ctx=ctx)
            sd = self.sb(f"{name}_sd", [NT, NB], ctx=ctx)
            rs = self.sb(f"{name}_rs", [NT, NB], ctx=ctx)
            nm = self.sb(f"{name}_nm", [NT, NB], ctx=ctx)
            ps = [self.ps(f"{name}_ps{k}", [P, 2, P], ctx) for k in range(2)]
            with nc.Block() as block:
                @block.vector
                def _(dve):
                    for b in range(NB):
                        nc.vector.bn_stats(st[:, b, :], self.x[:, b, :]).then_inc(chain, 1)
                    for b in range(NB):
                        dve.wait_ge(chain, b + 1)
                        nc.vector.bn_aggr(mv[:, b, :], st[:, b, :]).then_inc(chain, 1)
                    dve.wait_ge(chain, 2 * NB)
                    nc.vector.tensor_scalar(sd[:], mv[:, :, 1], EPS, None, ALU.add).then_inc(chain, 1)
                    dve.wait_ge(root, 1)
                    nc.vector.reciprocal(rs[:], sd[:]).then_inc(chain, 1)
                    dve.wait_ge(chain, 2 * NB + 2)
                    nc.vector.scalar_tensor_tensor(out=nm[:], in0=mv[:, :, 0], scalar=-1.0, in1=rs[:],
                                                   op0=ALU.mult, op1=ALU.mult).then_inc(rstd, 1)
                    for b in range(NB):
                        dve.wait_ge(turned, b + 1)
                        nc.vector.tensor_copy(self.hT[:, :, b * NT:(b + 1) * NT], ps[b % 2][:, :, 0:NT]).then_inc(kept, 1)

                @block.scalar
                def _(act):
                    act.wait_ge(chain, 2 * NB + 1)
                    nc.scalar.activation(sd[:], sd[:], ACT.Sqrt).then_inc(root, 1)
                    act.wait_ge(rstd, 1)
                    for b in range(NB):
                        nc.scalar.activation(self.h[:, b, :], self.x[:, b, :], ACT.Relu, scale=rs[:, b:b + 1],
                                             bias=nm[:, b:b + 1]).then_inc(made, 1)

                @block.tensor
                def _(t):
                    for b in range(NB):
                        t.wait_ge(made, b + 1)
                        if b >= 2:
                            t.wait_ge(kept, b - 1)
                        for k in range(2):
                            last = nc.tensor.transpose(ps[b % 2][:, k, 0:NT], self.h[:, b, k * P:(k + 1) * P],
                                                       self.ident[0:NT, 0:NT])
                        last.then_inc(turned, 1)

    def clear(self, name, tile):
        with self.nc.Block() as block:
            @block.gpsimd
            def _(pool):
                self.nc.gpsimd.memset(tile[:], 0.0)

    def start_events(self, engine, events):
        for event in events:
            engine.sem_inc(event, CREDIT)

    def sum_pass(self, name, table, width, window_table, window_width, attention):
        nc = self.nc
        ev = {k: self.sem(f"{name}_{k}") for k in (
            "one_hots", "expanded", "added", "weighed", "summed", "tile_added", "logit", "exps")}
        with ExitStack() as ctx:
            index = self.sb(f"{name}_index", [P, SLOTS, TG], I32, ctx)
            rows = self.sb(f"{name}_rows", [P, SLOTS, TG, width], ctx=ctx)
            line = self.sb(f"{name}_line", [P, SLOTS, GE], BF16, ctx)
            window = self.sb(f"{name}_window", [P, SLOTS, TG, window_width], ctx=ctx)
            by_node = self.sb(f"{name}_by_node", [P, SLOTS, GE], ctx=ctx)
            by_edge = self.sb(f"{name}_by_edge", [P, SLOTS, TG, P], ctx=ctx)
            logit = self.sb(f"{name}_logit", [P, 2, TG, H], ctx=ctx)
            exps = self.sb(f"{name}_exps", [P, 2, TG, H], ctx=ctx)
            ps_window = [self.ps(f"{name}_ps_window{b}", [P, TG, window_width], ctx) for b in range(2)]
            ps_sum = [self.ps(f"{name}_ps_sum{b}", [P, TG, 2, P], ctx) for b in range(2)]
            ps_den = [self.ps(f"{name}_ps_den{b}", [P, TG, P], ctx) for b in range(2)] if attention else None
            with nc.Block() as block:
                @block.sync
                def _(sp):
                    def fetch(i, s):
                        hold(sp, ev["added"], freed(i, s, SLOTS))
                        sp.dma_start(index[:, s, :], self.source[:, bass.ds(i * (SLOTS * TG) + s * TG, TG)]
                                     ).then_inc(self.index_in[s], 16)
                        hold(sp, ev["one_hots"], freed(i, s, SLOTS))
                        sp.dma_start(line[:, s, :], self.place_line[bass.ds(i * (SLOTS * GE) + s * GE, GE)]
                                     .partition_broadcast(P)).then_inc(self.line_in[s], 16)
                        hold(sp, ev["expanded"], freed(i, s, SLOTS))
                        for t, base in enumerate(self.bases(mybir.EngineType.SP, i, s)):
                            sp.dma_start(window[:, s, t, :], window_table[bass.ds(base, P), :]
                                         ).then_inc(self.window_in[s], 16)
                    pipelined(sp, [(fetch, 0)])

                @block.gpsimd
                def _(pool):
                    def gather(i, s):
                        hold(pool, *self.landed(self.index_in, i, s), least=16)
                        hold(pool, ev["summed"], freed(i, s, SLOTS))
                        for t in range(TG):
                            nc.gpsimd.indirect_dma_start(
                                rows[:, s, t, :], None, table,
                                bass.IndirectOffsetOnAxis(ap=index[:, s, t:t + 1], axis=0)
                            ).then_inc(self.rows_in[s], 16)
                    pipelined(pool, [(gather, 0)])

                @block.vector
                def _(dve):
                    self.start_events(dve, [ev["one_hots"], ev["added"], ev["logit"], ev["tile_added"]])

                    def by_nodes(i, s):
                        dve.wait_ge(ev["summed"], freed(i, s, SLOTS))
                        dve.wait_ge(*self.landed(self.line_in, i, s))
                        nc.vector.tensor_scalar(by_node[:, s, :], line[:, s, :], self.partition[:, 0:1], None,
                                                ALU.is_equal)

                    def by_edges(i, s):
                        place = self.place[:, bass.ds(i * (SLOTS * TG) + s * TG, TG)]
                        nc.vector.tensor_tensor(by_edge[:, s, :, :],
                                                self.columns[:].unsqueeze(1).to_broadcast([P, TG, P]),
                                                place.unsqueeze(2).to_broadcast([P, TG, P]),
                                                ALU.is_equal).then_inc(ev["one_hots"], 1)

                    def add(i, s):
                        dve.wait_ge(ev["expanded"], ready(i, s))
                        dve.wait_ge(*self.landed(self.rows_in, i, s, TG))
                        nc.vector.tensor_tensor(rows[:, s, :, :], ps_window[s % 2][:], rows[:, s, :, :],
                                                ALU.add).then_inc(ev["added"], 1)

                    def logit_step(i, s, k):
                        return i * (2 * SLOTS) + (2 * s + k + CREDIT)

                    def add_terms(i, s):
                        dve.wait_ge(ev["expanded"], ready(i, s))
                        dve.wait_ge(*self.landed(self.rows_in, i, s, TG))
                        dve.wait_ge(ev["weighed"], freed(i, s, 2))
                        nc.vector.tensor_tensor(logit[:, s % 2, :, :], rows[:, s, :, D:D + H],
                                                ps_window[s % 2][:, :, 0:H], ALU.add).then_inc(ev["logit"], 1)

                    def leak(i, s):
                        dve.wait_ge(ev["logit"], logit_step(i, s, 1))
                        at = logit[:, s % 2, :, :]
                        nc.vector.scalar_tensor_tensor(out=at, in0=at, scalar=0.2, in1=at, op0=ALU.mult,
                                                       op1=ALU.max).then_inc(ev["logit"], 1)

                    def less_largest(i, s):
                        dve.wait_ge(ev["logit"], logit_step(i, s, 2))
                        at = logit[:, s % 2, :, :]
                        nc.vector.tensor_tensor(at, at, ps_window[s % 2][:, :, H:2 * H],
                                                ALU.subtract).then_inc(ev["added"], 1)

                    def weigh(i, s, t):
                        if t == 0:
                            dve.wait_ge(ev["exps"], ready(i, s))
                        by_head = rows[:, s, t, 0:D].rearrange("p (h d) -> p h d", h=H)
                        last = nc.vector.tensor_tensor(by_head, by_head,
                                                       exps[:, s % 2, t, :].unsqueeze(2).to_broadcast([P, H, HD]),
                                                       ALU.mult)
                        if t == TG - 1:
                            last.then_inc(ev["weighed"], 1)

                    bases = []

                    def accumulate(i, s, t):
                        if t == 0:
                            bases[:] = self.bases(mybir.EngineType.DVE, i, s)
                            dve.wait_ge(ev["summed"], ready(i, s))
                        dve.wait_ge(ev["tile_added"], tiles_before(i, s, t))
                        if attention:
                            den = self.denomT[:, bass.ds(bases[t], P)]
                            nc.vector.tensor_tensor(den, den, ps_den[s % 2][0:H, t, :], ALU.add)
                        at = self.aggT[:, :, bass.ds(bases[t], P)]
                        nc.vector.tensor_tensor(at, at, ps_sum[s % 2][:, t, :, :], ALU.add
                                                ).then_inc(ev["tile_added"], 1)

                    def of_tile(stage, t):
                        return lambda i, s: stage(i, s, t)
                    acc = [of_tile(accumulate, t) for t in range(TG)]
                    wei = [of_tile(weigh, t) for t in range(TG)]
                    if attention:
                        self.start_events(dve, [ev["weighed"]])
                        pipelined(dve, [(acc[0], 0), (by_nodes, 4), (wei[0], 2), (acc[1], 0), (by_edges, 4),
                                        (wei[1], 2), (acc[2], 0), (add_terms, 3), (wei[2], 2), (leak, 3),
                                        (acc[3], 0), (less_largest, 3), (wei[3], 2)])
                    else:
                        pipelined(dve, [(acc[0], 0), (by_nodes, 4), (acc[1], 0), (by_edges, 4), (acc[2], 0),
                                        (add, 2), (acc[3], 0)])

                @block.scalar
                def _(act):
                    def relu(i, s):
                        act.wait_ge(ev["added"], ready(i, s))
                        nc.scalar.activation(rows[:, s, :, :], rows[:, s, :, :], ACT.Relu).then_inc(ev["weighed"], 1)

                    def exp(i, s):
                        act.wait_ge(ev["added"], ready(i, s))
                        act.wait_ge(ev["summed"], freed(i, s, 2))
                        nc.scalar.activation(exps[:, s % 2, :, :], logit[:, s % 2, :, :],
                                             ACT.Exp).then_inc(ev["exps"], 1)
                    self.start_events(act, [ev["exps"]] if attention else [ev["weighed"]])
                    pipelined(act, [(exp if attention else relu, 0)])

                @block.tensor
                def _(pe):
                    self.start_events(pe, [ev["expanded"], ev["summed"]])

                    def expand(i, s):
                        pe.wait_ge(ev["one_hots"], ready(i, s))
                        pe.wait_ge(*self.landed(self.window_in, i, s, TG))
                        pe.wait_ge(ev["added"], freed(i, s, 2))
                        for t in range(TG):
                            last = nc.tensor.matmul(ps_window[s % 2][:, t, :], by_node[:, s, t * P:(t + 1) * P],
                                                    window[:, s, t, :], start=True, stop=True)
                        last.then_inc(ev["expanded"], 1)

                    def gather_sums(i, s):
                        pe.wait_ge(ev["weighed"], ready(i, s))
                        pe.wait_ge(ev["tile_added"], tiles_before(i, s, -TG))
                        for t in range(TG):
                            if attention:
                                nc.tensor.matmul(ps_den[s % 2][0:H, t, :], exps[:, s % 2, t, :], by_edge[:, s, t, :],
                                                 start=True, stop=True)
                            for k in range(2):
                                last = nc.tensor.matmul(ps_sum[s % 2][:, t, k, :], rows[:, s, t, k * P:(k + 1) * P],
                                                        by_edge[:, s, t, :], start=True, stop=True)
                        last.then_inc(ev["summed"], 1)
                    pipelined(pe, [(gather_sums, 1), (expand, 3)])
        self.pass_over(self.index_in)
        self.pass_over(self.line_in)
        self.pass_over(self.rows_in, TG)
        self.pass_over(self.window_in, TG)

    def max_pass(self, name, blocks, outT, table=None, weighted=False, sums=None):
        nc = self.nc
        nk, width = len(blocks), sum(blocks)
        bw = blocks[0]
        ev = {k: self.sem(f"{name}_{k}") for k in (
            "weighed", "turned", "scanned", "back", "kept", "ends", "placed", "stored", "tile_added", "ones")}
        with ExitStack() as ctx:
            index = self.sb(f"{name}_index", [P, SLOTS, TG], I32, ctx)
            rows = self.sb(f"{name}_rows", [P, SLOTS, TG, width + (sums is not None)], ctx=ctx)
            line = self.sb(f"{name}_line", [P, SLOTS, GE], BF16, ctx)
            scan = self.sb(f"{name}_scan", [bw, 2, nk, GE], ctx=ctx)
            by_edge = self.sb(f"{name}_by_edge", [P, SLOTS, TG, width], ctx=ctx)
            ends = self.sb(f"{name}_ends", [P, SLOTS, TG, P], ctx=ctx)
            every = self.sb(f"{name}_every", [P, SLOTS, TG, P], ctx=ctx) if sums is not None else None
            ps_turned = [[self.ps(f"{name}_ps_turned{b}{k}", [bw, GE], ctx) for k in range(nk)] for b in range(2)]
            ps_back = self.ps(f"{name}_ps_back", [P, TG, width], ctx)
            ps_placed = self.ps(f"{name}_ps_placed", [bw, TG, nk, P], ctx)
            ps_sums = [self.ps(f"{name}_ps_sums{b}", [bw + 1, TG, P], ctx) if sums is not None else None
                       for b in range(2)]
            with nc.Block() as block:
                @block.sync
                def _(sp):
                    def mask(i, s):
                        hold(sp, ev["scanned"], freed(i, s, SLOTS))
                        sp.dma_start(line[:, s, :], self.mask_line[bass.ds(i * (SLOTS * GE) + s * GE, GE)]
                                     .partition_broadcast(P)).then_inc(self.line_in[s], 16)

                    def fetch_index(i, s):
                        hold(sp, ev["turned"], freed(i, s, SLOTS))
                        sp.dma_start(index[:, s, :], self.source[:, bass.ds(i * (SLOTS * TG) + s * TG, TG)]
                                     ).then_inc(self.index_in[s], 16)
                        mask(i, s)

                    def fetch_attributes(i, s):
                        hold(sp, ev["placed"], freed(i, s, SLOTS))
                        if isinstance(i, int) and i == NI - 1 and s == SLOTS - 1:
                            left = FULL - (NG - 1) * TG
                            src = self.a["edge_attr_96"]
                            sp.dma_start(rows[:, s, 0:left, 0:width], src[(FULL - left) * P:FULL * P, :].rearrange(
                                "(t p) f -> p t f", p=P)).then_inc(self.index_in[s], 16)
                            sp.dma_start(rows[0:REST, s, left, 0:width], src[FULL * P:E, :]).then_inc(self.index_in[s], 16)
                        else:
                            sp.dma_start(rows[:, s, :, 0:width], self.a["edge_attr_96"][
                                bass.ds(i * (SLOTS * GE) + s * GE, GE), :].rearrange("(t p) f -> p t f", p=P)
                            ).then_inc(self.index_in[s], 16)
                        mask(i, s)
                    pipelined(sp, [(fetch_index if table is not None else fetch_attributes, 0)])

                if sums is not None:
                    @block.gpsimd
                    def _(pool):
                        nc.gpsimd.memset(rows[:, :, :, width:width + 1], 1.0).then_inc(ev["ones"], 1)

                if table is not None:
                    @block.gpsimd
                    def _(pool):
                        def gather(i, s):
                            hold(pool, *self.landed(self.index_in, i, s), least=16)
                            for t in range(TG):
                                nc.gpsimd.indirect_dma_start(
                                    rows[:, s, t, :], None, table,
                                    bass.IndirectOffsetOnAxis(ap=index[:, s, t:t + 1], axis=0)
                                ).then_inc(self.rows_in[s], 16)
                        pipelined(pool, [(gather, 0)])

                def rows_landed(eng, i, s):
                    if table is not None:
                        eng.wait_ge(*self.landed(self.rows_in, i, s, TG))
                    else:
                        sem, value = self.landed(self.index_in, i, s)
                        last = isinstance(i, int) and i == NI - 1 and s == SLOTS - 1
                        eng.wait_ge(sem, value + 16 if last else value)

                @block.scalar
                def _(act):
                    self.start_events(act, [ev["kept"], ev["stored"]] + ([ev["weighed"]] if weighted else []))

                    def weigh(i, s, t):
                        if t == 0:
                            rows_landed(act, i, s)
                        w = self.weight[:, bass.ds(i * (SLOTS * TG) + (s * TG + t), 1)]
                        last = nc.scalar.activation(rows[:, s, t, :], rows[:, s, t, :], ACT.Copy, scale=w)
                        if t == TG - 1:
                            last.then_inc(ev["weighed"], 1)

                    def keep(i, s):
                        act.wait_ge(ev["back"], ready(i, s))
                        act.wait_ge(ev["placed"], freed(i, s, SLOTS))
                        nc.scalar.copy(by_edge[:, s, :, :], ps_back[:]).then_inc(ev["kept"], 1)

                    bases = []

                    def store(i, s, t):
                        if t == 0:
                            bases[:] = self.bases(mybir.EngineType.Activation, i, s)
                            act.wait_ge(ev["placed"], ready(i, s))
                        act.wait_ge(ev["stored"], tiles_before(i, s, t))
                        nc.scalar.copy(outT[:, :, bass.ds(bases[t], P)], ps_placed[:, t, :, :]
                                       ).then_inc(ev["stored"], 1)

                    def of_tile(stage, t):
                        return lambda i, s: stage(i, s, t)
                    stages = []
                    for t in range(TG):
                        stages.append((of_tile(store, t), 0))
                        if weighted:
                            stages.append((of_tile(weigh, t), 3))
                    pipelined(act, stages[:-1] + [(keep, 1)] + stages[-1:])

                @block.vector
                def _(dve):
                    self.start_events(dve, [ev["ends"]] + ([ev["tile_added"]] if sums is not None else []))

                    def one_hots(i, s, which, places):
                        place = places[:, bass.ds(i * (SLOTS * TG) + s * TG, TG)]
                        return nc.vector.tensor_tensor(
                            which[:, s, :, :], self.columns[:].unsqueeze(1).to_broadcast([P, TG, P]),
                            place.unsqueeze(2).to_broadcast([P, TG, P]), ALU.is_equal)

                    def every_edge(i, s):
                        dve.wait_ge(ev["placed"], freed(i, s, SLOTS))
                        one_hots(i, s, every, self.place)

                    def last_edges(i, s):
                        dve.wait_ge(ev["placed"], freed(i, s, SLOTS))
                        one_hots(i, s, ends, self.place_end).then_inc(ev["ends"], 1)

                    def run_scan(i, s):
                        dve.wait_ge(*self.landed(self.line_in, i, s))
                        dve.wait_ge(ev["turned"], ready(i, s))
                        dve.wait_ge(ev["back"], freed(i, s, 2))
                        dve.wait_ge(ev["scanned"], freed(i, s, 1))
                        for k in range(nk):
                            last = nc.vector.tensor_tensor_scan(
                                scan[:, s % 2, k, :], line[0:bw, s, :], ps_turned[s % 2][k][:],
                                scan[:, 1 - s % 2, k, GE - 1:GE], ALU.min, ALU.max)
                        last.then_inc(ev["scanned"], 1)

                    bases = []

                    def accumulate(i, s, t):
                        if t == 0:
                            bases[:] = self.bases(mybir.EngineType.DVE, i, s)
                            dve.wait_ge(ev["placed"], ready(i, s))
                        dve.wait_ge(ev["tile_added"], tiles_before(i, s, t))
                        at = sums[:, bass.ds(bases[t], P)]
                        nc.vector.tensor_tensor(at, at, ps_sums[s % 2][:, t, :], ALU.add
                                                ).then_inc(ev["tile_added"], 1)

                    def of_tile(stage, t):
                        return lambda i, s: stage(i, s, t)
                    nc.vector.memset(scan[:, 1, :, GE - 1:GE], 0.0).then_inc(ev["scanned"], CREDIT)
                    if sums is not None:
                        acc = [of_tile(accumulate, t) for t in range(TG)]
                        pipelined(dve, [(acc[0], 0), (every_edge, 2), (acc[1], 0), (last_edges, 2), (acc[2], 0),
                                        (run_scan, 2), (acc[3], 0)])
                    else:
                        pipelined(dve, [(last_edges, 2), (run_scan, 2)])

                @block.tensor
                def _(pe):
                    self.start_events(pe, [ev["turned"], ev["back"], ev["placed"]])
                    if sums is not None:
                        pe.wait_ge(ev["ones"], 1)

                    def turn(i, s):
                        if weighted:
                            pe.wait_ge(ev["weighed"], ready(i, s))
                        else:
                            rows_landed(pe, i, s)
                        pe.wait_ge(ev["scanned"], freed(i, s, 2))
                        for k in range(nk):
                            for t in range(TG):
                                last = nc.tensor.transpose(ps_turned[s % 2][k][:, t * P:(t + 1) * P],
                                                           rows[:, s, t, k * bw:(k + 1) * bw], self.ident[:])
                        last.then_inc(ev["turned"], 1)

                    def turn_back(i, s):
                        hold(pe, ev["scanned"], ready(i, s))
                        hold(pe, ev["kept"], freed(i, s, 1))
                        for t in range(TG):
                            for k in range(nk):
                                last = nc.tensor.transpose(ps_back[:, t, k * bw:(k + 1) * bw],
                                                           scan[:, s % 2, k, t * P:(t + 1) * P],
                                                           self.ident[0:bw, 0:bw])
                        last.then_inc(ev["back"], 1)

                    def put(i, s):
                        pe.wait_ge(ev["kept"], ready(i, s))
                        pe.wait_ge(ev["ends"], ready(i, s))
                        pe.wait_ge(ev["stored"], tiles_before(i, s, 0))
                        if sums is not None:
                            pe.wait_ge(ev["tile_added"], tiles_before(i, s, -TG))
                        for t in range(TG):
                            if sums is not None:
                                nc.tensor.matmul(ps_sums[s % 2][:, t, :], rows[:, s, t, :], every[:, s, t, :],
                                                 start=True, stop=True)
                            for k in range(nk):
                                last = nc.tensor.matmul(ps_placed[:, t, k, :], by_edge[:, s, t, k * bw:(k + 1) * bw],
                                                        ends[:, s, t, :], start=True, stop=True)
                        last.then_inc(ev["placed"], 1)
                    pipelined(pe, [(put, 0), (turn_back, 1), (turn, 2)])
        self.pass_over(self.line_in)
        if table is not None:
            self.pass_over(self.index_in)
            self.pass_over(self.rows_in, TG)
        else:
            self.pass_over(self.index_in, 1, more=(SLOTS - 1,))

    def row(self, vector, parts=NT):
        return vector.partition_broadcast(parts)

    def message_tables(self):
        nc, a = self.nc, self.a
        self.source_table = nc.dram_tensor("message_source_table", [N, D], F32).ap()
        self.window_table = nc.dram_tensor("message_window_table", [WN, D], F32).ap()
        loads, made, copied, biased, stores, clear = (self.sem(f"msg_{k}") for k in (
            "loads", "made", "copied", "biased", "stores", "clear"))
        with ExitStack() as ctx:
            w = self.sb("msg_w", [P, 2, 2 * D], ctx=ctx)
            bias = self.sb("msg_bias", [NT, D], ctx=ctx)
            out = self.sb("msg_out", [NT, NB, 2 * D], ctx=ctx)
            zero = self.sb("msg_zero", [P, D], ctx=ctx)
            ps_source = [self.ps(f"msg_table_ps_s{k}", [NT, D], ctx) for k in range(2)]
            ps_window = [self.ps(f"msg_table_ps_w{k}", [NT, D], ctx) for k in range(2)]
            with nc.Block() as block:
                @block.sync
                def _(sp):
                    for half in range(2):
                        sp.dma_start(w[:, :, half * D:(half + 1) * D],
                                     a["L0_gnn_W_msg"][half * D:(half + 1) * D, :].rearrange("(k p) n -> p k n", p=P)
                                     ).then_inc(loads, 16)
                    sp.dma_start(bias[:], self.row(a["L0_gnn_b_msg"])).then_inc(loads, 16)
                    sp.wait_ge(clear, 1)
                    sp.dma_start(self.window_table[N:WN, :], zero[:]).then_inc(stores, 16)
                    for b in range(NB):
                        sp.wait_ge(copied, b + 1)
                        sp.dma_start(self.source_table[b * NT:(b + 1) * NT, :], out[:, b, 0:D]).then_inc(stores, 16)
                        sp.wait_ge(biased, b + 1)
                        sp.dma_start(self.window_table[b * NT:(b + 1) * NT, :], out[:, b, D:2 * D]).then_inc(stores, 16)
                    sp.wait_ge(stores, 16 * (2 * NB + 1))

                @block.gpsimd
                def _(pool):
                    nc.gpsimd.memset(zero[:], 0.0).then_inc(clear, 1)
                    nc.gpsimd.memset(self.aggT[:], 0.0)

                @block.tensor
                def _(pe):
                    pe.wait_ge(loads, 48)
                    for b in range(NB):
                        if b >= 2:
                            pe.wait_ge(copied, b - 1)
                            pe.wait_ge(biased, b - 1)
                        for half, ps in enumerate((ps_source, ps_window)):
                            for k in range(2):
                                last = nc.tensor.matmul(ps[b % 2][:], self.hT[:, k, b * NT:(b + 1) * NT],
                                                        w[:, k, half * D:(half + 1) * D], start=k == 0, stop=k == 1)
                        last.then_inc(made, 1)

                @block.scalar
                def _(act):
                    for b in range(NB):
                        act.wait_ge(made, b + 1)
                        nc.scalar.copy(out[:, b, 0:D], ps_source[b % 2][:]).then_inc(copied, 1)

                @block.vector
                def _(dve):
                    dve.wait_ge(loads, 48)
                    for b in range(NB):
                        dve.wait_ge(made, b + 1)
                        nc.vector.tensor_tensor(out[:, b, D:2 * D], ps_window[b % 2][:], bias[:],
                                                ALU.add).then_inc(biased, 1)

    def message_update(self):
        nc, a = self.nc, self.a
        loads, made, added, relued, chain, root, scaled = (self.sem(f"upd_{k}") for k in (
            "loads", "made", "added", "relued", "chain", "root", "scaled"))
        u = self.h
        with ExitStack() as ctx:
            w = self.sb("upd_w", [P, 4, D], ctx=ctx)
            bias, gamma, beta = (self.sb(f"upd_{k}", [NT, D], ctx=ctx) for k in ("bias", "gamma", "beta"))
            st = self.sb("upd_st", [NT, NB, 6], ctx=ctx)
            mv = self.sb("upd_mv", [NT, NB, 2], ctx=ctx)
            sd, rs, nm = (self.sb(f"upd_{k}", [NT, NB], ctx=ctx) for k in ("sd", "rs", "nm"))
            ps = [self.ps(f"upd_ps{k}", [NT, D], ctx) for k in range(2)]
            with nc.Block() as block:
                @block.sync
                def _(sp):
                    sp.dma_start(w[:], a["L0_gnn_W_upd"].rearrange("(k p) n -> p k n", p=P)).then_inc(loads, 16)
                    for t, k in ((bias, "b_upd"), (gamma, "gamma"), (beta, "beta")):
                        sp.dma_start(t[:], self.row(a[f"L0_gnn_{k}"])).then_inc(loads, 16)

                @block.tensor
                def _(pe):
                    pe.wait_ge(loads, 64)
                    for b in range(NB):
                        if b >= 2:
                            pe.wait_ge(added, b - 1)
                        for k in range(4):
                            src = self.hT if k < 2 else self.aggT
                            last = nc.tensor.matmul(ps[b % 2][:], src[:, k % 2, b * NT:(b + 1) * NT], w[:, k, :],
                                                    start=k == 0, stop=k == 3)
                        last.then_inc(made, 1)

                @block.scalar
                def _(act):
                    for b in range(NB):
                        act.wait_ge(added, b + 1)
                        nc.scalar.activation(u[:, b, :], u[:, b, :], ACT.Relu).then_inc(relued, 1)
                    act.wait_ge(chain, 2 * NB + 1)
                    nc.scalar.activation(sd[:], sd[:], ACT.Sqrt).then_inc(root, 1)
                    act.wait_ge(chain, 2 * NB + 3)
                    for b in range(NB):
                        nc.scalar.activation(u[:, b, :], u[:, b, :], ACT.Identity, scale=rs[:, b:b + 1],
                                             bias=nm[:, b:b + 1]).then_inc(scaled, 1)

                @block.vector
                def _(dve):
                    dve.wait_ge(loads, 64)
                    for b in range(NB + 1):
                        if b < NB:
                            dve.wait_ge(made, b + 1)
                            nc.vector.tensor_tensor(u[:, b, :], ps[b % 2][:], bias[:], ALU.add).then_inc(added, 1)
                        if b > 0:
                            dve.wait_ge(relued, b)
                            nc.vector.bn_stats(st[:, b - 1, :], u[:, b - 1, :]).then_inc(chain, 1)
                    for b in range(NB):
                        dve.wait_ge(chain, NB + b)
                        nc.vector.bn_aggr(mv[:, b, :], st[:, b, :]).then_inc(chain, 1)
                    dve.wait_ge(chain, 2 * NB)
                    nc.vector.tensor_scalar(sd[:], mv[:, :, 1], EPS, None, ALU.add).then_inc(chain, 1)
                    dve.wait_ge(root, 1)
                    nc.vector.reciprocal(rs[:], sd[:]).then_inc(chain, 1)
                    dve.wait_ge(chain, 2 * NB + 2)
                    nc.vector.scalar_tensor_tensor(out=nm[:], in0=mv[:, :, 0], scalar=-1.0, in1=rs[:],
                                                   op0=ALU.mult, op1=ALU.mult).then_inc(chain, 1)
                    nc.vector.tensor_tensor(self.x[:], self.x[:], beta[:].unsqueeze(1).to_broadcast([NT, NB, D]),
                                            ALU.add).then_inc(chain, 1)
                    for b in range(NB):
                        dve.wait_ge(scaled, b + 1)
                        nc.vector.tensor_tensor(u[:, b, :], u[:, b, :], gamma[:], ALU.mult).then_inc(chain, 1)
                        if b > 0:
                            dve.wait_ge(chain, 2 * NB + 4 + b)
                            nc.vector.tensor_tensor(self.x[:, b - 1, :], self.x[:, b - 1, :], u[:, b - 1, :], ALU.add)
                    dve.wait_ge(chain, 3 * NB + 4)
                    nc.vector.tensor_tensor(self.x[:, NB - 1, :], self.x[:, NB - 1, :], u[:, NB - 1, :], ALU.add)

    def mlp(self, maxT, sums):
        nc, a = self.nc, self.a
        loads, chain, spread, graph, b1_made, hidden, relued, outer, added, based = (self.sem(f"mlp_{k}") for k in (
            "loads", "chain", "spread", "graph", "b1_made", "hidden", "relued", "outer", "added", "based"))
        HB = HID // P
        with ExitStack() as ctx:
            w1 = self.sb("mlp_w1", [P, 6, HID], ctx=ctx)
            w2 = self.sb("mlp_w2", [P, HB, D], ctx=ctx)
            b1 = self.sb("mlp_b1", [P, HB], ctx=ctx)
            b2 = self.sb("mlp_b2", [NT, D], ctx=ctx)
            u0 = self.sb("mlp_u0", [U, 1], ctx=ctx)
            hid = self.sb("mlp_hid", [P, HB, CH], ctx=ctx)
            mean = self.sb("mlp_mean", [AF, N], ctx=ctx)
            pick = self.sb("mlp_pick", [AF + 1, AF], ctx=ctx)
            ps_g = self.ps("mlp_ps_g", [P, HB], ctx)
            ps_h = [self.ps(f"mlp_ps_h{k}", [P, 512], ctx) for k in range(3)]
            ps_o = [self.ps(f"mlp_ps_o{k}", [NT, D], ctx) for k in range(2)]
            parts = [(0, P), (P, P), (D, AF), (D + AF, AF), (D + 2 * AF, AF), (D + 3 * AF, U)]
            with nc.Block() as block:
                @block.sync
                def _(sp):
                    for k, (r, n) in enumerate(parts):
                        sp.dma_start(w1[0:n, k, :], a["L1_gnn_W1"][r:r + n, :]).then_inc(loads, 16)
                    sp.dma_start(w2[:], a["L1_gnn_W2"].rearrange("(k p) n -> p k n", p=P)).then_inc(loads, 16)
                    sp.dma_start(b1[:], a["L1_gnn_b1"].rearrange("(k p) -> p k", p=P),
                                 allow_slow_non_contiguous=True).then_inc(loads, 16)
                    sp.dma_start(b2[:], self.row(a["L1_gnn_b2"])).then_inc(loads, 16)
                    sp.dma_start(u0[:], a["L1_gnn_u"][0:1, :].rearrange("o f -> f o"),
                                 allow_slow_non_contiguous=True).then_inc(loads, 16)

                @block.gpsimd
                def _(pool):
                    nc.gpsimd.tensor_tensor(self.x[:], self.x[:], self.h[:], ALU.add).then_inc(based, 1)
                    pool.wait_ge(loads, 160)
                    pool.wait_ge(based, 1)
                    nc.gpsimd.tensor_tensor(self.x[:], self.x[:], b2[:].unsqueeze(1).to_broadcast([NT, NB, D]),
                                            ALU.add).then_inc(based, 1)

                @block.vector
                def _(dve):
                    nc.vector.tensor_scalar(pick[:], self.ones[0:AF + 1, 0:AF], self.partition[0:AF + 1, 0:1],
                                            float(AF), ALU.mult, ALU.is_equal).then_inc(chain, 1)
                    for c, (c0, cn) in enumerate(CHUNKS):
                        dve.wait_ge(spread, c + 1)
                        cnt = mean[:, c0:c0 + cn]
                        nc.vector.tensor_scalar(cnt, ps_h[c % 3][0:AF, 0:cn], 1.0, None, ALU.max).then_inc(chain, 1)
                        dve.wait_ge(chain, 3 * c + 2)
                        nc.vector.reciprocal(cnt, cnt).then_inc(chain, 1)
                        dve.wait_ge(chain, 3 * c + 3)
                        nc.vector.tensor_tensor(cnt, cnt, sums[0:AF, c0:c0 + cn], ALU.mult).then_inc(chain, 1)
                    dve.wait_ge(graph, 1)
                    nc.vector.tensor_tensor(b1[:], b1[:], ps_g[:], ALU.add).then_inc(b1_made, 1)
                    dve.wait_ge(based, 2)
                    for b in range(NB):
                        dve.wait_ge(outer, b + 1)
                        nc.vector.tensor_tensor(self.x[:, b, :], self.x[:, b, :], ps_o[b % 2][:], ALU.add
                                                ).then_inc(added, 1)

                @block.scalar
                def _(act):
                    act.wait_ge(b1_made, 1)
                    n = 0
                    for c, (c0, cn) in enumerate(CHUNKS):
                        for k in range(HB):
                            act.wait_ge(hidden, n + 1)
                            if c > 0 and k == 0:
                                act.wait_ge(outer, CH // NT * c)
                            nc.scalar.activation(hid[:, k, 0:cn], ps_h[n % 3][:, 0:cn], ACT.Relu,
                                                 bias=b1[:, k:k + 1]).then_inc(relued, 1)
                            n += 1

                @block.tensor
                def _(pe):
                    pe.wait_ge(loads, 160)
                    for k in range(HB):
                        last = nc.tensor.matmul(ps_g[:, k:k + 1], w1[0:U, 5, k * P:(k + 1) * P], u0[:],
                                                start=True, stop=True)
                    last.then_inc(graph, 1)
                    pe.wait_ge(chain, 1)
                    for c, (c0, cn) in enumerate(CHUNKS):
                        if c >= 3:
                            pe.wait_ge(chain, 3 * (c - 3) + 2)
                        nc.tensor.matmul(ps_h[c % 3][0:AF, 0:cn], pick[:], sums[:, c0:c0 + cn],
                                         start=True, stop=True).then_inc(spread, 1)
                    pe.wait_ge(chain, 3 * len(CHUNKS) + 1)
                    n = b = 0
                    for c0, cn in CHUNKS:
                        moving = [self.hT[:, 0, c0:c0 + cn], self.hT[:, 1, c0:c0 + cn], sums[0:AF, c0:c0 + cn],
                                  maxT[:, 0, c0:c0 + cn], mean[:, c0:c0 + cn]]
                        for k in range(HB):
                            if n >= 3:
                                pe.wait_ge(relued, n - 2)
                            for j, m in enumerate(moving):
                                last = nc.tensor.matmul(ps_h[n % 3][:, 0:cn], w1[0:parts[j][1], j, k * P:(k + 1) * P],
                                                        m, start=j == 0, stop=j == len(moving) - 1)
                            last.then_inc(hidden, 1)
                            n += 1
                        pe.wait_ge(relued, n)
                        for t in range(cn // NT):
                            if b >= 2:
                                pe.wait_ge(added, b - 1)
                            for k in range(HB):
                                last = nc.tensor.matmul(ps_o[b % 2][:], hid[:, k, t * NT:(t + 1) * NT], w2[:, k, :],
                                                        start=k == 0, stop=k == HB - 1)
                            last.then_inc(outer, 1)
                            b += 1

    def attention_tables(self):
        nc, a = self.nc, self.a
        AW = D + H
        folds_made = 0
        self.attention_table = nc.dram_tensor("att_table", [N, AW], F32).ap()
        self.head_table = nc.dram_tensor("att_heads", [N, H], F32).ap()
        loads, clears, marks, chain, turned, folded, rhs, made, kept, dmade, dkept, stores = (
            self.sem(f"att_{k}") for k in ("loads", "clears", "marks", "chain", "turned", "folded", "rhs", "made",
                                           "kept", "dmade", "dkept", "stores"))
        with ExitStack() as ctx:
            wc = self.sb("att_wc", [P, 2, D], ctx=ctx)
            wp = self.sb("att_wp", [U, P], ctx=ctx)
            av = self.sb("att_av", [P, 2, 2], ctx=ctx)
            ap = self.sb("att_ap", [U, 2], ctx=ctx)
            comb = self.sb("att_comb", [P, H, 2], ctx=ctx)
            own = self.sb("att_own", [P, 2, H], ctx=ctx)
            own_b = self.sb("att_own_b", [P, 2, H], ctx=ctx)
            own_p = self.sb("att_own_p", [U, H], ctx=ctx)
            own_pb = self.sb("att_own_pb", [U, H], ctx=ctx)
            fold = self.sb("att_fold", [P, 2, 2, H], ctx=ctx)
            fold_p = self.sb("att_fold_p", [U, 2, H], ctx=ctx)
            w = self.sb("att_w", [P, 2, D + 2 * H], ctx=ctx)
            out = self.sb("att_out", [NT, NB, AW], ctx=ctx)
            ps_t = self.ps("att_ps_t", [P, 2, 2, P], ctx)
            ps_v = self.ps("att_ps_v", [P, 2, 2 * H], ctx)
            ps = [self.ps(f"att_ps{k}", [NT, D + 2 * H], ctx) for k in range(2)]
            ps_d = [self.ps(f"att_ps_d{k}", [H, 512], ctx) for k in range(2)]
            with nc.Block() as block:
                @block.sync
                def _(sp):
                    sp.wait_ge(clears, 2)
                    sp.dma_start(wc[:, :, 0:CD], a["L2_gnn_Wc"].rearrange("(k p) n -> p k n", p=P)).then_inc(loads, 16)
                    sp.dma_start(wp[:, P - POS:P], a["L2_gnn_Wp"]).then_inc(loads, 16)
                    for k, name in enumerate(("src", "dst")):
                        sp.dma_start(av[:, :, k:k + 1], a[f"L2_gnn_attn_{name}"].rearrange(
                            "o (k g) d -> (g d) k o", k=2), allow_slow_non_contiguous=True).then_inc(loads, 16)
                        sp.dma_start(ap[:, k:k + 1], a[f"L2_gnn_pos_attn_{name}"].rearrange("o h d -> (h d) o"),
                                     allow_slow_non_contiguous=True).then_inc(loads, 16)
                    sp.dma_start(comb[:], a["L2_gnn_att_comb"].partition_broadcast(P)).then_inc(loads, 16)
                    for b in range(NB):
                        sp.wait_ge(kept, b + 1)
                        sp.dma_start(self.attention_table[b * NT:(b + 1) * NT, :], out[:, b, :]).then_inc(stores, 16)
                        sp.dma_start(self.head_table[b * NT:(b + 1) * NT, :], out[:, b, D:AW]).then_inc(stores, 16)
                    sp.wait_ge(stores, 32 * NB)

                @block.gpsimd
                def _(pool):
                    nc.gpsimd.memset(wc[:], 0.0).then_inc(clears, 1)
                    nc.gpsimd.memset(wp[:], 0.0).then_inc(clears, 1)
                    nc.gpsimd.iota(own[:], pattern=[[P, 2], [-HD, H]], base=0, channel_multiplier=1,
                                   allow_small_or_imprecise_dtypes=True).then_inc(marks, 1)
                    nc.gpsimd.iota(own_p[:], pattern=[[-POS, H]], base=0, channel_multiplier=1,
                                   allow_small_or_imprecise_dtypes=True).then_inc(marks, 1)
                    nc.gpsimd.memset(self.aggT[:], 0.0)
                    nc.gpsimd.memset(self.denomT[:], 0.0)

                @block.vector
                def _(dve):
                    nonlocal folds_made
                    steps = 0

                    def link(ins):
                        nonlocal steps
                        steps += 1
                        ins.then_inc(chain, 1)
                        dve.wait_ge(chain, steps)
                    dve.wait_ge(marks, 2)
                    for dist, less, size in ((own, own_b, HD), (own_p, own_pb, POS)):
                        link(nc.vector.tensor_scalar(less[:], dist[:], float(size), None, ALU.is_lt))
                        link(nc.vector.tensor_scalar(dist[:], dist[:], 0.0, None, ALU.is_ge))
                        link(nc.vector.tensor_tensor(dist[:], dist[:], less[:], ALU.mult))
                    dve.wait_ge(loads, 16 * 7)
                    for blk in range(2):
                        link(nc.vector.tensor_tensor(own_b[:, blk, :], own[:, blk, :], comb[:, :, 0], ALU.mult))
                        for k in range(2):
                            link(nc.vector.tensor_scalar(fold[:, blk, k, :], own_b[:, blk, :], av[:, blk, k:k + 1],
                                                         None, ALU.mult))
                    link(nc.vector.tensor_tensor(own_pb[:], own_p[:], comb[0:U, :, 1], ALU.mult))
                    for k in range(2):
                        link(nc.vector.tensor_scalar(fold_p[:, k, :], own_pb[:], ap[:, k:k + 1], None, ALU.mult))
                    folds_made = steps
                    dve.wait_ge(turned, 1)
                    nc.vector.tensor_copy(w[:, :, 0:D], ps_t[:].rearrange("p i f n -> p i (f n)")).then_inc(rhs, 1)
                    dve.wait_ge(folded, 1)
                    nc.vector.tensor_copy(w[:, :, D:D + 2 * H], ps_v[:]).then_inc(rhs, 1)
                    for c, (c0, cn) in enumerate(CHUNKS):
                        dve.wait_ge(dmade, c + 1)
                        nc.vector.tensor_copy(self.dstT[:, c0:c0 + cn], ps_d[c % 2][:, 0:cn]).then_inc(dkept, 1)

                @block.tensor
                def _(pe):
                    pe.wait_ge(loads, 16 * 7)
                    for i in range(2):
                        for f in range(2):
                            last = nc.tensor.transpose(ps_t[:, i, f, :], wc[:, f, i * P:(i + 1) * P], self.ident[:])
                    last.then_inc(turned, 1)
                    pe.wait_ge(chain, folds_made)
                    for i in range(2):
                        for f in range(2):
                            last = nc.tensor.matmul(ps_v[:, i, :], wc[:, f, i * P:(i + 1) * P],
                                                    fold[:, f, :, :].rearrange("p k h -> p (k h)"),
                                                    start=f == 0, stop=i == 0 and f == 1)
                    nc.tensor.matmul(ps_v[:, 1, :], wp[:], fold_p[:].rearrange("p k h -> p (k h)"),
                                     start=False, stop=True).then_inc(folded, 1)
                    pe.wait_ge(rhs, 2)
                    for b in range(NB):
                        if b >= 2:
                            pe.wait_ge(kept, b - 1)
                        for k in range(2):
                            last = nc.tensor.matmul(ps[b % 2][:], self.hT[:, k, b * NT:(b + 1) * NT], w[:, k, :],
                                                    start=k == 0, stop=k == 1)
                        last.then_inc(made, 1)
                    for c, (c0, cn) in enumerate(CHUNKS):
                        if c >= 2:
                            pe.wait_ge(dkept, c - 1)
                        for k in range(2):
                            last = nc.tensor.matmul(ps_d[c % 2][:, 0:cn], w[:, k, D + H:D + 2 * H],
                                                    self.hT[:, k, c0:c0 + cn], start=k == 0, stop=k == 1)
                        last.then_inc(dmade, 1)

                @block.scalar
                def _(act):
                    for b in range(NB):
                        act.wait_ge(made, b + 1)
                        nc.scalar.copy(out[:, b, :], ps[b % 2][:, 0:AW]).then_inc(kept, 1)

    def logit_table(self, largestT):
        nc = self.nc
        self.logit_rows = nc.dram_tensor("logit_window_table", [WN, 2 * H], F32).ap()
        chain, made, kept, clear, stores = (self.sem(f"log_{k}") for k in ("chain", "made", "kept", "clear", "stores"))
        with ExitStack() as ctx:
            out = self.sb("log_out", [NT, NB, 2 * H], ctx=ctx)
            zero = self.sb("log_zero", [P, 2 * H], ctx=ctx)
            ps = self.ps("log_ps", [NT, NB, 2 * H], ctx)
            with nc.Block() as block:
                @block.gpsimd
                def _(pool):
                    nc.gpsimd.memset(zero[:], 0.0).then_inc(clear, 1)

                @block.vector
                def _(dve):
                    m, d = largestT[:, 0, 0:N], self.dstT[:, 0:N]
                    nc.vector.tensor_tensor(m, m, d, ALU.add).then_inc(chain, 1)
                    dve.wait_ge(chain, 1)
                    nc.vector.scalar_tensor_tensor(out=m, in0=m, scalar=0.2, in1=m, op0=ALU.mult,
                                                   op1=ALU.max).then_inc(chain, 1)
                    dve.wait_ge(made, 1)
                    nc.vector.tensor_copy(out[:], ps[:]).then_inc(kept, 1)

                @block.tensor
                def _(pe):
                    pe.wait_ge(chain, 2)
                    for b in range(NB):
                        nodes = slice(b * NT, (b + 1) * NT)
                        nc.tensor.transpose(ps[:, b, 0:H], self.dstT[:, nodes], self.ident[0:H, 0:H])
                        last = nc.tensor.transpose(ps[:, b, H:2 * H], largestT[:, 0, nodes], self.ident[0:H, 0:H])
                    last.then_inc(made, 1)

                @block.sync
                def _(sp):
                    sp.wait_ge(clear, 1)
                    sp.dma_start(self.logit_rows[N:WN, :], zero[:]).then_inc(stores, 16)
                    sp.wait_ge(kept, 1)
                    sp.dma_start(self.logit_rows[0:N, :].rearrange("(b p) k -> p b k", p=NT), out[:]).then_inc(stores, 16)
                    sp.wait_ge(stores, 32)

    def attention_update(self):
        nc = self.nc
        marks, chain, spread, inverted, divided, turned, added, based = (self.sem(f"fin_{k}") for k in (
            "marks", "chain", "spread", "inverted", "divided", "turned", "added", "based"))
        with ExitStack() as ctx:
            own = self.sb("fin_own", [H, D], ctx=ctx)
            less = self.sb("fin_less", [H, D], ctx=ctx)
            inv = self.sb("fin_inv", [P, 2, 512], ctx=ctx)
            ps_d = [self.ps(f"fin_ps_d{k}", [P, 512], ctx) for k in range(2)]
            ps = [self.ps(f"fin_ps{k}", [NT, D], ctx) for k in range(2)]
            with nc.Block() as block:
                @block.gpsimd
                def _(pool):
                    nc.gpsimd.iota(own[:], pattern=[[1, D]], base=0, channel_multiplier=-HD,
                                   allow_small_or_imprecise_dtypes=True).then_inc(marks, 1)
                    nc.gpsimd.tensor_tensor(self.x[:], self.x[:], self.h[:], ALU.add).then_inc(based, 1)

                @block.vector
                def _(dve):
                    den = self.denomT[:, 0:N]
                    nc.vector.tensor_scalar(den, den, 1e-30, None, ALU.max).then_inc(chain, 1)
                    dve.wait_ge(marks, 1)
                    nc.vector.tensor_scalar(less[:], own[:], float(HD), None, ALU.is_lt).then_inc(chain, 1)
                    dve.wait_ge(chain, 2)
                    nc.vector.tensor_scalar(own[:], own[:], 0.0, None, ALU.is_ge).then_inc(chain, 1)
                    dve.wait_ge(chain, 3)
                    nc.vector.tensor_tensor(own[:], own[:], less[:], ALU.mult).then_inc(chain, 1)
                    n = 0
                    for c0, cn in CHUNKS:
                        for k in range(2):
                            dve.wait_ge(spread, n + 1)
                            nc.vector.reciprocal(inv[:, n % 2, 0:cn], ps_d[n % 2][:, 0:cn]).then_inc(inverted, 1)
                            dve.wait_ge(inverted, n + 1)
                            at = self.aggT[:, k, c0:c0 + cn]
                            nc.vector.tensor_tensor(at, at, inv[:, n % 2, 0:cn], ALU.mult).then_inc(divided, 1)
                            n += 1
                    dve.wait_ge(based, 1)
                    for b in range(NB):
                        dve.wait_ge(turned, b + 1)
                        nc.vector.tensor_tensor(self.x[:, b, :], self.x[:, b, :], ps[b % 2][:], ALU.add
                                                ).then_inc(added, 1)

                @block.tensor
                def _(pe):
                    pe.wait_ge(chain, 4)
                    n = 0
                    for c0, cn in CHUNKS:
                        for k in range(2):
                            if n >= 2:
                                pe.wait_ge(inverted, n - 1)
                            nc.tensor.matmul(ps_d[n % 2][:, 0:cn], own[:, k * P:(k + 1) * P],
                                             self.denomT[:, c0:c0 + cn], start=True, stop=True).then_inc(spread, 1)
                            n += 1
                    pe.wait_ge(divided, n)
                    for b in range(NB):
                        if b >= 2:
                            pe.wait_ge(added, b - 1)
                        for k in range(2):
                            last = nc.tensor.transpose(ps[b % 2][:, k * P:(k + 1) * P],
                                                       self.aggT[:, k, b * NT:(b + 1) * NT], self.ident[:])
                        last.then_inc(turned, 1)

    def pool_table(self):
        nc, a = self.nc, self.a
        loads, turned, kept, made, added, relued, stores = (self.sem(f"pool_{k}") for k in (
            "loads", "turned", "kept", "made", "added", "relued", "stores"))
        names = ("pool", "self", "neigh")
        self.wT = {k: self.sb(f"w_{k}T", [P, 2, D]) for k in names}
        with ExitStack() as ctx:
            raw = self.sb("pool_raw", [P, 3, 2, D], ctx=ctx)
            bias = self.sb("pool_bias", [NT, D], ctx=ctx)
            out = self.sb("pool_out", [NT, NB, D], ctx=ctx)
            ps_t = [self.ps(f"pool_ps_t{k}", [P, 2, 2, P], ctx) for k in range(3)]
            ps = [self.ps(f"pool_ps{k}", [NT, D], ctx) for k in range(2)]
            with nc.Block() as block:
                @block.sync
                def _(sp):
                    for k, name in enumerate(names):
                        sp.dma_start(raw[:, k, :, :], a[f"L3_gnn_W_{name}"].rearrange("(k p) n -> p k n", p=P)
                                     ).then_inc(loads, 16)
                    sp.dma_start(bias[:], self.row(a["L3_gnn_b_pool"])).then_inc(loads, 16)
                    for b in range(NB):
                        sp.wait_ge(relued, b + 1)
                        sp.dma_start(self.source_table[b * NT:(b + 1) * NT, :], out[:, b, :]).then_inc(stores, 16)
                    sp.wait_ge(stores, 16 * NB)

                @block.tensor
                def _(pe):
                    pe.wait_ge(loads, 64)
                    for k in range(3):
                        for i in range(2):
                            for o in range(2):
                                last = nc.tensor.transpose(ps_t[k][:, i, o, :], raw[:, k, o, i * P:(i + 1) * P],
                                                           self.ident[:])
                        last.then_inc(turned, 1)
                    pe.wait_ge(kept, 1)
                    for b in range(NB):
                        if b >= 2:
                            pe.wait_ge(added, b - 1)
                        for k in range(2):
                            last = nc.tensor.matmul(ps[b % 2][:], self.hT[:, k, b * NT:(b + 1) * NT],
                                                    self.wT["pool"][:, k, :], start=k == 0, stop=k == 1)
                        last.then_inc(made, 1)

                @block.vector
                def _(dve):
                    for k, name in enumerate(names):
                        dve.wait_ge(turned, k + 1)
                        nc.vector.tensor_copy(self.wT[name][:], ps_t[k][:].rearrange("p i o n -> p i (o n)")
                                              ).then_inc(kept, 1)
                    dve.wait_ge(loads, 64)
                    for b in range(NB):
                        dve.wait_ge(made, b + 1)
                        nc.vector.tensor_tensor(out[:, b, :], ps[b % 2][:], bias[:], ALU.add).then_inc(added, 1)

                @block.scalar
                def _(act):
                    for b in range(NB):
                        act.wait_ge(added, b + 1)
                        nc.scalar.activation(out[:, b, :], out[:, b, :], ACT.Relu).then_inc(relued, 1)

    def pool_update(self):
        nc, a = self.nc, self.a
        loads, made, biased, added, stores = (self.sem(f"out_{k}") for k in (
            "loads", "made", "biased", "added", "stores"))
        with ExitStack() as ctx:
            b_self, b_neigh = (self.sb(f"out_{k}", [NT, D], ctx=ctx) for k in ("b_self", "b_neigh"))
            ps = [self.ps(f"out_ps{k}", [NT, D], ctx) for k in range(2)]
            with nc.Block() as block:
                @block.sync
                def _(sp):
                    sp.dma_start(b_self[:], self.row(a["L3_gnn_b_self"])).then_inc(loads, 16)
                    sp.dma_start(b_neigh[:], self.row(a["L3_gnn_b_neigh"])).then_inc(loads, 16)
                    for b in range(NB):
                        sp.wait_ge(added, b + 1)
                        sp.dma_start(self.out[b * NT:(b + 1) * NT, :], self.x[:, b, :]).then_inc(stores, 16)
                    sp.wait_ge(stores, 16 * NB)

                @block.gpsimd
                def _(pool):
                    pool.wait_ge(loads, 32)
                    for k, bias in enumerate((b_self, b_neigh)):
                        if k:
                            pool.wait_ge(biased, k)
                        nc.gpsimd.tensor_tensor(self.x[:], self.x[:], bias[:].unsqueeze(1).to_broadcast([NT, NB, D]),
                                                ALU.add).then_inc(biased, 1)

                @block.tensor
                def _(pe):
                    for b in range(NB):
                        if b >= 2:
                            pe.wait_ge(added, b - 1)
                        for k in range(4):
                            src, w = (self.hT, self.wT["self"]) if k < 2 else (self.aggT, self.wT["neigh"])
                            last = nc.tensor.matmul(ps[b % 2][:], src[:, k % 2, b * NT:(b + 1) * NT], w[:, k % 2, :],
                                                    start=k == 0, stop=k == 3)
                        last.then_inc(made, 1)

                @block.vector
                def _(dve):
                    dve.wait_ge(biased, 2)
                    for b in range(NB):
                        dve.wait_ge(made, b + 1)
                        nc.vector.tensor_tensor(self.x[:, b, :], self.x[:, b, :], ps[b % 2][:], ALU.add
                                                ).then_inc(added, 1)


def build(nc, a, out):
    with ExitStack() as ctx:
        k = Kernel(nc, ctx, a, out)
        k.prepare()
        k.normalize("norm0")
        k.message_tables()
        k.sum_pass("msg", k.source_table, D, k.window_table, D, attention=False)
        k.message_update()
        k.normalize("norm1")
        with ExitStack() as layer:
            maxT = k.sb("maxT", [AF, 1, WN], ctx=layer)
            sums = k.sb("sums", [AF + 1, WN], ctx=layer)
            k.clear("attr_clear", sums)
            k.max_pass("attr", [AF], maxT, sums=sums)
            k.mlp(maxT, sums)
        k.normalize("norm2")
        with ExitStack() as layer:
            k.dstT = k.sb("dstT", [H, N], ctx=layer)
            k.denomT = k.sb("denomT", [H, WN], ctx=layer)
            largestT = k.sb("largestT", [H, 1, WN], ctx=layer)
            k.attention_tables()
            k.max_pass("logit", [H], largestT, table=k.head_table)
            k.logit_table(largestT)
            k.sum_pass("att", k.attention_table, D + H, k.logit_rows, 2 * H, attention=True)
            k.attention_update()
        k.normalize("norm3")
        k.pool_table()
        k.max_pass("pool_max", [P, P], k.aggT, table=k.source_table, weighted=True)
        k.pool_update()


_INS = ["x", "src", "dst", "edge_attr_96", "edge_weight1",
        "L0_gnn_W_msg", "L0_gnn_b_msg", "L0_gnn_W_upd", "L0_gnn_b_upd", "L0_gnn_gamma", "L0_gnn_beta",
        "L1_gnn_u", "L1_gnn_W1", "L1_gnn_b1", "L1_gnn_W2", "L1_gnn_b2",
        "L2_gnn_Wc", "L2_gnn_Wp", "L2_gnn_attn_src", "L2_gnn_attn_dst", "L2_gnn_pos_attn_src",
        "L2_gnn_pos_attn_dst", "L2_gnn_att_comb",
        "L3_gnn_W_pool", "L3_gnn_b_pool", "L3_gnn_W_self", "L3_gnn_b_self", "L3_gnn_W_neigh", "L3_gnn_b_neigh"]


def kernel(**inputs):
    import numpy as _np
    import concourse.bacc as _bacc
    from concourse import mybir as _mybir
    from concourse.bass_utils import run_bass_kernel_spmd as _run

    nc = _bacc.Bacc("TRN2", target_bir_lowering=False, num_devices=1)
    arrays, aps = {}, {}
    for name in _INS:
        arr = _np.ascontiguousarray(inputs[name])
        arrays[f"in_{name}"] = arr
        aps[name] = nc.dram_tensor(f"in_{name}", arr.shape, _mybir.dt.from_np(arr.dtype), kind="ExternalInput").ap()
    out = nc.dram_tensor("out_x", (N, D), F32, kind="ExternalOutput").ap()
    build(nc, aps, out)
    r = _run(nc, [arrays], core_ids=[0])
    return r.results[0]["out_x"]
```

```python
from contextlib import ExitStack

import concourse.bass as bass
from concourse import mybir

F32 = mybir.dt.float32
BF16 = mybir.dt.bfloat16
I32 = mybir.dt.int32
ALU = mybir.AluOpType
ACT = mybir.ActivationFunctionType

P = 128
N = 3125
E = 53125
D = 256
NT = 125
NB = N // NT
WN = N + P
TG = 4
GE = TG * P
SLOTS = 8
BUFS = 4
PAIR = 2
T = -(-E // (GE * SLOTS)) * TG * SLOTS
NG = T // TG
NI = NG // SLOTS
RQ = 4
RT = T // RQ
FULL = E // P
REST = E - FULL * P
AF = 96
U = 64
HID = 1024
H = 4
HD = 64
POS = 16
CD = D - POS
CREDIT = SLOTS + TG
FLT = 3.3895313892515355e38
EPS = 1e-5
BANK = 512
CH = 500
CHUNKS = [(c, min(CH, N - c)) for c in range(0, N, CH)]


def ready(i, s):
    return i * SLOTS + (s + 1 + CREDIT)


def freed(i, s, buffers):
    return i * SLOTS + (s + 1 + CREDIT - buffers)


def tiles_before(i, s, t):
    return i * (SLOTS * TG) + (s * TG + t + CREDIT)


def hold(eng, sem, value, least=1):
    value = value if isinstance(value, int) else eng.to_reg(value)
    eng.wait_ge(sem, least)
    eng.wait_ge(sem, value)


def pipelined(eng, stages):
    for g in range(-max(ahead for _, ahead in stages), 0):
        for stage, ahead in stages:
            if g + ahead >= 0:
                stage(0, g + ahead)
    with eng.Fori(0, NI - 1) as i:
        for s in range(SLOTS):
            for stage, ahead in stages:
                k = s + ahead
                stage(i + 1 if k >= SLOTS else i, k % SLOTS)
    for s in range(SLOTS):
        for stage, ahead in stages:
            if s + ahead < SLOTS:
                stage(NI - 1, s + ahead)


class Kernel:

    def __init__(self, nc, ctx, a, out):
        self.nc, self.ctx, self.a, self.out = nc, ctx, a, out
        self.before = {}
        sem = self.sem
        self.index_in = [sem(f"index_in{s}") for s in range(SLOTS // PAIR)]
        self.rows_in = [sem(f"rows_in{s}") for s in range(SLOTS)]
        self.line_in = [sem(f"line_in{s}") for s in range(BUFS // PAIR)]
        self.window_in = [sem(f"window_in{s}") for s in range(BUFS)]

    def sem(self, name):
        return self.ctx.enter_context(self.nc.semaphore(name))

    def sb(self, name, shape, dt=F32, ctx=None):
        return (ctx or self.ctx).enter_context(self.nc.sbuf_tensor(name, shape, dt))

    def ps(self, name, shape, ctx):
        size = 1
        for n in shape[1:]:
            size *= n
        banks = ctx.enter_context(self.nc.psum_tensor(name, [shape[0], -(-size // BANK) * BANK], F32))
        flat = banks[:, 0:size]
        if len(shape) == 3:
            return flat.rearrange("p (a b) -> p a b", a=shape[1])
        if len(shape) == 4:
            return flat.rearrange("p (a b c) -> p a b c", a=shape[1], b=shape[2])
        return flat

    def landed(self, semaphores, i, s, transfers=1, groups=1):
        n, turn = len(semaphores), s // groups
        sem = semaphores[turn % n]
        per_trip = 16 * transfers * SLOTS // (groups * n)
        return sem, i * per_trip + (self.before.get(sem.name, 0) + 16 * transfers * (turn // n + 1))

    def pass_over(self, semaphores, transfers=1, groups=1):
        for sem in semaphores:
            self.before[sem.name] = self.before.get(sem.name, 0) + 16 * transfers * NG // (groups * len(semaphores))

    def bases(self, engine, i, s):
        _, values = self.nc.values_load_multi_w_load_instructions(
            self.base[0:1, bass.ds(i * (SLOTS * TG) + s * TG, TG)], engines=[engine], min_val=0, max_val=N - 1,
            skip_runtime_bounds_check_because="destinations are node numbers")
        return values

    def prepare(self):
        nc, a, sb = self.nc, self.a, self.sb
        lines_made = 0
        self.x = sb("x", [NT, NB, D])
        self.hT = sb("hT", [P, 2, N])
        self.h = sb("h", [NT, NB, D])
        self.source = sb("source", [P, T], I32)
        self.place = sb("place", [P, T])
        self.place_end = sb("place_end", [P, T])
        self.is_end = sb("is_end", [P, T])
        self.weight = sb("weight", [P, T])
        self.base = sb("base", [1, T], I32)
        self.columns = sb("columns", [P, P])
        self.partition = sb("partition", [P, 1])
        self.ident = sb("ident", [P, P])
        self.ones = sb("ones", [P, P])
        self.aggT = sb("aggT", [P, 2, WN])
        self.place_line = nc.dram_tensor("place_line", [T * P], BF16).ap()
        self.mask_line = nc.dram_tensor("mask_line", [T * P], BF16).ap()
        loads, constants, chain = self.sem("prep_loads"), self.sem("prep_constants"), self.sem("prep_chain")
        clears, pe, stores = self.sem("prep_clears"), self.sem("prep_transposed"), self.sem("prep_stores")
        with ExitStack() as ctx:
            def tmp(name, shape, dt=F32):
                return self.sb(name, shape, dt, ctx)
            raw = {k: tmp(k, [RT, RQ, P], I32) for k in ("src_rows", "dst_rows")}
            w_rows = tmp("w_rows", [RT, RQ, P])
            before, after = tmp("before", [RT, RQ], I32), tmp("after", [RT, RQ], I32)
            src_f, dst_f, other = tmp("src_f", [RT, RQ, P]), tmp("dst_f", [RT, RQ, P]), tmp("other", [RT, RQ, P])
            before_f, after_f = tmp("before_f", [RT, RQ]), tmp("after_f", [RT, RQ])
            rel, rel_end, flag = tmp("rel", [RT, RQ, P]), tmp("rel_end", [RT, RQ, P]), tmp("flag", [RT, RQ, P])
            mask = tmp("mask", [RT, RQ, P], BF16)
            rel16 = tmp("rel16", [RT, RQ, P], BF16)
            psT = [self.ps(f"prep_ps{k}", [P, T], ctx) for k in range(4)]
            whole = (RQ - 1) * RT
            transfers = []
            for tile, flat in ((raw["src_rows"], a["src"]), (raw["dst_rows"], a["dst"]),
                               (w_rows, a["edge_weight1"].rearrange("e o -> (e o)"))):
                transfers += [
                    (tile[:, 0:RQ - 1, :], flat[0:whole * P].rearrange("(q r c) -> r q c", r=RT, c=P)),
                    (tile[0:FULL - whole, RQ - 1, :], flat[whole * P:FULL * P].rearrange("(r c) -> r c", c=P)),
                    (tile[FULL - whole:FULL - whole + 1, RQ - 1, 0:REST],
                     flat[FULL * P:E].rearrange("(r c) -> r c", r=1))]
            dst = a["dst"]
            ends = dst[P:FULL * P].rearrange("(j c) -> j c", c=P)[:, P - 1:P]
            firsts = dst[P:FULL * P].rearrange("(j c) -> j c", c=P)[:, 0:1]
            transfers += [(before[1:2, 0:1], dst[P - 1:P].rearrange("(r c) -> r c", r=1)),
                          (before[2:RT, 0:1], ends[0:RT - 2, :])]
            transfers += [(before[:, q:q + 1], ends[q * RT - 2:(q + 1) * RT - 2, :]) for q in range(1, RQ - 1)]
            transfers += [(before[0:FULL + 1 - whole, RQ - 1:RQ], ends[whole - 2:FULL - 1, :])]
            transfers += [(after[:, q:q + 1], firsts[q * RT:(q + 1) * RT, :]) for q in range(RQ - 1)]
            transfers += [(after[0:FULL - 1 - whole, RQ - 1:RQ], firsts[whole:FULL - 1, :]),
                          (after[FULL - 1 - whole:FULL - whole, RQ - 1:RQ],
                           dst[FULL * P:FULL * P + 1].rearrange("(r c) -> r c", r=1))]
            transfers += [(self.base[0:1, 0:FULL], dst[0:FULL * P].rearrange("(j c) -> c j", c=P)[0:1, :]),
                          (self.base[0:1, FULL:FULL + 1], dst[FULL * P:FULL * P + 1].rearrange("(r c) -> r c", r=1)),
                          (self.x[:, :, :], a["x"].rearrange("(b p) d -> p b d", p=NT))]
            with nc.Block() as block:
                @block.gpsimd
                def _(pool):
                    nc.gpsimd.iota(self.columns[:], pattern=[[1, P]], base=0, channel_multiplier=0,
                                   allow_small_or_imprecise_dtypes=True).then_inc(constants, 1)
                    nc.gpsimd.iota(self.partition[:], pattern=[[0, 1]], base=0, channel_multiplier=1,
                                   allow_small_or_imprecise_dtypes=True).then_inc(constants, 1)

                @block.vector
                def _(dve):
                    nonlocal lines_made
                    steps = 0

                    def link(ins):
                        nonlocal steps
                        steps += 1
                        ins.then_inc(chain, 1)
                        dve.wait_ge(chain, steps)
                    nc.vector.memset(raw["src_rows"][:], 0).then_inc(clears, 1)
                    nc.vector.memset(raw["dst_rows"][:], -1).then_inc(clears, 1)
                    nc.vector.memset(w_rows[:], 0.0).then_inc(clears, 1)
                    nc.vector.memset(before[:], -1).then_inc(clears, 1)
                    nc.vector.memset(after[:], -1).then_inc(clears, 1)
                    nc.vector.memset(self.ones[:], 1.0)
                    dve.wait_ge(constants, 2)
                    link(nc.vector.tensor_scalar(self.ident[:], self.columns[:], self.partition[:, 0:1], None,
                                                 ALU.is_equal))
                    dve.wait_ge(loads, 16 * len(transfers))
                    link(nc.vector.tensor_copy(src_f[:], raw["src_rows"][:]))
                    link(nc.vector.tensor_copy(dst_f[:], raw["dst_rows"][:]))
                    link(nc.vector.tensor_copy(before_f[:], before[:]))
                    link(nc.vector.tensor_copy(after_f[:], after[:]))
                    link(nc.vector.tensor_tensor(rel[:], dst_f[:], dst_f[:, :, 0:1].to_broadcast([RT, RQ, P]),
                                                 ALU.subtract))
                    link(nc.vector.tensor_copy(other[:, :, 0:P - 1], dst_f[:, :, 1:P]))
                    link(nc.vector.tensor_copy(other[:, :, P - 1:P], after_f[:].unsqueeze(2)))
                    link(nc.vector.tensor_tensor(flag[:], dst_f[:], other[:], ALU.not_equal))
                    link(nc.vector.scalar_tensor_tensor(out=rel_end[:], in0=rel[:], scalar=1.0, in1=flag[:],
                                                        op0=ALU.add, op1=ALU.mult))
                    link(nc.vector.tensor_scalar(rel_end[:], rel_end[:], -1.0, None, ALU.add))
                    link(nc.vector.tensor_copy(other[:, :, 1:P], dst_f[:, :, 0:P - 1]))
                    link(nc.vector.tensor_copy(other[:, :, 0:1], before_f[:].unsqueeze(2)))
                    link(nc.vector.tensor_tensor(flag[:], dst_f[:], other[:], ALU.not_equal))
                    link(nc.vector.tensor_scalar(other[:], flag[:], -FLT, FLT, ALU.mult, ALU.add))
                    link(nc.vector.scalar_tensor_tensor(out=mask[:], in0=flag[:], scalar=-FLT, in1=other[:],
                                                        op0=ALU.mult, op1=ALU.add))
                    link(nc.vector.tensor_copy(rel16[:], rel[:]))
                    lines_made = steps
                    for k, dst in enumerate((self.source, self.place, self.place_end, self.weight)):
                        dve.wait_ge(pe, k + 1)
                        nc.vector.tensor_copy(dst[:], psT[k][:])
                    dve.wait_ge(pe, 3)
                    nc.vector.tensor_scalar(self.is_end[:], psT[2][:], 0.0, None, ALU.is_ge)

                @block.tensor
                def _(t):
                    t.wait_ge(chain, lines_made)
                    for k, rows in enumerate((src_f, rel, rel_end, w_rows)):
                        for q in range(RQ):
                            last = nc.tensor.transpose(psT[k][:, q * RT:(q + 1) * RT], rows[:, q, :],
                                                       self.ident[0:RT, 0:RT])
                        last.then_inc(pe, 1)

                @block.sync
                def _(sp):
                    sp.wait_ge(clears, 5)
                    for tile, src in transfers:
                        sp.dma_start(tile, src, allow_slow_non_contiguous=True).then_inc(loads, 16)
                    sp.wait_ge(chain, lines_made)
                    sp.dma_start(self.mask_line.rearrange("(q r c) -> r q c", r=RT, c=P), mask[:]).then_inc(stores, 16)
                    sp.dma_start(self.place_line.rearrange("(q r c) -> r q c", r=RT, c=P), rel16[:]).then_inc(stores, 16)
                    sp.wait_ge(stores, 32)

    def normalize(self, name):
        nc = self.nc
        chain, root, rstd, made = (self.sem(f"{name}_{k}") for k in ("stats", "root", "rstd", "h"))
        turned, kept = self.sem(f"{name}_turned"), self.sem(f"{name}_kept")
        with ExitStack() as ctx:
            st = self.sb(f"{name}_st", [NT, NB, 6], ctx=ctx)
            mv = self.sb(f"{name}_mv", [NT, NB, 2], ctx=ctx)
            sd = self.sb(f"{name}_sd", [NT, NB], ctx=ctx)
            rs = self.sb(f"{name}_rs", [NT, NB], ctx=ctx)
            nm = self.sb(f"{name}_nm", [NT, NB], ctx=ctx)
            ps = [self.ps(f"{name}_ps{k}", [P, 2, P], ctx) for k in range(2)]
            with nc.Block() as block:
                @block.vector
                def _(dve):
                    for b in range(NB):
                        nc.vector.bn_stats(st[:, b, :], self.x[:, b, :]).then_inc(chain, 1)
                    for b in range(NB):
                        dve.wait_ge(chain, b + 1)
                        nc.vector.bn_aggr(mv[:, b, :], st[:, b, :]).then_inc(chain, 1)
                    dve.wait_ge(chain, 2 * NB)
                    nc.vector.tensor_scalar(sd[:], mv[:, :, 1], EPS, None, ALU.add).then_inc(chain, 1)
                    dve.wait_ge(root, 1)
                    nc.vector.reciprocal(rs[:], sd[:]).then_inc(chain, 1)
                    dve.wait_ge(chain, 2 * NB + 2)
                    nc.vector.scalar_tensor_tensor(out=nm[:], in0=mv[:, :, 0], scalar=-1.0, in1=rs[:],
                                                   op0=ALU.mult, op1=ALU.mult).then_inc(rstd, 1)
                    for b in range(NB):
                        dve.wait_ge(turned, b + 1)
                        nc.vector.tensor_copy(self.hT[:, :, b * NT:(b + 1) * NT], ps[b % 2][:, :, 0:NT]).then_inc(kept, 1)

                @block.scalar
                def _(act):
                    act.wait_ge(chain, 2 * NB + 1)
                    nc.scalar.activation(sd[:], sd[:], ACT.Sqrt).then_inc(root, 1)
                    act.wait_ge(rstd, 1)
                    for b in range(NB):
                        nc.scalar.activation(self.h[:, b, :], self.x[:, b, :], ACT.Relu, scale=rs[:, b:b + 1],
                                             bias=nm[:, b:b + 1]).then_inc(made, 1)

                @block.tensor
                def _(t):
                    for b in range(NB):
                        t.wait_ge(made, b + 1)
                        if b >= 2:
                            t.wait_ge(kept, b - 1)
                        for k in range(2):
                            last = nc.tensor.transpose(ps[b % 2][:, k, 0:NT], self.h[:, b, k * P:(k + 1) * P],
                                                       self.ident[0:NT, 0:NT])
                        last.then_inc(turned, 1)

    def clear(self, name, tile):
        with self.nc.Block() as block:
            @block.gpsimd
            def _(pool):
                self.nc.gpsimd.memset(tile[:], 0.0)

    def fetch_index(self, sp, index, i, s):
        sp.dma_start(index[:, s:s + PAIR, :], self.source[:, bass.ds(i * (SLOTS * TG) + s * TG, PAIR * TG)].rearrange(
            "p (g t) -> p g t", g=PAIR)).then_inc(self.index_in[s // PAIR], 16)

    def fetch_line(self, sp, line, row, i, s):
        b = s % BUFS
        sp.dma_start(line[:, b:b + PAIR, :].rearrange("p g e -> p (g e)"),
                     row[bass.ds(i * (SLOTS * GE) + s * GE, PAIR * GE)].partition_broadcast(P)
                     ).then_inc(self.line_in[b // PAIR], 16)

    def start_events(self, engine, events):
        for event in events:
            engine.sem_inc(event, CREDIT)

    def sum_pass(self, name, table, width, window_table, window_width, attention):
        nc = self.nc
        ev = {k: self.sem(f"{name}_{k}") for k in (
            "nodes_hot", "edges_hot", "expanded", "added", "weighed", "summed", "tile_added")
            + (("logit", "exps") if attention else ())}
        with ExitStack() as ctx:
            index = self.sb(f"{name}_index", [P, SLOTS, TG], I32, ctx)
            rows = self.sb(f"{name}_rows", [P, SLOTS, TG, width], ctx=ctx)
            line = self.sb(f"{name}_line", [P, BUFS, GE], BF16, ctx)
            window = self.sb(f"{name}_window", [P, BUFS, TG, window_width], ctx=ctx)
            by_node = self.sb(f"{name}_by_node", [P, BUFS, GE], ctx=ctx)
            by_edge = self.sb(f"{name}_by_edge", [P, BUFS, TG, P], ctx=ctx)
            logit = self.sb(f"{name}_logit", [P, 2, TG, H], ctx=ctx)
            exps = self.sb(f"{name}_exps", [P, BUFS, TG, H], ctx=ctx)
            ps_window = [self.ps(f"{name}_ps_window{b}", [P, TG, window_width], ctx) for b in range(2)]
            ps_sum = [self.ps(f"{name}_ps_sum{b}", [P, TG, 2, P], ctx) for b in range(2)]
            ps_den = [self.ps(f"{name}_ps_den{b}", [P, TG, P], ctx) for b in range(2)] if attention else None
            with nc.Block() as block:
                @block.sync
                def _(sp):
                    def fetch_index(i, s):
                        if s % PAIR == 0:
                            hold(sp, ev["added"], freed(i, s + PAIR - 1, SLOTS))
                            self.fetch_index(sp, index, i, s)

                    def fetch_window(i, s):
                        if s % PAIR == 0:
                            hold(sp, ev["nodes_hot"], freed(i, s + PAIR - 1, BUFS))
                            self.fetch_line(sp, line, self.place_line, i, s)
                        hold(sp, ev["expanded"], freed(i, s, BUFS))
                        for t, base in enumerate(self.bases(mybir.EngineType.SP, i, s)):
                            sp.dma_start(window[:, s % BUFS, t, :], window_table[bass.ds(base, P), :]
                                         ).then_inc(self.window_in[s % BUFS], 16)
                    pipelined(sp, [(fetch_index, 3), (fetch_window, 0)])

                @block.gpsimd
                def _(pool):
                    def gather(i, s):
                        hold(pool, *self.landed(self.index_in, i, s, groups=PAIR), least=16)
                        hold(pool, ev["summed"], freed(i, s, SLOTS))
                        for t in range(TG):
                            nc.gpsimd.indirect_dma_start(
                                rows[:, s, t, :], None, table,
                                bass.IndirectOffsetOnAxis(ap=index[:, s, t:t + 1], axis=0)
                            ).then_inc(self.rows_in[s], 16)
                    pipelined(pool, [(gather, 0)])

                @block.vector
                def _(dve):
                    self.start_events(dve, [ev[k] for k in ("nodes_hot", "edges_hot", "added", "tile_added")])

                    def by_nodes(i, s):
                        dve.wait_ge(ev["expanded"], freed(i, s, BUFS))
                        dve.wait_ge(*self.landed(self.line_in, i, s, groups=PAIR))
                        nc.vector.tensor_scalar(by_node[:, s % BUFS, :], line[:, s % BUFS, :],
                                                self.partition[:, 0:1], None, ALU.is_equal).then_inc(ev["nodes_hot"], 1)

                    def by_edges(i, s):
                        place = self.place[:, bass.ds(i * (SLOTS * TG) + s * TG, TG)]
                        dve.wait_ge(ev["summed"], freed(i, s, BUFS))
                        nc.vector.tensor_tensor(by_edge[:, s % BUFS, :, :],
                                                self.columns[:].unsqueeze(1).to_broadcast([P, TG, P]),
                                                place.unsqueeze(2).to_broadcast([P, TG, P]),
                                                ALU.is_equal).then_inc(ev["edges_hot"], 1)

                    def add(i, s):
                        dve.wait_ge(ev["expanded"], ready(i, s))
                        dve.wait_ge(*self.landed(self.rows_in, i, s, TG))
                        nc.vector.tensor_tensor(rows[:, s, :, :], ps_window[s % 2][:], rows[:, s, :, :],
                                                ALU.add).then_inc(ev["added"], 1)

                    def logit_step(i, s, k):
                        return i * (2 * SLOTS) + (2 * s + k + CREDIT)

                    def add_terms(i, s):
                        dve.wait_ge(ev["expanded"], ready(i, s))
                        dve.wait_ge(*self.landed(self.rows_in, i, s, TG))
                        dve.wait_ge(ev["exps"], freed(i, s, 2))
                        nc.vector.tensor_tensor(logit[:, s % 2, :, :], rows[:, s, :, D:D + H],
                                                ps_window[s % 2][:, :, 0:H], ALU.add).then_inc(ev["logit"], 1)

                    def leak(i, s):
                        dve.wait_ge(ev["logit"], logit_step(i, s, 1))
                        at = logit[:, s % 2, :, :]
                        nc.vector.scalar_tensor_tensor(out=at, in0=at, scalar=0.2, in1=at, op0=ALU.mult,
                                                       op1=ALU.max).then_inc(ev["logit"], 1)

                    def less_largest(i, s):
                        dve.wait_ge(ev["logit"], logit_step(i, s, 2))
                        at = logit[:, s % 2, :, :]
                        nc.vector.tensor_tensor(at, at, ps_window[s % 2][:, :, H:2 * H],
                                                ALU.subtract).then_inc(ev["added"], 1)

                    bases = []

                    def accumulate(i, s, t):
                        if t == 0:
                            bases[:] = self.bases(mybir.EngineType.DVE, i, s)
                            dve.wait_ge(ev["summed"], ready(i, s))
                        dve.wait_ge(ev["tile_added"], tiles_before(i, s, t))
                        if attention:
                            den = self.denomT[:, bass.ds(bases[t], P)]
                            nc.vector.tensor_tensor(den, den, ps_den[s % 2][0:H, t, :], ALU.add)
                        at = self.aggT[:, :, bass.ds(bases[t], P)]
                        nc.vector.tensor_tensor(at, at, ps_sum[s % 2][:, t, :, :], ALU.add
                                                ).then_inc(ev["tile_added"], 1)

                    def of_tile(stage, t):
                        return lambda i, s: stage(i, s, t)
                    acc = [of_tile(accumulate, t) for t in range(TG)]
                    if attention:
                        self.start_events(dve, [ev["logit"]])
                        pipelined(dve, [(acc[0], 0), (add_terms, 4), (by_nodes, 6), (acc[1], 0), (leak, 4),
                                        (by_edges, 4), (acc[2], 0), (less_largest, 4), (acc[3], 0)])
                    else:
                        pipelined(dve, [(acc[0], 0), (by_nodes, 5), (acc[1], 0), (by_edges, 4), (acc[2], 0),
                                        (add, 3), (acc[3], 0)])

                @block.scalar
                def _(act):
                    def relu(i, s):
                        act.wait_ge(ev["added"], ready(i, s))
                        nc.scalar.activation(rows[:, s, :, :], rows[:, s, :, :], ACT.Relu).then_inc(ev["weighed"], 1)

                    def exp(i, s):
                        act.wait_ge(ev["added"], ready(i, s))
                        act.wait_ge(ev["summed"], freed(i, s, BUFS))
                        nc.scalar.activation(exps[:, s % BUFS, :, :], logit[:, s % 2, :, :],
                                             ACT.Exp).then_inc(ev["exps"], 1)

                    def weigh(i, s):
                        act.wait_ge(ev["exps"], ready(i, s))
                        for t in range(TG):
                            for h in range(H):
                                head = rows[:, s, t, h * HD:(h + 1) * HD]
                                last = nc.scalar.activation(head, head, ACT.Copy, scale=exps[:, s % BUFS, t, h:h + 1])
                        last.then_inc(ev["weighed"], 1)
                    self.start_events(act, [ev["weighed"]] + ([ev["exps"]] if attention else []))
                    pipelined(act, [(exp, 3), (weigh, 2)] if attention else [(relu, 2)])

                @block.tensor
                def _(pe):
                    self.start_events(pe, [ev["expanded"], ev["summed"]])

                    def expand(i, s):
                        pe.wait_ge(ev["nodes_hot"], ready(i, s))
                        pe.wait_ge(*self.landed(self.window_in, i, s, TG))
                        pe.wait_ge(ev["added"], freed(i, s, 2))
                        for t in range(TG):
                            last = nc.tensor.matmul(ps_window[s % 2][:, t, :], by_node[:, s % BUFS, t * P:(t + 1) * P],
                                                    window[:, s % BUFS, t, :], start=True, stop=True)
                        last.then_inc(ev["expanded"], 1)

                    def gather_sums(i, s):
                        pe.wait_ge(ev["edges_hot"], ready(i, s))
                        pe.wait_ge(ev["weighed"], ready(i, s))
                        pe.wait_ge(ev["tile_added"], tiles_before(i, s, -TG))
                        for t in range(TG):
                            if attention:
                                nc.tensor.matmul(ps_den[s % 2][0:H, t, :], exps[:, s % BUFS, t, :],
                                                 by_edge[:, s % BUFS, t, :], start=True, stop=True)
                            for k in range(2):
                                last = nc.tensor.matmul(ps_sum[s % 2][:, t, k, :], rows[:, s, t, k * P:(k + 1) * P],
                                                        by_edge[:, s % BUFS, t, :], start=True, stop=True)
                        last.then_inc(ev["summed"], 1)
                    pipelined(pe, [(gather_sums, 1), (expand, 5 if attention else 4)])
        self.pass_over(self.index_in, groups=PAIR)
        self.pass_over(self.line_in, groups=PAIR)
        self.pass_over(self.rows_in, TG)
        self.pass_over(self.window_in, TG)

    def max_pass(self, name, blocks, outT, table=None, weighted=False, sums=None):
        nc = self.nc
        nk, width = len(blocks), sum(blocks)
        bw = blocks[0]
        attributes_in = [self.sem(f"{name}_in{s}") for s in range(SLOTS)] if table is None else None
        ev = {k: self.sem(f"{name}_{k}") for k in (
            "turned", "scanned", "back", "kept", "ends", "placed", "stored")
            + (("weighed",) if weighted else ()) + (("tile_added", "ones") if sums is not None else ())}
        with ExitStack() as ctx:
            index = self.sb(f"{name}_index", [P, SLOTS, TG], I32, ctx)
            rows = self.sb(f"{name}_rows", [P, SLOTS, TG, width + (sums is not None)], ctx=ctx)
            line = self.sb(f"{name}_line", [P, BUFS, GE], BF16, ctx)
            scan = self.sb(f"{name}_scan", [bw, 2, nk, GE], ctx=ctx)
            by_edge = self.sb(f"{name}_by_edge", [P, BUFS, TG, width], ctx=ctx)
            ends = self.sb(f"{name}_ends", [P, BUFS, TG, P], ctx=ctx)
            one = 2 if nk == 1 else 1
            ps_turned = [[self.ps(f"{name}_ps_turned{b}{k}", [bw, GE], ctx) for k in range(nk)] for b in range(one)]
            ps_back = [self.ps(f"{name}_ps_back{b}", [P, TG, width], ctx) for b in range(one)]
            ps_placed = [self.ps(f"{name}_ps_placed{b}", [bw, TG, nk, P], ctx) for b in range(2)]
            ps_sums = [self.ps(f"{name}_ps_sums{b}", [bw + 1, TG, P], ctx) if sums is not None else None
                       for b in range(2)]
            with nc.Block() as block:
                @block.sync
                def _(sp):
                    def mask(i, s):
                        if s % PAIR == 0:
                            hold(sp, ev["scanned"], freed(i, s + PAIR - 1, BUFS))
                            self.fetch_line(sp, line, self.mask_line, i, s)

                    def fetch_index(i, s):
                        if s % PAIR == 0:
                            hold(sp, ev["turned"], freed(i, s + PAIR - 1, SLOTS))
                            self.fetch_index(sp, index, i, s)

                    def fetch_attributes(i, s):
                        hold(sp, ev["placed"], freed(i, s, SLOTS))
                        if isinstance(i, int) and i == NI - 1 and s == SLOTS - 1:
                            left = FULL - (NG - 1) * TG
                            src = self.a["edge_attr_96"]
                            sp.dma_start(rows[:, s, 0:left, 0:width], src[(FULL - left) * P:FULL * P, :].rearrange(
                                "(t p) f -> p t f", p=P)).then_inc(attributes_in[s], 16)
                            sp.dma_start(rows[0:REST, s, left, 0:width], src[FULL * P:E, :]).then_inc(
                                attributes_in[s], 16)
                        else:
                            sp.dma_start(rows[:, s, :, 0:width], self.a["edge_attr_96"][
                                bass.ds(i * (SLOTS * GE) + s * GE, GE), :].rearrange("(t p) f -> p t f", p=P)
                            ).then_inc(attributes_in[s], 16)
                    pipelined(sp, [(fetch_index if table is not None else fetch_attributes, 3), (mask, 0)])

                if sums is not None:
                    @block.gpsimd
                    def _(pool):
                        nc.gpsimd.memset(rows[:, :, :, width:width + 1], 1.0).then_inc(ev["ones"], 1)

                if table is not None:
                    @block.gpsimd
                    def _(pool):
                        def gather(i, s):
                            hold(pool, *self.landed(self.index_in, i, s, groups=PAIR), least=16)
                            hold(pool, ev["turned"], freed(i, s, SLOTS))
                            for t in range(TG):
                                nc.gpsimd.indirect_dma_start(
                                    rows[:, s, t, :], None, table,
                                    bass.IndirectOffsetOnAxis(ap=index[:, s, t:t + 1], axis=0)
                                ).then_inc(self.rows_in[s], 16)
                        pipelined(pool, [(gather, 0)])

                def rows_landed(eng, i, s):
                    if table is not None:
                        eng.wait_ge(*self.landed(self.rows_in, i, s, TG))
                    else:
                        sem, value = self.landed(attributes_in, i, s)
                        last = isinstance(i, int) and i == NI - 1 and s == SLOTS - 1
                        eng.wait_ge(sem, value + 16 if last else value)

                def keep(eng, copy):
                    def stage(i, s):
                        eng.wait_ge(ev["back"], ready(i, s))
                        eng.wait_ge(ev["placed"], freed(i, s, BUFS))
                        copy(by_edge[:, s % BUFS, :, :], ps_back[s % one][:]).then_inc(ev["kept"], 1)
                    return stage

                @block.scalar
                def _(act):
                    self.start_events(act, [ev["stored"], ev["weighed"] if weighted else ev["kept"]])

                    def weigh(i, s, t):
                        if t == 0:
                            rows_landed(act, i, s)
                        w = self.weight[:, bass.ds(i * (SLOTS * TG) + (s * TG + t), 1)]
                        last = nc.scalar.activation(rows[:, s, t, :], rows[:, s, t, :], ACT.Copy, scale=w)
                        if t == TG - 1:
                            last.then_inc(ev["weighed"], 1)

                    bases = []

                    def store(i, s, t):
                        if t == 0:
                            bases[:] = self.bases(mybir.EngineType.Activation, i, s)
                            act.wait_ge(ev["placed"], ready(i, s))
                        act.wait_ge(ev["stored"], tiles_before(i, s, t))
                        nc.scalar.copy(outT[:, :, bass.ds(bases[t], P)], ps_placed[s % 2][:, t, :, :]
                                       ).then_inc(ev["stored"], 1)

                    def keep_ends(i, s, t):
                        if t == 0:
                            act.wait_ge(ev["back"], ready(i, s))
                            act.wait_ge(ev["placed"], freed(i, s, BUFS))
                        is_end = self.is_end[:, bass.ds(i * (SLOTS * TG) + (s * TG + t), 1)]
                        last = nc.scalar.activation(by_edge[:, s % BUFS, t, :], ps_back[s % one][:, t, :], ACT.Copy,
                                                    scale=is_end)
                        if t == TG - 1:
                            last.then_inc(ev["kept"], 1)

                    def of_tile(stage, t):
                        return lambda i, s: stage(i, s, t)
                    stages = []
                    for t in range(TG):
                        stages.append((of_tile(store, t), 0))
                        if weighted:
                            stages.append((of_tile(weigh, t), 5))
                    if sums is not None:
                        for t in range(TG):
                            stages.insert(2 * t + 1, (of_tile(keep_ends, t), 2))
                    elif not weighted:
                        stages.insert(1, (keep(act, nc.scalar.copy), 2))
                    pipelined(act, stages)

                @block.vector
                def _(dve):
                    self.start_events(dve, [ev["ends"]] + ([ev["tile_added"]] if sums is not None else []))
                    if weighted:
                        self.start_events(dve, [ev["kept"]])

                    def one_hots(i, s):
                        dve.wait_ge(ev["placed"], freed(i, s, BUFS))
                        place = self.place_end if sums is None else self.place
                        place = place[:, bass.ds(i * (SLOTS * TG) + s * TG, TG)]
                        nc.vector.tensor_tensor(ends[:, s % BUFS, :, :],
                                                self.columns[:].unsqueeze(1).to_broadcast([P, TG, P]),
                                                place.unsqueeze(2).to_broadcast([P, TG, P]),
                                                ALU.is_equal).then_inc(ev["ends"], 1)

                    def run_scan(i, s):
                        dve.wait_ge(*self.landed(self.line_in, i, s, groups=PAIR))
                        dve.wait_ge(ev["turned"], ready(i, s))
                        dve.wait_ge(ev["back"], freed(i, s, 2))
                        dve.wait_ge(ev["scanned"], freed(i, s, 1))
                        for k in range(nk):
                            last = nc.vector.tensor_tensor_scan(
                                scan[:, s % 2, k, :], line[0:bw, s % BUFS, :], ps_turned[s % one][k][:],
                                scan[:, 1 - s % 2, k, GE - 1:GE], ALU.min, ALU.max)
                        last.then_inc(ev["scanned"], 1)

                    bases = []

                    def accumulate(i, s, t):
                        if t == 0:
                            bases[:] = self.bases(mybir.EngineType.DVE, i, s)
                            dve.wait_ge(ev["placed"], ready(i, s))
                        dve.wait_ge(ev["tile_added"], tiles_before(i, s, t))
                        at = sums[:, bass.ds(bases[t], P)]
                        nc.vector.tensor_tensor(at, at, ps_sums[s % 2][:, t, :], ALU.add
                                                ).then_inc(ev["tile_added"], 1)

                    def of_tile(stage, t):
                        return lambda i, s: stage(i, s, t)
                    nc.vector.memset(scan[:, 1, :, GE - 1:GE], 0.0).then_inc(ev["scanned"], CREDIT)
                    if sums is not None:
                        acc = [of_tile(accumulate, t) for t in range(TG)]
                        pipelined(dve, [(acc[0], 0), (run_scan, 3), (acc[1], 0), (one_hots, 2), (acc[2], 0), (acc[3], 0)])
                    elif weighted:
                        pipelined(dve, [(run_scan, 3), (one_hots, 2), (keep(dve, nc.vector.tensor_copy), 2)])
                    else:
                        pipelined(dve, [(run_scan, 3), (one_hots, 2)])

                @block.tensor
                def _(pe):
                    self.start_events(pe, [ev["turned"], ev["back"], ev["placed"]])
                    if sums is not None:
                        pe.wait_ge(ev["ones"], 1)

                    def turn(i, s):
                        if weighted:
                            pe.wait_ge(ev["weighed"], ready(i, s))
                        else:
                            rows_landed(pe, i, s)
                        pe.wait_ge(ev["scanned"], freed(i, s, one))
                        for k in range(nk):
                            for t in range(TG):
                                last = nc.tensor.transpose(ps_turned[s % one][k][:, t * P:(t + 1) * P],
                                                           rows[:, s, t, k * bw:(k + 1) * bw], self.ident[:])
                        last.then_inc(ev["turned"], 1)

                    def turn_back(i, s):
                        hold(pe, ev["scanned"], ready(i, s))
                        hold(pe, ev["kept"], freed(i, s, one))
                        for t in range(TG):
                            for k in range(nk):
                                last = nc.tensor.transpose(ps_back[s % one][:, t, k * bw:(k + 1) * bw],
                                                           scan[:, s % 2, k, t * P:(t + 1) * P],
                                                           self.ident[0:bw, 0:bw])
                        last.then_inc(ev["back"], 1)

                    def put(i, s):
                        pe.wait_ge(ev["kept"], ready(i, s))
                        pe.wait_ge(ev["ends"], ready(i, s))
                        pe.wait_ge(ev["stored"], tiles_before(i, s, -TG))
                        if sums is not None:
                            pe.wait_ge(ev["tile_added"], tiles_before(i, s, -TG))
                        for t in range(TG):
                            if sums is not None:
                                nc.tensor.matmul(ps_sums[s % 2][:, t, :], rows[:, s, t, :], ends[:, s % BUFS, t, :],
                                                 start=True, stop=True)
                            for k in range(nk):
                                last = nc.tensor.matmul(ps_placed[s % 2][:, t, k, :],
                                                        by_edge[:, s % BUFS, t, k * bw:(k + 1) * bw],
                                                        ends[:, s % BUFS, t, :], start=True, stop=True)
                        last.then_inc(ev["placed"], 1)
                    pipelined(pe, [(turn_back, 2), (put, 1), (turn, 4)])
        self.pass_over(self.line_in, groups=PAIR)
        if table is not None:
            self.pass_over(self.index_in, groups=PAIR)
            self.pass_over(self.rows_in, TG)

    def row(self, vector, parts=NT):
        return vector.partition_broadcast(parts)

    def message_tables(self):
        nc, a = self.nc, self.a
        self.source_table = nc.dram_tensor("message_source_table", [N, D], F32).ap()
        self.window_table = nc.dram_tensor("message_window_table", [WN, D], F32).ap()
        loads, made, copied, biased, stores, clear = (self.sem(f"msg_{k}") for k in (
            "loads", "made", "copied", "biased", "stores", "clear"))
        with ExitStack() as ctx:
            w = self.sb("msg_w", [P, 2, 2 * D], ctx=ctx)
            bias = self.sb("msg_bias", [NT, D], ctx=ctx)
            out = self.sb("msg_out", [NT, NB, 2 * D], ctx=ctx)
            zero = self.sb("msg_zero", [P, D], ctx=ctx)
            ps_source = [self.ps(f"msg_table_ps_s{k}", [NT, D], ctx) for k in range(2)]
            ps_window = [self.ps(f"msg_table_ps_w{k}", [NT, D], ctx) for k in range(2)]
            with nc.Block() as block:
                @block.sync
                def _(sp):
                    for half in range(2):
                        sp.dma_start(w[:, :, half * D:(half + 1) * D],
                                     a["L0_gnn_W_msg"][half * D:(half + 1) * D, :].rearrange("(k p) n -> p k n", p=P)
                                     ).then_inc(loads, 16)
                    sp.dma_start(bias[:], self.row(a["L0_gnn_b_msg"])).then_inc(loads, 16)
                    sp.wait_ge(clear, 1)
                    sp.dma_start(self.window_table[N:WN, :], zero[:]).then_inc(stores, 16)
                    for b in range(NB):
                        sp.wait_ge(copied, b + 1)
                        sp.dma_start(self.source_table[b * NT:(b + 1) * NT, :], out[:, b, 0:D]).then_inc(stores, 16)
                        sp.wait_ge(biased, b + 1)
                        sp.dma_start(self.window_table[b * NT:(b + 1) * NT, :], out[:, b, D:2 * D]).then_inc(stores, 16)
                    sp.wait_ge(stores, 16 * (2 * NB + 1))

                @block.gpsimd
                def _(pool):
                    nc.gpsimd.memset(zero[:], 0.0).then_inc(clear, 1)
                    nc.gpsimd.memset(self.aggT[:], 0.0)

                @block.tensor
                def _(pe):
                    pe.wait_ge(loads, 48)
                    for b in range(NB):
                        if b >= 2:
                            pe.wait_ge(copied, b - 1)
                            pe.wait_ge(biased, b - 1)
                        for half, ps in enumerate((ps_source, ps_window)):
                            for k in range(2):
                                last = nc.tensor.matmul(ps[b % 2][:], self.hT[:, k, b * NT:(b + 1) * NT],
                                                        w[:, k, half * D:(half + 1) * D], start=k == 0, stop=k == 1)
                        last.then_inc(made, 1)

                @block.scalar
                def _(act):
                    for b in range(NB):
                        act.wait_ge(made, b + 1)
                        nc.scalar.copy(out[:, b, 0:D], ps_source[b % 2][:]).then_inc(copied, 1)

                @block.vector
                def _(dve):
                    dve.wait_ge(loads, 48)
                    for b in range(NB):
                        dve.wait_ge(made, b + 1)
                        nc.vector.tensor_tensor(out[:, b, D:2 * D], ps_window[b % 2][:], bias[:],
                                                ALU.add).then_inc(biased, 1)

    def message_update(self):
        nc, a = self.nc, self.a
        loads, made, added, relued, chain, root, scaled = (self.sem(f"upd_{k}") for k in (
            "loads", "made", "added", "relued", "chain", "root", "scaled"))
        u = self.h
        with ExitStack() as ctx:
            w = self.sb("upd_w", [P, 4, D], ctx=ctx)
            bias, gamma, beta = (self.sb(f"upd_{k}", [NT, D], ctx=ctx) for k in ("bias", "gamma", "beta"))
            st = self.sb("upd_st", [NT, NB, 6], ctx=ctx)
            mv = self.sb("upd_mv", [NT, NB, 2], ctx=ctx)
            sd, rs, nm = (self.sb(f"upd_{k}", [NT, NB], ctx=ctx) for k in ("sd", "rs", "nm"))
            ps = [self.ps(f"upd_ps{k}", [NT, D], ctx) for k in range(2)]
            with nc.Block() as block:
                @block.sync
                def _(sp):
                    sp.dma_start(w[:], a["L0_gnn_W_upd"].rearrange("(k p) n -> p k n", p=P)).then_inc(loads, 16)
                    for t, k in ((bias, "b_upd"), (gamma, "gamma"), (beta, "beta")):
                        sp.dma_start(t[:], self.row(a[f"L0_gnn_{k}"])).then_inc(loads, 16)

                @block.tensor
                def _(pe):
                    pe.wait_ge(loads, 64)
                    for b in range(NB):
                        if b >= 2:
                            pe.wait_ge(added, b - 1)
                        for k in range(4):
                            src = self.hT if k < 2 else self.aggT
                            last = nc.tensor.matmul(ps[b % 2][:], src[:, k % 2, b * NT:(b + 1) * NT], w[:, k, :],
                                                    start=k == 0, stop=k == 3)
                        last.then_inc(made, 1)

                @block.scalar
                def _(act):
                    for b in range(NB):
                        act.wait_ge(added, b + 1)
                        nc.scalar.activation(u[:, b, :], u[:, b, :], ACT.Relu).then_inc(relued, 1)
                    act.wait_ge(chain, 2 * NB + 1)
                    nc.scalar.activation(sd[:], sd[:], ACT.Sqrt).then_inc(root, 1)
                    act.wait_ge(chain, 2 * NB + 3)
                    for b in range(NB):
                        nc.scalar.activation(u[:, b, :], u[:, b, :], ACT.Identity, scale=rs[:, b:b + 1],
                                             bias=nm[:, b:b + 1]).then_inc(scaled, 1)

                @block.vector
                def _(dve):
                    dve.wait_ge(loads, 64)
                    for b in range(NB + 1):
                        if b < NB:
                            dve.wait_ge(made, b + 1)
                            nc.vector.tensor_tensor(u[:, b, :], ps[b % 2][:], bias[:], ALU.add).then_inc(added, 1)
                        if b > 0:
                            dve.wait_ge(relued, b)
                            nc.vector.bn_stats(st[:, b - 1, :], u[:, b - 1, :]).then_inc(chain, 1)
                    for b in range(NB):
                        dve.wait_ge(chain, NB + b)
                        nc.vector.bn_aggr(mv[:, b, :], st[:, b, :]).then_inc(chain, 1)
                    dve.wait_ge(chain, 2 * NB)
                    nc.vector.tensor_scalar(sd[:], mv[:, :, 1], EPS, None, ALU.add).then_inc(chain, 1)
                    dve.wait_ge(root, 1)
                    nc.vector.reciprocal(rs[:], sd[:]).then_inc(chain, 1)
                    dve.wait_ge(chain, 2 * NB + 2)
                    nc.vector.scalar_tensor_tensor(out=nm[:], in0=mv[:, :, 0], scalar=-1.0, in1=rs[:],
                                                   op0=ALU.mult, op1=ALU.mult).then_inc(chain, 1)
                    nc.vector.tensor_tensor(self.x[:], self.x[:], beta[:].unsqueeze(1).to_broadcast([NT, NB, D]),
                                            ALU.add).then_inc(chain, 1)
                    for b in range(NB):
                        dve.wait_ge(scaled, b + 1)
                        nc.vector.tensor_tensor(u[:, b, :], u[:, b, :], gamma[:], ALU.mult).then_inc(chain, 1)
                        if b > 0:
                            dve.wait_ge(chain, 2 * NB + 4 + b)
                            nc.vector.tensor_tensor(self.x[:, b - 1, :], self.x[:, b - 1, :], u[:, b - 1, :], ALU.add)
                    dve.wait_ge(chain, 3 * NB + 4)
                    nc.vector.tensor_tensor(self.x[:, NB - 1, :], self.x[:, NB - 1, :], u[:, NB - 1, :], ALU.add)

    def mlp(self, maxT, sums):
        nc, a = self.nc, self.a
        loads, chain, spread, graph, b1_made, hidden, relued, outer, added, based = (self.sem(f"mlp_{k}") for k in (
            "loads", "chain", "spread", "graph", "b1_made", "hidden", "relued", "outer", "added", "based"))
        HB = HID // P
        with ExitStack() as ctx:
            w1 = self.sb("mlp_w1", [P, 6, HID], ctx=ctx)
            w2 = self.sb("mlp_w2", [P, HB, D], ctx=ctx)
            b1 = self.sb("mlp_b1", [P, HB], ctx=ctx)
            b2 = self.sb("mlp_b2", [NT, D], ctx=ctx)
            u0 = self.sb("mlp_u0", [U, 1], ctx=ctx)
            hid = self.sb("mlp_hid", [P, HB, CH], ctx=ctx)
            mean = self.sb("mlp_mean", [AF, N], ctx=ctx)
            pick = self.sb("mlp_pick", [AF + 1, AF], ctx=ctx)
            ps_g = self.ps("mlp_ps_g", [P, HB], ctx)
            ps_h = [self.ps(f"mlp_ps_h{k}", [P, 512], ctx) for k in range(3)]
            ps_o = [self.ps(f"mlp_ps_o{k}", [NT, D], ctx) for k in range(2)]
            parts = [(0, P), (P, P), (D, AF), (D + AF, AF), (D + 2 * AF, AF), (D + 3 * AF, U)]
            with nc.Block() as block:
                @block.sync
                def _(sp):
                    for k, (r, n) in enumerate(parts):
                        sp.dma_start(w1[0:n, k, :], a["L1_gnn_W1"][r:r + n, :]).then_inc(loads, 16)
                    sp.dma_start(w2[:], a["L1_gnn_W2"].rearrange("(k p) n -> p k n", p=P)).then_inc(loads, 16)
                    sp.dma_start(b1[:], a["L1_gnn_b1"].rearrange("(k p) -> p k", p=P),
                                 allow_slow_non_contiguous=True).then_inc(loads, 16)
                    sp.dma_start(b2[:], self.row(a["L1_gnn_b2"])).then_inc(loads, 16)
                    sp.dma_start(u0[:], a["L1_gnn_u"][0:1, :].rearrange("o f -> f o"),
                                 allow_slow_non_contiguous=True).then_inc(loads, 16)

                @block.gpsimd
                def _(pool):
                    nc.gpsimd.tensor_tensor(self.x[:], self.x[:], self.h[:], ALU.add).then_inc(based, 1)
                    pool.wait_ge(loads, 160)
                    pool.wait_ge(based, 1)
                    nc.gpsimd.tensor_tensor(self.x[:], self.x[:], b2[:].unsqueeze(1).to_broadcast([NT, NB, D]),
                                            ALU.add).then_inc(based, 1)

                @block.vector
                def _(dve):
                    nc.vector.tensor_scalar(pick[:], self.ones[0:AF + 1, 0:AF], self.partition[0:AF + 1, 0:1],
                                            float(AF), ALU.mult, ALU.is_equal).then_inc(chain, 1)
                    for c, (c0, cn) in enumerate(CHUNKS):
                        dve.wait_ge(spread, c + 1)
                        cnt = mean[:, c0:c0 + cn]
                        nc.vector.tensor_scalar(cnt, ps_h[c % 3][0:AF, 0:cn], 1.0, None, ALU.max).then_inc(chain, 1)
                        dve.wait_ge(chain, 3 * c + 2)
                        nc.vector.reciprocal(cnt, cnt).then_inc(chain, 1)
                        dve.wait_ge(chain, 3 * c + 3)
                        nc.vector.tensor_tensor(cnt, cnt, sums[0:AF, c0:c0 + cn], ALU.mult).then_inc(chain, 1)
                    dve.wait_ge(graph, 1)
                    nc.vector.tensor_tensor(b1[:], b1[:], ps_g[:], ALU.add).then_inc(b1_made, 1)
                    dve.wait_ge(based, 2)
                    for b in range(NB):
                        dve.wait_ge(outer, b + 1)
                        nc.vector.tensor_tensor(self.x[:, b, :], self.x[:, b, :], ps_o[b % 2][:], ALU.add
                                                ).then_inc(added, 1)

                @block.scalar
                def _(act):
                    act.wait_ge(b1_made, 1)
                    n = 0
                    for c, (c0, cn) in enumerate(CHUNKS):
                        for k in range(HB):
                            act.wait_ge(hidden, n + 1)
                            if c > 0 and k == 0:
                                act.wait_ge(outer, CH // NT * c)
                            nc.scalar.activation(hid[:, k, 0:cn], ps_h[n % 3][:, 0:cn], ACT.Relu,
                                                 bias=b1[:, k:k + 1]).then_inc(relued, 1)
                            n += 1

                @block.tensor
                def _(pe):
                    pe.wait_ge(loads, 160)
                    for k in range(HB):
                        last = nc.tensor.matmul(ps_g[:, k:k + 1], w1[0:U, 5, k * P:(k + 1) * P], u0[:],
                                                start=True, stop=True)
                    last.then_inc(graph, 1)
                    pe.wait_ge(chain, 1)
                    for c, (c0, cn) in enumerate(CHUNKS):
                        if c >= 3:
                            pe.wait_ge(chain, 3 * (c - 3) + 2)
                        nc.tensor.matmul(ps_h[c % 3][0:AF, 0:cn], pick[:], sums[:, c0:c0 + cn],
                                         start=True, stop=True).then_inc(spread, 1)
                    pe.wait_ge(chain, 3 * len(CHUNKS) + 1)
                    n = b = 0
                    for c0, cn in CHUNKS:
                        moving = [self.hT[:, 0, c0:c0 + cn], self.hT[:, 1, c0:c0 + cn], sums[0:AF, c0:c0 + cn],
                                  maxT[:, 0, c0:c0 + cn], mean[:, c0:c0 + cn]]
                        for k in range(HB):
                            if n >= 3:
                                pe.wait_ge(relued, n - 2)
                            for j, m in enumerate(moving):
                                last = nc.tensor.matmul(ps_h[n % 3][:, 0:cn], w1[0:parts[j][1], j, k * P:(k + 1) * P],
                                                        m, start=j == 0, stop=j == len(moving) - 1)
                            last.then_inc(hidden, 1)
                            n += 1
                        pe.wait_ge(relued, n)
                        for t in range(cn // NT):
                            if b >= 2:
                                pe.wait_ge(added, b - 1)
                            for k in range(HB):
                                last = nc.tensor.matmul(ps_o[b % 2][:], hid[:, k, t * NT:(t + 1) * NT], w2[:, k, :],
                                                        start=k == 0, stop=k == HB - 1)
                            last.then_inc(outer, 1)
                            b += 1

    def attention_tables(self):
        nc, a = self.nc, self.a
        AW = D + H
        folds_made = 0
        self.attention_table = nc.dram_tensor("att_table", [N, AW], F32).ap()
        self.head_table = nc.dram_tensor("att_heads", [N, H], F32).ap()
        loads, clears, marks, chain, turned, folded, rhs, made, kept, dmade, dkept, stores = (
            self.sem(f"att_{k}") for k in ("loads", "clears", "marks", "chain", "turned", "folded", "rhs", "made",
                                           "kept", "dmade", "dkept", "stores"))
        with ExitStack() as ctx:
            wc = self.sb("att_wc", [P, 2, D], ctx=ctx)
            wp = self.sb("att_wp", [U, P], ctx=ctx)
            av = self.sb("att_av", [P, 2, 2], ctx=ctx)
            ap = self.sb("att_ap", [U, 2], ctx=ctx)
            comb = self.sb("att_comb", [P, H, 2], ctx=ctx)
            own = self.sb("att_own", [P, 2, H], ctx=ctx)
            own_b = self.sb("att_own_b", [P, 2, H], ctx=ctx)
            own_p = self.sb("att_own_p", [U, H], ctx=ctx)
            own_pb = self.sb("att_own_pb", [U, H], ctx=ctx)
            fold = self.sb("att_fold", [P, 2, 2, H], ctx=ctx)
            fold_p = self.sb("att_fold_p", [U, 2, H], ctx=ctx)
            w = self.sb("att_w", [P, 2, D + 2 * H], ctx=ctx)
            out = self.sb("att_out", [NT, NB, AW], ctx=ctx)
            ps_t = self.ps("att_ps_t", [P, 2, 2, P], ctx)
            ps_v = self.ps("att_ps_v", [P, 2, 2 * H], ctx)
            ps = [self.ps(f"att_ps{k}", [NT, D + 2 * H], ctx) for k in range(2)]
            ps_d = [self.ps(f"att_ps_d{k}", [H, 512], ctx) for k in range(2)]
            with nc.Block() as block:
                @block.sync
                def _(sp):
                    sp.wait_ge(clears, 2)
                    sp.dma_start(wc[:, :, 0:CD], a["L2_gnn_Wc"].rearrange("(k p) n -> p k n", p=P)).then_inc(loads, 16)
                    sp.dma_start(wp[:, P - POS:P], a["L2_gnn_Wp"]).then_inc(loads, 16)
                    for k, name in enumerate(("src", "dst")):
                        sp.dma_start(av[:, :, k:k + 1], a[f"L2_gnn_attn_{name}"].rearrange(
                            "o (k g) d -> (g d) k o", k=2), allow_slow_non_contiguous=True).then_inc(loads, 16)
                        sp.dma_start(ap[:, k:k + 1], a[f"L2_gnn_pos_attn_{name}"].rearrange("o h d -> (h d) o"),
                                     allow_slow_non_contiguous=True).then_inc(loads, 16)
                    sp.dma_start(comb[:], a["L2_gnn_att_comb"].partition_broadcast(P)).then_inc(loads, 16)
                    for b in range(NB):
                        sp.wait_ge(kept, b + 1)
                        sp.dma_start(self.attention_table[b * NT:(b + 1) * NT, :], out[:, b, :]).then_inc(stores, 16)
                        sp.dma_start(self.head_table[b * NT:(b + 1) * NT, :], out[:, b, D:AW]).then_inc(stores, 16)
                    sp.wait_ge(stores, 32 * NB)

                @block.gpsimd
                def _(pool):
                    nc.gpsimd.memset(wc[:], 0.0).then_inc(clears, 1)
                    nc.gpsimd.memset(wp[:], 0.0).then_inc(clears, 1)
                    nc.gpsimd.iota(own[:], pattern=[[P, 2], [-HD, H]], base=0, channel_multiplier=1,
                                   allow_small_or_imprecise_dtypes=True).then_inc(marks, 1)
                    nc.gpsimd.iota(own_p[:], pattern=[[-POS, H]], base=0, channel_multiplier=1,
                                   allow_small_or_imprecise_dtypes=True).then_inc(marks, 1)
                    nc.gpsimd.memset(self.aggT[:], 0.0)
                    nc.gpsimd.memset(self.denomT[:], 0.0)

                @block.vector
                def _(dve):
                    nonlocal folds_made
                    steps = 0

                    def link(ins):
                        nonlocal steps
                        steps += 1
                        ins.then_inc(chain, 1)
                        dve.wait_ge(chain, steps)
                    dve.wait_ge(marks, 2)
                    for dist, less, size in ((own, own_b, HD), (own_p, own_pb, POS)):
                        link(nc.vector.tensor_scalar(less[:], dist[:], float(size), None, ALU.is_lt))
                        link(nc.vector.tensor_scalar(dist[:], dist[:], 0.0, None, ALU.is_ge))
                        link(nc.vector.tensor_tensor(dist[:], dist[:], less[:], ALU.mult))
                    dve.wait_ge(loads, 16 * 7)
                    for blk in range(2):
                        link(nc.vector.tensor_tensor(own_b[:, blk, :], own[:, blk, :], comb[:, :, 0], ALU.mult))
                        for k in range(2):
                            link(nc.vector.tensor_scalar(fold[:, blk, k, :], own_b[:, blk, :], av[:, blk, k:k + 1],
                                                         None, ALU.mult))
                    link(nc.vector.tensor_tensor(own_pb[:], own_p[:], comb[0:U, :, 1], ALU.mult))
                    for k in range(2):
                        link(nc.vector.tensor_scalar(fold_p[:, k, :], own_pb[:], ap[:, k:k + 1], None, ALU.mult))
                    folds_made = steps
                    dve.wait_ge(turned, 1)
                    nc.vector.tensor_copy(w[:, :, 0:D], ps_t[:].rearrange("p i f n -> p i (f n)")).then_inc(rhs, 1)
                    dve.wait_ge(folded, 1)
                    nc.vector.tensor_copy(w[:, :, D:D + 2 * H], ps_v[:]).then_inc(rhs, 1)
                    for c, (c0, cn) in enumerate(CHUNKS):
                        dve.wait_ge(dmade, c + 1)
                        nc.vector.tensor_copy(self.dstT[:, c0:c0 + cn], ps_d[c % 2][:, 0:cn]).then_inc(dkept, 1)

                @block.tensor
                def _(pe):
                    pe.wait_ge(loads, 16 * 7)
                    for i in range(2):
                        for f in range(2):
                            last = nc.tensor.transpose(ps_t[:, i, f, :], wc[:, f, i * P:(i + 1) * P], self.ident[:])
                    last.then_inc(turned, 1)
                    pe.wait_ge(chain, folds_made)
                    for i in range(2):
                        for f in range(2):
                            last = nc.tensor.matmul(ps_v[:, i, :], wc[:, f, i * P:(i + 1) * P],
                                                    fold[:, f, :, :].rearrange("p k h -> p (k h)"),
                                                    start=f == 0, stop=i == 0 and f == 1)
                    nc.tensor.matmul(ps_v[:, 1, :], wp[:], fold_p[:].rearrange("p k h -> p (k h)"),
                                     start=False, stop=True).then_inc(folded, 1)
                    pe.wait_ge(rhs, 2)
                    for b in range(NB):
                        if b >= 2:
                            pe.wait_ge(kept, b - 1)
                        for k in range(2):
                            last = nc.tensor.matmul(ps[b % 2][:], self.hT[:, k, b * NT:(b + 1) * NT], w[:, k, :],
                                                    start=k == 0, stop=k == 1)
                        last.then_inc(made, 1)
                    for c, (c0, cn) in enumerate(CHUNKS):
                        if c >= 2:
                            pe.wait_ge(dkept, c - 1)
                        for k in range(2):
                            last = nc.tensor.matmul(ps_d[c % 2][:, 0:cn], w[:, k, D + H:D + 2 * H],
                                                    self.hT[:, k, c0:c0 + cn], start=k == 0, stop=k == 1)
                        last.then_inc(dmade, 1)

                @block.scalar
                def _(act):
                    for b in range(NB):
                        act.wait_ge(made, b + 1)
                        nc.scalar.copy(out[:, b, :], ps[b % 2][:, 0:AW]).then_inc(kept, 1)

    def logit_table(self, largestT):
        nc = self.nc
        self.logit_rows = nc.dram_tensor("logit_window_table", [WN, 2 * H], F32).ap()
        chain, made, kept, clear, stores = (self.sem(f"log_{k}") for k in ("chain", "made", "kept", "clear", "stores"))
        with ExitStack() as ctx:
            out = self.sb("log_out", [NT, NB, 2 * H], ctx=ctx)
            zero = self.sb("log_zero", [P, 2 * H], ctx=ctx)
            ps = self.ps("log_ps", [NT, NB, 2 * H], ctx)
            with nc.Block() as block:
                @block.gpsimd
                def _(pool):
                    nc.gpsimd.memset(zero[:], 0.0).then_inc(clear, 1)

                @block.vector
                def _(dve):
                    m, d = largestT[:, 0, 0:N], self.dstT[:, 0:N]
                    nc.vector.tensor_tensor(m, m, d, ALU.add).then_inc(chain, 1)
                    dve.wait_ge(chain, 1)
                    nc.vector.scalar_tensor_tensor(out=m, in0=m, scalar=0.2, in1=m, op0=ALU.mult,
                                                   op1=ALU.max).then_inc(chain, 1)
                    dve.wait_ge(made, 1)
                    nc.vector.tensor_copy(out[:], ps[:]).then_inc(kept, 1)

                @block.tensor
                def _(pe):
                    pe.wait_ge(chain, 2)
                    for b in range(NB):
                        nodes = slice(b * NT, (b + 1) * NT)
                        nc.tensor.transpose(ps[:, b, 0:H], self.dstT[:, nodes], self.ident[0:H, 0:H])
                        last = nc.tensor.transpose(ps[:, b, H:2 * H], largestT[:, 0, nodes], self.ident[0:H, 0:H])
                    last.then_inc(made, 1)

                @block.sync
                def _(sp):
                    sp.wait_ge(clear, 1)
                    sp.dma_start(self.logit_rows[N:WN, :], zero[:]).then_inc(stores, 16)
                    sp.wait_ge(kept, 1)
                    sp.dma_start(self.logit_rows[0:N, :].rearrange("(b p) k -> p b k", p=NT), out[:]).then_inc(stores, 16)
                    sp.wait_ge(stores, 32)

    def attention_update(self):
        nc = self.nc
        marks, chain, spread, inverted, divided, turned, added, based = (self.sem(f"fin_{k}") for k in (
            "marks", "chain", "spread", "inverted", "divided", "turned", "added", "based"))
        with ExitStack() as ctx:
            own = self.sb("fin_own", [H, D], ctx=ctx)
            less = self.sb("fin_less", [H, D], ctx=ctx)
            inv = self.sb("fin_inv", [P, 2, 512], ctx=ctx)
            ps_d = [self.ps(f"fin_ps_d{k}", [P, 512], ctx) for k in range(2)]
            ps = [self.ps(f"fin_ps{k}", [NT, D], ctx) for k in range(2)]
            with nc.Block() as block:
                @block.gpsimd
                def _(pool):
                    nc.gpsimd.iota(own[:], pattern=[[1, D]], base=0, channel_multiplier=-HD,
                                   allow_small_or_imprecise_dtypes=True).then_inc(marks, 1)
                    nc.gpsimd.tensor_tensor(self.x[:], self.x[:], self.h[:], ALU.add).then_inc(based, 1)

                @block.vector
                def _(dve):
                    den = self.denomT[:, 0:N]
                    nc.vector.tensor_scalar(den, den, 1e-30, None, ALU.max).then_inc(chain, 1)
                    dve.wait_ge(marks, 1)
                    nc.vector.tensor_scalar(less[:], own[:], float(HD), None, ALU.is_lt).then_inc(chain, 1)
                    dve.wait_ge(chain, 2)
                    nc.vector.tensor_scalar(own[:], own[:], 0.0, None, ALU.is_ge).then_inc(chain, 1)
                    dve.wait_ge(chain, 3)
                    nc.vector.tensor_tensor(own[:], own[:], less[:], ALU.mult).then_inc(chain, 1)
                    n = 0
                    for c0, cn in CHUNKS:
                        for k in range(2):
                            dve.wait_ge(spread, n + 1)
                            nc.vector.reciprocal(inv[:, n % 2, 0:cn], ps_d[n % 2][:, 0:cn]).then_inc(inverted, 1)
                            dve.wait_ge(inverted, n + 1)
                            at = self.aggT[:, k, c0:c0 + cn]
                            nc.vector.tensor_tensor(at, at, inv[:, n % 2, 0:cn], ALU.mult).then_inc(divided, 1)
                            n += 1
                    dve.wait_ge(based, 1)
                    for b in range(NB):
                        dve.wait_ge(turned, b + 1)
                        nc.vector.tensor_tensor(self.x[:, b, :], self.x[:, b, :], ps[b % 2][:], ALU.add
                                                ).then_inc(added, 1)

                @block.tensor
                def _(pe):
                    pe.wait_ge(chain, 4)
                    n = 0
                    for c0, cn in CHUNKS:
                        for k in range(2):
                            if n >= 2:
                                pe.wait_ge(inverted, n - 1)
                            nc.tensor.matmul(ps_d[n % 2][:, 0:cn], own[:, k * P:(k + 1) * P],
                                             self.denomT[:, c0:c0 + cn], start=True, stop=True).then_inc(spread, 1)
                            n += 1
                    pe.wait_ge(divided, n)
                    for b in range(NB):
                        if b >= 2:
                            pe.wait_ge(added, b - 1)
                        for k in range(2):
                            last = nc.tensor.transpose(ps[b % 2][:, k * P:(k + 1) * P],
                                                       self.aggT[:, k, b * NT:(b + 1) * NT], self.ident[:])
                        last.then_inc(turned, 1)

    def pool_table(self):
        nc, a = self.nc, self.a
        loads, turned, kept, made, added, relued, stores = (self.sem(f"pool_{k}") for k in (
            "loads", "turned", "kept", "made", "added", "relued", "stores"))
        names = ("pool", "self", "neigh")
        self.wT = {k: self.sb(f"w_{k}T", [P, 2, D]) for k in names}
        with ExitStack() as ctx:
            raw = self.sb("pool_raw", [P, 3, 2, D], ctx=ctx)
            bias = self.sb("pool_bias", [NT, D], ctx=ctx)
            out = self.sb("pool_out", [NT, NB, D], ctx=ctx)
            ps_t = [self.ps(f"pool_ps_t{k}", [P, 2, 2, P], ctx) for k in range(3)]
            ps = [self.ps(f"pool_ps{k}", [NT, D], ctx) for k in range(2)]
            with nc.Block() as block:
                @block.sync
                def _(sp):
                    for k, name in enumerate(names):
                        sp.dma_start(raw[:, k, :, :], a[f"L3_gnn_W_{name}"].rearrange("(k p) n -> p k n", p=P)
                                     ).then_inc(loads, 16)
                    sp.dma_start(bias[:], self.row(a["L3_gnn_b_pool"])).then_inc(loads, 16)
                    for b in range(NB):
                        sp.wait_ge(relued, b + 1)
                        sp.dma_start(self.source_table[b * NT:(b + 1) * NT, :], out[:, b, :]).then_inc(stores, 16)
                    sp.wait_ge(stores, 16 * NB)

                @block.tensor
                def _(pe):
                    pe.wait_ge(loads, 64)
                    for k in range(3):
                        for i in range(2):
                            for o in range(2):
                                last = nc.tensor.transpose(ps_t[k][:, i, o, :], raw[:, k, o, i * P:(i + 1) * P],
                                                           self.ident[:])
                        last.then_inc(turned, 1)
                    pe.wait_ge(kept, 1)
                    for b in range(NB):
                        if b >= 2:
                            pe.wait_ge(added, b - 1)
                        for k in range(2):
                            last = nc.tensor.matmul(ps[b % 2][:], self.hT[:, k, b * NT:(b + 1) * NT],
                                                    self.wT["pool"][:, k, :], start=k == 0, stop=k == 1)
                        last.then_inc(made, 1)

                @block.vector
                def _(dve):
                    for k, name in enumerate(names):
                        dve.wait_ge(turned, k + 1)
                        nc.vector.tensor_copy(self.wT[name][:], ps_t[k][:].rearrange("p i o n -> p i (o n)")
                                              ).then_inc(kept, 1)
                    dve.wait_ge(loads, 64)
                    for b in range(NB):
                        dve.wait_ge(made, b + 1)
                        nc.vector.tensor_tensor(out[:, b, :], ps[b % 2][:], bias[:], ALU.add).then_inc(added, 1)

                @block.scalar
                def _(act):
                    for b in range(NB):
                        act.wait_ge(added, b + 1)
                        nc.scalar.activation(out[:, b, :], out[:, b, :], ACT.Relu).then_inc(relued, 1)

    def pool_update(self):
        nc, a = self.nc, self.a
        loads, made, biased, added, stores = (self.sem(f"out_{k}") for k in (
            "loads", "made", "biased", "added", "stores"))
        with ExitStack() as ctx:
            b_self, b_neigh = (self.sb(f"out_{k}", [NT, D], ctx=ctx) for k in ("b_self", "b_neigh"))
            ps = [self.ps(f"out_ps{k}", [NT, D], ctx) for k in range(2)]
            with nc.Block() as block:
                @block.sync
                def _(sp):
                    sp.dma_start(b_self[:], self.row(a["L3_gnn_b_self"])).then_inc(loads, 16)
                    sp.dma_start(b_neigh[:], self.row(a["L3_gnn_b_neigh"])).then_inc(loads, 16)
                    for b in range(NB):
                        sp.wait_ge(added, b + 1)
                        sp.dma_start(self.out[b * NT:(b + 1) * NT, :], self.x[:, b, :]).then_inc(stores, 16)
                    sp.wait_ge(stores, 16 * NB)

                @block.gpsimd
                def _(pool):
                    pool.wait_ge(loads, 32)
                    for k, bias in enumerate((b_self, b_neigh)):
                        if k:
                            pool.wait_ge(biased, k)
                        nc.gpsimd.tensor_tensor(self.x[:], self.x[:], bias[:].unsqueeze(1).to_broadcast([NT, NB, D]),
                                                ALU.add).then_inc(biased, 1)

                @block.tensor
                def _(pe):
                    for b in range(NB):
                        if b >= 2:
                            pe.wait_ge(added, b - 1)
                        for k in range(4):
                            src, w = (self.hT, self.wT["self"]) if k < 2 else (self.aggT, self.wT["neigh"])
                            last = nc.tensor.matmul(ps[b % 2][:], src[:, k % 2, b * NT:(b + 1) * NT], w[:, k % 2, :],
                                                    start=k == 0, stop=k == 3)
                        last.then_inc(made, 1)

                @block.vector
                def _(dve):
                    dve.wait_ge(biased, 2)
                    for b in range(NB):
                        dve.wait_ge(made, b + 1)
                        nc.vector.tensor_tensor(self.x[:, b, :], self.x[:, b, :], ps[b % 2][:], ALU.add
                                                ).then_inc(added, 1)


def build(nc, a, out):
    with ExitStack() as ctx:
        k = Kernel(nc, ctx, a, out)
        k.prepare()
        k.normalize("norm0")
        k.message_tables()
        k.sum_pass("msg", k.source_table, D, k.window_table, D, attention=False)
        k.message_update()
        k.normalize("norm1")
        with ExitStack() as layer:
            maxT = k.sb("maxT", [AF, 1, WN], ctx=layer)
            sums = k.sb("sums", [AF + 1, WN], ctx=layer)
            k.clear("attr_clear", sums)
            k.max_pass("attr", [AF], maxT, sums=sums)
            k.mlp(maxT, sums)
        k.normalize("norm2")
        with ExitStack() as layer:
            k.dstT = k.sb("dstT", [H, N], ctx=layer)
            k.denomT = k.sb("denomT", [H, WN], ctx=layer)
            largestT = k.sb("largestT", [H, 1, WN], ctx=layer)
            k.attention_tables()
            k.max_pass("logit", [H], largestT, table=k.head_table)
            k.logit_table(largestT)
            k.sum_pass("att", k.attention_table, D + H, k.logit_rows, 2 * H, attention=True)
            k.attention_update()
        k.normalize("norm3")
        k.pool_table()
        k.max_pass("pool_max", [P, P], k.aggT, table=k.source_table, weighted=True)
        k.pool_update()


_INS = ["x", "src", "dst", "edge_attr_96", "edge_weight1",
        "L0_gnn_W_msg", "L0_gnn_b_msg", "L0_gnn_W_upd", "L0_gnn_b_upd", "L0_gnn_gamma", "L0_gnn_beta",
        "L1_gnn_u", "L1_gnn_W1", "L1_gnn_b1", "L1_gnn_W2", "L1_gnn_b2",
        "L2_gnn_Wc", "L2_gnn_Wp", "L2_gnn_attn_src", "L2_gnn_attn_dst", "L2_gnn_pos_attn_src",
        "L2_gnn_pos_attn_dst", "L2_gnn_att_comb",
        "L3_gnn_W_pool", "L3_gnn_b_pool", "L3_gnn_W_self", "L3_gnn_b_self", "L3_gnn_W_neigh", "L3_gnn_b_neigh"]


def kernel(**inputs):
    import numpy as _np
    import concourse.bacc as _bacc
    from concourse import mybir as _mybir
    from concourse.bass_utils import run_bass_kernel_spmd as _run

    nc = _bacc.Bacc("TRN2", target_bir_lowering=False, num_devices=1)
    arrays, aps = {}, {}
    for name in _INS:
        arr = _np.ascontiguousarray(inputs[name])
        arrays[f"in_{name}"] = arr
        aps[name] = nc.dram_tensor(f"in_{name}", arr.shape, _mybir.dt.from_np(arr.dtype), kind="ExternalInput").ap()
    out = nc.dram_tensor("out_x", (N, D), F32, kind="ExternalOutput").ap()
    build(nc, aps, out)
    r = _run(nc, [arrays], core_ids=[0])
    return r.results[0]["out_x"]
```

```python
from contextlib import ExitStack

import concourse.bass as bass
from concourse import mybir

F32 = mybir.dt.float32
BF16 = mybir.dt.bfloat16
I32 = mybir.dt.int32
ALU = mybir.AluOpType
ACT = mybir.ActivationFunctionType

P_BITS = 7
P = 1 << P_BITS
N = 3125
E = 53125
D = 256
NT = 125
NB = N // NT
LB = -(-N // P)
WN = N + P
TG = 4
HALF = TG // 2
GE = TG * P
SLOTS = 8
BUFS = 4
PAIR = 2
T = -(-E // (GE * SLOTS)) * TG * SLOTS
NG = T // TG
NI = NG // SLOTS
RQ = 4
RT = T // RQ
FULL = E // P
REST = E - FULL * P
AF = 96
U = 64
HID = 1024
SPLIT = 3
H_BITS = 2
H = 1 << H_BITS
HD = 64
POS = 16
CD = D - POS
CREDIT = SLOTS
FLT = 3.3895313892515355e38
EPS = 1e-5
BANK = 512
PART = 5
CH = 500
CHUNKS = [(c, min(CH, N - c)) for c in range(0, N, CH)]


def hold(eng, sem, value, least=1):
    value = value if isinstance(value, int) else eng.to_reg(value)
    eng.wait_ge(sem, least)
    eng.wait_ge(sem, value)


def pipelined(eng, stages):
    for g in range(-max(ahead for _, ahead in stages), 0):
        for stage, ahead in stages:
            if g + ahead >= 0:
                stage(0, g + ahead)
    with eng.Fori(0, NI - 1) as i:
        for s in range(SLOTS):
            for stage, ahead in stages:
                k = s + ahead
                stage(i + 1 if k >= SLOTS else i, k % SLOTS)
    for s in range(SLOTS):
        for stage, ahead in stages:
            if s + ahead < SLOTS:
                stage(NI - 1, s + ahead)


class Kernel:

    def __init__(self, nc, ctx, a, out):
        self.nc, self.ctx, self.a, self.out = nc, ctx, a, out
        self.before = {}
        self.event, self.reached = {}, {}
        self.count = 0
        sem = self.sem
        self.index_in = [sem(f"index_in{s}") for s in range(SLOTS // PAIR)]
        self.rows_in = [sem(f"rows_in{s}") for s in range(SLOTS)]
        self.line_in = [sem(f"line_in{s}") for s in range(BUFS // PAIR)]
        self.window_in = [sem(f"window_in{s}") for s in range(BUFS)]

        self.norm_events = [sem(f"norm_{k}") for k in ("stats", "root", "rstd", "h", "turned", "kept")]
        self.stats_made = sem("stats_made")
        self.normalized = 0

    def sem(self, name):
        return self.ctx.enter_context(self.nc.semaphore(name))

    def sb(self, name, shape, dt=F32, ctx=None):
        return (ctx or self.ctx).enter_context(self.nc.sbuf_tensor(name, shape, dt))

    def ps(self, name, shape, ctx):
        size = 1
        for n in shape[1:]:
            size *= n
        banks = ctx.enter_context(self.nc.psum_tensor(name, [shape[0], -(-size // BANK) * BANK], F32))
        flat = banks[:, 0:size]
        if len(shape) == 3:
            return flat.rearrange("p (a b) -> p a b", a=shape[1])
        if len(shape) == 4:
            return flat.rearrange("p (a b c) -> p a b c", a=shape[1], b=shape[2])
        return flat

    def events(self, *names):
        for name in names:
            if name not in self.event:
                self.event[name] = self.sem(f"event_{name}")
                self.reached[self.event[name].name] = 0
        return [self.event[name] for name in names]

    def credit(self, event):
        more = self.count + CREDIT - self.reached[event.name]
        self.reached[event.name] = self.count + CREDIT + NG
        return more

    def split(self, dve, event, value, rest, parts):
        nc, n = self.nc, 0
        for k in range(SPLIT):
            nc.vector.tensor_copy(parts[k], value if k == 0 else rest).then_inc(event, 1)
            n += 1
            dve.wait_ge(event, n)
            if k < SPLIT - 1:
                nc.vector.tensor_tensor(rest, value if k == 0 else rest, parts[k], ALU.subtract).then_inc(event, 1)
                n += 1
                dve.wait_ge(event, n)

    def start_events(self, engine, events):
        for event in events:
            engine.sem_inc(event, self.credit(event))

    def ready(self, i, s):
        return i * SLOTS + (self.count + s + 1 + CREDIT)

    def freed(self, i, s, buffers):
        return i * SLOTS + (self.count + s + 1 + CREDIT - buffers)

    def landed(self, semaphores, i, s, transfers=1, groups=1):
        n, turn = len(semaphores), s // groups
        sem = semaphores[turn % n]
        per_trip = 16 * transfers * SLOTS // (groups * n)
        return sem, i * per_trip + (self.before.get(sem.name, 0) + 16 * transfers * (turn // n + 1))

    def pass_over(self, semaphores, transfers=1, groups=1):
        for sem in semaphores:
            self.before[sem.name] = self.before.get(sem.name, 0) + 16 * transfers * NG // (groups * len(semaphores))

    def bases(self, engine, i, s, held):
        if s % PAIR == 0:
            _, values = self.nc.values_load_multi_w_load_instructions(
                self.base[0:1, bass.ds(i * (SLOTS * TG) + s * TG, PAIR * TG)], engines=[engine], min_val=0,
                max_val=N - 1, skip_runtime_bounds_check_because="destinations are node numbers")
            held[:] = values
        return held[s % PAIR * TG:(s % PAIR + 1) * TG]

    def after_tile_before(self, engine, events, i, s, t):
        if t == 0:
            engine.wait_ge(events[TG - 1], self.freed(i, s, 1))
        else:
            engine.wait_ge(events[t - 1], self.ready(i, s))

    def prepare(self, ctx):
        nc, a, sb = self.nc, self.a, self.sb
        self.x = sb("x", [NT, NB, D])
        self.stats = sb("stats", [NT, NB, 6])
        self.hT = sb("hT", [P, 2, N])
        self.h = sb("h", [NT, NB, D])
        self.source = sb("source", [P, T], I32)
        self.place = sb("place", [P, T])
        self.place_end = sb("place_end", [P, T])
        self.weight = sb("weight", [P, T])
        self.base = sb("base", [1, T], I32)
        self.columns = sb("columns", [P, P])
        self.partition = sb("partition", [P, 1])
        self.ident = sb("ident", [P, P])
        self.ones = sb("ones", [P, P])
        self.aggT = sb("aggT", [P, 3, WN])
        self.denomT = self.aggT[0:H, 2, :]
        self.place_line = nc.dram_tensor("place_line", [T * P], BF16).ap()
        self.mask_line = nc.dram_tensor("mask_line", [T * P], BF16).ap()
        self.carry_line = nc.dram_tensor("carry_line", [T * P], BF16).ap()
        self.block_line = nc.dram_tensor("block_line", [T * P], BF16).ap()
        self.within_line = nc.dram_tensor("within_line", [T * P], BF16).ap()
        loads, constants, chain = self.sem("prep_loads"), self.sem("prep_constants"), self.sem("prep_chain")
        clears, pe, stores = self.sem("prep_clears"), self.sem("prep_transposed"), self.sem("prep_stores")
        x_in = self.sem("prep_x_in")
        def tmp(name, shape, dt=F32):
            return self.sb(name, shape, dt, ctx)
        raw = {k: tmp(k, [RT, RQ, P], I32) for k in ("src_rows", "dst_rows")}
        w_rows = tmp("w_rows", [RT, RQ, P])
        before, after = tmp("before", [RT, RQ], I32), tmp("after", [RT, RQ], I32)
        src_f, dst_f, other = tmp("src_f", [RT, RQ, P]), tmp("dst_f", [RT, RQ, P]), tmp("other", [RT, RQ, P])
        before_f, after_f = tmp("before_f", [RT, RQ]), tmp("after_f", [RT, RQ])
        rel, rel_end, flag = tmp("rel", [RT, RQ, P]), tmp("rel_end", [RT, RQ, P]), tmp("flag", [RT, RQ, P])
        mask, carry = tmp("mask", [RT, RQ, P], BF16), tmp("carry", [RT, RQ, P], BF16)
        rel16 = tmp("rel16", [RT, RQ, P], BF16)
        block_i, within_i = tmp("block_i", [RT, RQ, P], I32), tmp("within_i", [RT, RQ, P], I32)
        block16, within16 = tmp("block16", [RT, RQ, P], BF16), tmp("within16", [RT, RQ, P], BF16)
        psT = [self.ps(f"prep_ps{k}", [P, T], ctx) for k in range(4)]
        whole = (RQ - 1) * RT
        lines_made = 21
        transfers = []
        for tile, flat in ((raw["src_rows"], a["src"]), (raw["dst_rows"], a["dst"]),
                           (w_rows, a["edge_weight1"].rearrange("e o -> (e o)"))):
            transfers += [
                (tile[:, 0:RQ - 1, :], flat[0:whole * P].rearrange("(q r c) -> r q c", r=RT, c=P)),
                (tile[0:FULL - whole, RQ - 1, :], flat[whole * P:FULL * P].rearrange("(r c) -> r c", c=P)),
                (tile[FULL - whole:FULL - whole + 1, RQ - 1, 0:REST],
                 flat[FULL * P:E].rearrange("(r c) -> r c", r=1))]
        dst = a["dst"]
        ends = dst[P:FULL * P].rearrange("(j c) -> j c", c=P)[:, P - 1:P]
        firsts = dst[P:FULL * P].rearrange("(j c) -> j c", c=P)[:, 0:1]
        transfers += [(before[1:2, 0:1], dst[P - 1:P].rearrange("(r c) -> r c", r=1)),
                      (before[2:RT, 0:1], ends[0:RT - 2, :])]
        transfers += [(before[:, q:q + 1], ends[q * RT - 2:(q + 1) * RT - 2, :]) for q in range(1, RQ - 1)]
        transfers += [(before[0:FULL + 1 - whole, RQ - 1:RQ], ends[whole - 2:FULL - 1, :])]
        transfers += [(after[:, q:q + 1], firsts[q * RT:(q + 1) * RT, :]) for q in range(RQ - 1)]
        transfers += [(after[0:FULL - 1 - whole, RQ - 1:RQ], firsts[whole:FULL - 1, :]),
                      (after[FULL - 1 - whole:FULL - whole, RQ - 1:RQ],
                       dst[FULL * P:FULL * P + 1].rearrange("(r c) -> r c", r=1))]
        transfers += [(self.base[0:1, 0:FULL], dst[0:FULL * P].rearrange("(j c) -> c j", c=P)[0:1, :]),
                      (self.base[0:1, FULL:FULL + 1], dst[FULL * P:FULL * P + 1].rearrange("(r c) -> r c", r=1))]
        with nc.Block() as block:
            @block.gpsimd
            def _(pool):
                nc.gpsimd.iota(self.columns[:], pattern=[[1, P]], base=0, channel_multiplier=0,
                               allow_small_or_imprecise_dtypes=True).then_inc(constants, 1)
                nc.gpsimd.iota(self.partition[:], pattern=[[0, 1]], base=0, channel_multiplier=1,
                               allow_small_or_imprecise_dtypes=True).then_inc(constants, 1)

            @block.vector
            def _(dve):
                nc.vector.memset(raw["src_rows"][:], 0).then_inc(clears, 1)
                nc.vector.memset(raw["dst_rows"][:], -1).then_inc(clears, 1)
                nc.vector.memset(w_rows[:], 0.0).then_inc(clears, 1)
                nc.vector.memset(before[:], -1).then_inc(clears, 1)
                nc.vector.memset(after[:], -1).then_inc(clears, 1)
                nc.vector.memset(self.ones[:], 1.0)
                dve.wait_ge(constants, 2)
                nc.vector.tensor_scalar(self.ident[:], self.columns[:], self.partition[:, 0:1], None, ALU.is_equal)
                for b in range(NB):
                    self.tile_stats(dve, b, x_in, 16)

            @block.sync
            def _(sp):
                sp.dma_start(self.x[:, :, :], a["x"].rearrange("(b p) d -> p b d", p=NT)).then_inc(x_in, 16)
                sp.wait_ge(clears, 5)
                for tile, src in transfers:
                    sp.dma_start(tile, src, allow_slow_non_contiguous=True).then_inc(loads, 16)

        def flags(dve, fill):
            steps = 0

            def link(ins):
                nonlocal steps
                steps += 1
                ins.then_inc(chain, 1)
                fill()
                dve.wait_ge(chain, steps)
            dve.wait_ge(loads, 16 * len(transfers))
            link(nc.vector.tensor_copy(src_f[:], raw["src_rows"][:]))
            link(nc.vector.tensor_copy(dst_f[:], raw["dst_rows"][:]))
            link(nc.vector.tensor_copy(before_f[:], before[:]))
            link(nc.vector.tensor_copy(after_f[:], after[:]))
            link(nc.vector.tensor_tensor(rel[:], dst_f[:], dst_f[:, :, 0:1].to_broadcast([RT, RQ, P]),
                                         ALU.subtract))
            link(nc.vector.tensor_copy(other[:, :, 0:P - 1], dst_f[:, :, 1:P]))
            link(nc.vector.tensor_copy(other[:, :, P - 1:P], after_f[:].unsqueeze(2)))
            link(nc.vector.tensor_tensor(flag[:], dst_f[:], other[:], ALU.not_equal))
            link(nc.vector.scalar_tensor_tensor(out=rel_end[:], in0=rel[:], scalar=1.0, in1=flag[:],
                                                op0=ALU.add, op1=ALU.mult))
            link(nc.vector.tensor_scalar(rel_end[:], rel_end[:], -1.0, None, ALU.add))
            link(nc.vector.tensor_copy(other[:, :, 1:P], dst_f[:, :, 0:P - 1]))
            link(nc.vector.tensor_copy(other[:, :, 0:1], before_f[:].unsqueeze(2)))
            link(nc.vector.tensor_tensor(flag[:], dst_f[:], other[:], ALU.not_equal))
            link(nc.vector.tensor_scalar(other[:], flag[:], -FLT, FLT, ALU.mult, ALU.add))
            link(nc.vector.tensor_scalar(carry[:], flag[:], -1.0, 1.0, ALU.mult, ALU.add))
            link(nc.vector.scalar_tensor_tensor(out=mask[:], in0=flag[:], scalar=-FLT, in1=other[:],
                                                op0=ALU.mult, op1=ALU.add))
            link(nc.vector.tensor_copy(rel16[:], rel[:]))
            link(nc.vector.tensor_scalar(block_i[:], raw["src_rows"][:], P_BITS, None,
                                         ALU.logical_shift_right))
            link(nc.vector.tensor_copy(block16[:], block_i[:]))
            link(nc.vector.tensor_scalar(within_i[:], raw["src_rows"][:], P - 1, None, ALU.bitwise_and))
            link(nc.vector.tensor_copy(within16[:], within_i[:]))
            assert steps == lines_made
            for k, dst in enumerate((self.source, self.place, self.place_end, self.weight)):
                dve.wait_ge(pe, k + 1)
                nc.vector.tensor_copy(dst[:], psT[k][:])

        def turn(t):
            t.wait_ge(chain, lines_made)
            for k, rows in enumerate((src_f, rel, rel_end, w_rows)):
                for q in range(RQ):
                    last = nc.tensor.transpose(psT[k][:, q * RT:(q + 1) * RT], rows[:, q, :],
                                               self.ident[0:RT, 0:RT])
                last.then_inc(pe, 1)

        def store(sp):
            sp.wait_ge(chain, lines_made)
            lines = ((self.mask_line, mask), (self.place_line, rel16), (self.block_line, block16),
                     (self.within_line, within16), (self.carry_line, carry))
            for line, rows in lines:
                sp.dma_start(line.rearrange("(q r c) -> r q c", r=RT, c=P), rows[:]).then_inc(stores, 16)
            sp.wait_ge(stores, 16 * len(lines))
        return flags, turn, store

    def tile_stats(self, dve, b, done, value):
        dve.wait_ge(done, value)
        self.nc.vector.bn_stats(self.stats[:, b, :], self.x[:, b, :]).then_inc(self.stats_made, 1)

    def normalize(self, name):
        nc = self.nc
        chain, root, rstd, made, turned, kept = self.norm_events
        c0, r0, n0 = (self.normalized * k for k in (NB + 2, 1, NB))
        self.normalized += 1
        bufs = 4
        with ExitStack() as ctx:
            mv = self.sb(f"{name}_mv", [NT, NB, 2], ctx=ctx)
            sd = self.sb(f"{name}_sd", [NT, NB], ctx=ctx)
            rs = self.sb(f"{name}_rs", [NT, NB], ctx=ctx)
            nm = self.sb(f"{name}_nm", [NT, NB], ctx=ctx)
            ps = [self.ps(f"{name}_ps{k}", [P, 2, P], ctx) for k in range(bufs)]
            with nc.Block() as block:
                @block.vector
                def _(dve):
                    dve.wait_ge(self.stats_made, n0 + NB)
                    for b in range(NB):
                        nc.vector.bn_aggr(mv[:, b, :], self.stats[:, b, :]).then_inc(chain, 1)
                    dve.wait_ge(chain, c0 + NB)
                    nc.vector.tensor_scalar(sd[:], mv[:, :, 1], EPS, None, ALU.add).then_inc(chain, 1)
                    dve.wait_ge(root, r0 + 1)
                    nc.vector.reciprocal(rs[:], sd[:]).then_inc(chain, 1)
                    dve.wait_ge(chain, c0 + NB + 2)
                    nc.vector.scalar_tensor_tensor(out=nm[:], in0=mv[:, :, 0], scalar=-1.0, in1=rs[:],
                                                   op0=ALU.mult, op1=ALU.mult).then_inc(rstd, 1)
                    for b in range(NB):
                        dve.wait_ge(turned, n0 + b + 1)
                        nc.vector.tensor_copy(self.hT[:, :, b * NT:(b + 1) * NT], ps[b % bufs][:, :, 0:NT]
                                              ).then_inc(kept, 1)

                @block.scalar
                def _(act):
                    act.wait_ge(chain, c0 + NB + 1)
                    nc.scalar.activation(sd[:], sd[:], ACT.Sqrt).then_inc(root, 1)
                    act.wait_ge(rstd, r0 + 1)
                    for b in range(NB):
                        nc.scalar.activation(self.h[:, b, :], self.x[:, b, :], ACT.Relu, scale=rs[:, b:b + 1],
                                             bias=nm[:, b:b + 1]).then_inc(made, 1)

                @block.tensor
                def _(t):
                    for b in range(NB):
                        t.wait_ge(made, n0 + b + 1)
                        if b >= bufs:
                            t.wait_ge(kept, n0 + b + 1 - bufs)
                        for k in range(2):
                            last = nc.tensor.transpose(ps[b % bufs][:, k, 0:NT], self.h[:, b, k * P:(k + 1) * P],
                                                       self.ident[0:NT, 0:NT])
                        last.then_inc(turned, 1)

    def fetch_index(self, sp, index, i, s):
        sp.dma_start(index[:, s:s + PAIR, :], self.source[:, bass.ds(i * (SLOTS * TG) + s * TG, PAIR * TG)].rearrange(
            "p (g t) -> p g t", g=PAIR)).then_inc(self.index_in[s // PAIR], 16)

    def fetch_line(self, sp, line, row, i, s, semaphores=None):
        b = s % BUFS
        sp.dma_start(line[:, b:b + PAIR, :].rearrange("p g e -> p (g e)"),
                     row[bass.ds(i * (SLOTS * GE) + s * GE, PAIR * GE)].partition_broadcast(P)
                     ).then_inc((semaphores or self.line_in)[b // PAIR], 16)

    def one_hots(self, out, places, i, s, half):
        place = places[:, bass.ds(i * (SLOTS * TG) + (s * TG + half * HALF), HALF)]
        return self.nc.vector.tensor_tensor(out[:, half * HALF:(half + 1) * HALF, :],
                                            self.columns[:].unsqueeze(1).to_broadcast([P, HALF, P]),
                                            place.unsqueeze(2).to_broadcast([P, HALF, P]), ALU.is_equal)

    def self_products(self, name, w, loads, loaded, out, addend):
        nc = self.nc
        made, added = self.sem(f"{name}_self_made"), self.sem(f"{name}_self_added")

        def multiply(pe, banks):
            pe.wait_ge(loads, loaded)
            for b in range(NB):
                if b >= len(banks):
                    pe.wait_ge(added, b + 1 - len(banks))
                for k in range(2):
                    last = nc.tensor.matmul(banks[b % len(banks)], self.hT[:, k, b * NT:(b + 1) * NT], w[:, k, :],
                                            start=k == 0, stop=k == 1)
                last.then_inc(made, 1)
            pe.wait_ge(added, NB)

        def add(dve, banks):
            dve.wait_ge(loads, loaded)
            for b in range(NB):
                dve.wait_ge(made, b + 1)
                nc.vector.tensor_tensor(out[:, b, :], banks[b % len(banks)], addend(b), ALU.add).then_inc(added, 1)
        return multiply, add

    def load(self, engine, transfers, sem):
        for tile, source in transfers:
            engine.dma_start(tile, source, allow_slow_non_contiguous=True).then_inc(sem, 16)

    def sum_pass(self, name, table, width, window_table, window_width, attention, ahead=None):
        nc = self.nc
        names = ["nodes_hot", "edges_hot", "expanded", "added", "weighed", "summed"] + (["exps"] if attention else [])
        ev = dict(zip(names, self.events(*names)))
        logit_steps = self.sem("logit_steps") if attention else None
        zeroed = self.sem("exps_zeroed") if attention else None
        tile_added = self.events(*(f"tile_added{t}" for t in range(TG)))
        with ExitStack() as ctx:
            index = self.sb(f"{name}_index", [P, SLOTS, TG], I32, ctx)
            rows = self.sb(f"{name}_rows", [P, SLOTS, TG, width], ctx=ctx)
            line = self.sb(f"{name}_line", [P, BUFS, GE], BF16, ctx)
            kind, parts = (BF16, SPLIT) if attention else (F32, 1)
            window = self.sb(f"{name}_window", [P, BUFS, TG, parts * window_width], kind, ctx)
            by_node = self.sb(f"{name}_by_node", [P, BUFS, GE], kind, ctx)
            by_edge = self.sb(f"{name}_by_edge", [P, BUFS, TG, P], ctx=ctx)
            logit = self.sb(f"{name}_logit", [P, BUFS, TG, H], ctx=ctx)
            exps = self.sb(f"{name}_exps", [P, BUFS, TG, P], ctx=ctx) if attention else None
            blocks = 3 if attention else 2
            ps_window = [self.ps(f"{name}_ps_window{b}", [P, TG, window_width], ctx) for b in range(2)]
            ps_sum = [self.ps(f"{name}_ps_sum{b}", [P, TG, blocks, P], ctx) for b in range(2)]
            with nc.Block() as block:
                @block.sync
                def _(sp):
                    def fetch_index(i, s):
                        if s % PAIR == 0:
                            hold(sp, ev["added"], self.freed(i, s + PAIR - 1, SLOTS))
                            self.fetch_index(sp, index, i, s)

                    def fetch_window(i, s):
                        if s % PAIR == 0:
                            hold(sp, ev["nodes_hot"], self.freed(i, s + PAIR - 1, BUFS))
                            self.fetch_line(sp, line, self.place_line, i, s)
                        hold(sp, ev["expanded"], self.freed(i, s, BUFS))
                        for t, base in enumerate(self.bases(mybir.EngineType.SP, i, s, sp_bases)):
                            sp.dma_start(window[:, s % BUFS, t, :], window_table[bass.ds(base, P), :]
                                         ).then_inc(self.window_in[s % BUFS], 16)
                    sp_bases = []
                    if ahead:
                        self.load(sp, *ahead)
                    pipelined(sp, [(fetch_index, 3), (fetch_window, 0)])

                @block.gpsimd
                def _(pool):
                    if attention:
                        nc.gpsimd.memset(exps[:], 0.0).then_inc(zeroed, 1)

                    def gather(i, s):
                        hold(pool, *self.landed(self.index_in, i, s, groups=PAIR), least=16)
                        hold(pool, ev["summed"], self.freed(i, s, SLOTS))
                        for t in range(TG):
                            nc.gpsimd.indirect_dma_start(
                                rows[:, s, t, :], None, table,
                                bass.IndirectOffsetOnAxis(ap=index[:, s, t:t + 1], axis=0)
                            ).then_inc(self.rows_in[s], 16)
                    pipelined(pool, [(gather, 0)])

                @block.vector
                def _(dve):
                    self.start_events(dve, [ev[k] for k in ("nodes_hot", "edges_hot", "added")] + tile_added)

                    def by_nodes(i, s):
                        dve.wait_ge(*self.landed(self.line_in, i, s, groups=PAIR))
                        nc.vector.tensor_scalar(by_node[:, s % BUFS, :], line[:, s % BUFS, :],
                                                self.partition[:, 0:1], None, ALU.is_equal).then_inc(ev["nodes_hot"], 1)

                    def by_edges(i, s, half):
                        last = self.one_hots(by_edge[:, s % BUFS, :, :], self.place, i, s, half)
                        if half == 1:
                            last.then_inc(ev["edges_hot"], 1)

                    def add(i, s):
                        dve.wait_ge(ev["expanded"], self.ready(i, s))
                        dve.wait_ge(*self.landed(self.rows_in, i, s, TG))
                        nc.vector.tensor_tensor(rows[:, s, :, :], ps_window[s % 2][:], rows[:, s, :, :],
                                                ALU.add).then_inc(ev["added"], 1)

                    def logit_step(i, s, k):
                        return i * (2 * SLOTS) + (2 * s + k + CREDIT)

                    def add_terms(i, s):
                        dve.wait_ge(ev["expanded"], self.ready(i, s))
                        dve.wait_ge(*self.landed(self.rows_in, i, s, TG))
                        nc.vector.tensor_tensor(logit[:, s % BUFS, :, :], rows[:, s, :, D:D + H],
                                                ps_window[s % 2][:, :, 0:H], ALU.add).then_inc(logit_steps, 1)

                    def leak(i, s):
                        dve.wait_ge(logit_steps, logit_step(i, s, 1))
                        at = logit[:, s % BUFS, :, :]
                        nc.vector.scalar_tensor_tensor(out=at, in0=at, scalar=0.2, in1=at, op0=ALU.mult,
                                                       op1=ALU.max).then_inc(logit_steps, 1)

                    def less_largest(i, s):
                        dve.wait_ge(logit_steps, logit_step(i, s, 2))
                        at = logit[:, s % BUFS, :, :]
                        nc.vector.tensor_tensor(at, at, ps_window[s % 2][:, :, H:2 * H],
                                                ALU.subtract).then_inc(ev["added"], 1)

                    held, bases = [], []

                    def accumulate(i, s, t):
                        if t == 0:
                            bases[:] = self.bases(mybir.EngineType.DVE, i, s, held)
                            dve.wait_ge(ev["summed"], self.ready(i, s))
                        self.after_tile_before(dve, tile_added, i, s, t)
                        at = self.aggT[:, 0:blocks, bass.ds(bases[t], P)]
                        nc.vector.tensor_tensor(at, at, ps_sum[s % 2][:, t, :, :], ALU.add
                                                ).then_inc(tile_added[t], 1)

                    def of_tile(stage, t):
                        return lambda i, s: stage(i, s, t)
                    acc = [of_tile(accumulate, t) for t in range(TG)]
                    hot = [of_tile(by_edges, half) for half in range(2)]
                    if attention:
                        dve.sem_inc(logit_steps, CREDIT)
                        pipelined(dve, [(acc[0], 0), (add_terms, 4), (by_nodes, 6), (acc[1], 0), (leak, 4),
                                        (hot[0], 4), (acc[2], 0), (less_largest, 4), (hot[1], 4), (acc[3], 0)])
                    else:
                        pipelined(dve, [(acc[0], 0), (by_nodes, 5), (acc[1], 0), (hot[0], 4), (hot[1], 4), (acc[2], 0),
                                        (add, 3), (acc[3], 0)])

                @block.scalar
                def _(act):
                    if attention:
                        act.wait_ge(zeroed, 1)

                    def relu(i, s):
                        act.wait_ge(ev["added"], self.ready(i, s))
                        nc.scalar.activation(rows[:, s, :, :], rows[:, s, :, :], ACT.Relu).then_inc(ev["weighed"], 1)

                    def exp(i, s):
                        act.wait_ge(ev["added"], self.ready(i, s))
                        act.wait_ge(ev["summed"], self.freed(i, s, BUFS))
                        nc.scalar.activation(exps[:, s % BUFS, :, 0:H], logit[:, s % BUFS, :, :],
                                             ACT.Exp).then_inc(ev["exps"], 1)

                    def weigh(i, s):
                        act.wait_ge(ev["exps"], self.ready(i, s))
                        for t in range(TG):
                            for h in range(H):
                                head = rows[:, s, t, h * HD:(h + 1) * HD]
                                last = nc.scalar.activation(head, head, ACT.Copy, scale=exps[:, s % BUFS, t, h:h + 1])
                        last.then_inc(ev["weighed"], 1)
                    self.start_events(act, [ev["weighed"]] + ([ev["exps"]] if attention else []))
                    pipelined(act, [(exp, 3), (weigh, 2)] if attention else [(relu, 2)])

                @block.tensor
                def _(pe):
                    self.start_events(pe, [ev["expanded"], ev["summed"]])

                    def expand(i, s):
                        pe.wait_ge(ev["nodes_hot"], self.ready(i, s))
                        pe.wait_ge(*self.landed(self.window_in, i, s, TG))
                        pe.wait_ge(ev["added"], self.freed(i, s, 2))
                        for t in range(TG):
                            for k in range(parts):
                                last = nc.tensor.matmul(
                                    ps_window[s % 2][:, t, :], by_node[:, s % BUFS, t * P:(t + 1) * P],
                                    window[:, s % BUFS, t, k * window_width:(k + 1) * window_width],
                                    start=k == 0, stop=k == parts - 1)
                        last.then_inc(ev["expanded"], 1)

                    def gather_sums(i, s):
                        pe.wait_ge(ev["edges_hot"], self.ready(i, s))
                        pe.wait_ge(ev["weighed"], self.ready(i, s))
                        pe.wait_ge(tile_added[TG - 1], self.freed(i, s, 2))
                        for t in range(TG):
                            if attention:
                                nc.tensor.matmul(ps_sum[s % 2][:, t, 2, :], exps[:, s % BUFS, t, :],
                                                 by_edge[:, s % BUFS, t, :], start=True, stop=True)
                            for k in range(2):
                                last = nc.tensor.matmul(ps_sum[s % 2][:, t, k, :], rows[:, s, t, k * P:(k + 1) * P],
                                                        by_edge[:, s % BUFS, t, :], start=True, stop=True)
                        last.then_inc(ev["summed"], 1)
                    pipelined(pe, [(gather_sums, 1), (expand, 5 if attention else 4)])
        self.pass_over(self.index_in, groups=PAIR)
        self.pass_over(self.line_in, groups=PAIR)
        self.pass_over(self.rows_in, TG)
        self.pass_over(self.window_in, TG)
        self.count += CREDIT + NG

    def max_pass(self, name, outT, table=None, ahead=None, first=None):
        nc = self.nc
        attributes = table is None
        nk = 2
        bw = AF + 1 if attributes else D // nk
        source_blocks = 1 if attributes else nk
        names = ["turned", "scanned", "back", "kept", "ends", "placed"] + ([] if attributes else ["weighed"])
        ev = dict(zip(names, self.events(*names)))
        stored = self.events(*(f"stored{t}" for t in range(TG)))
        ones_made = self.sem(f"{name}_ones") if attributes else None
        attributes_in = [self.sem(f"{name}_in{s}") for s in range(SLOTS)] if attributes else None
        carry_in = self.window_in[0:2]
        with ExitStack() as ctx:
            index = None if attributes else self.sb(f"{name}_index", [P, SLOTS, TG], I32, ctx)
            rows = self.sb(f"{name}_rows", [P, SLOTS, TG, source_blocks * bw], ctx=ctx)
            line = self.sb(f"{name}_line", [P, BUFS, GE], BF16, ctx)
            carry = self.sb(f"{name}_carry", [P, BUFS, GE], BF16, ctx) if attributes else None
            scan = self.sb(f"{name}_scan", [bw, 2, nk, GE], ctx=ctx)
            by_edge = self.sb(f"{name}_by_edge", [P, BUFS, TG, nk * bw], ctx=ctx)
            ends = self.sb(f"{name}_ends", [P, BUFS, TG, P], ctx=ctx)
            turned_bufs = 2 // source_blocks
            ps_turned = [[self.ps(f"{name}_ps_turned{b}{k}", [bw, GE], ctx) for k in range(source_blocks)]
                         for b in range(turned_bufs)]
            ps_back = self.ps(f"{name}_ps_back", [P, TG, BANK // 2], ctx)
            ps_placed = [self.ps(f"{name}_ps_placed{b}", [bw, TG, nk, P], ctx) for b in range(2)]
            banks = None if attributes else [
                ps[0:NT, t, :, :].rearrange("p k n -> p (k n)") for ps in ps_placed for t in (0, HALF)]
            with nc.Block() as block:
                @block.sync
                def _(sp):
                    def mask(i, s):
                        if s % PAIR == 0:
                            hold(sp, ev["scanned"], self.freed(i, s + PAIR - 1, BUFS))
                            self.fetch_line(sp, line, self.mask_line, i, s)
                            if attributes:
                                self.fetch_line(sp, carry, self.carry_line, i, s, carry_in)

                    def fetch_index(i, s):
                        if s % PAIR == 0:
                            hold(sp, ev["turned"], self.freed(i, s + PAIR - 1, SLOTS))
                            self.fetch_index(sp, index, i, s)

                    def fetch_attributes(i, s):
                        hold(sp, ev["placed"], self.freed(i, s, SLOTS))
                        if isinstance(i, int) and i == NI - 1 and s == SLOTS - 1:
                            left = FULL - (NG - 1) * TG
                            src = self.a["edge_attr_96"]
                            sp.dma_start(rows[:, s, 0:left, 0:AF], src[(FULL - left) * P:FULL * P, :].rearrange(
                                "(t p) f -> p t f", p=P)).then_inc(attributes_in[s], 16)
                            sp.dma_start(rows[0:REST, s, left, 0:AF], src[FULL * P:E, :]).then_inc(
                                attributes_in[s], 16)
                        else:
                            sp.dma_start(rows[:, s, :, 0:AF], self.a["edge_attr_96"][
                                bass.ds(i * (SLOTS * GE) + s * GE, GE), :].rearrange("(t p) f -> p t f", p=P)
                            ).then_inc(attributes_in[s], 16)
                    pipelined(sp, [(fetch_attributes if attributes else fetch_index, 3), (mask, 0)])

                if attributes:
                    @block.gpsimd
                    def _(pool):
                        nc.gpsimd.memset(rows[:, :, :, AF:AF + 1], 1.0).then_inc(ones_made, 1)
                        if ahead:
                            self.load(pool, *ahead)

                if not attributes:
                    @block.gpsimd
                    def _(pool):
                        def gather(i, s):
                            hold(pool, *self.landed(self.index_in, i, s, groups=PAIR), least=16)
                            hold(pool, ev["turned"], self.freed(i, s, SLOTS))
                            for t in range(TG):
                                nc.gpsimd.indirect_dma_start(
                                    rows[:, s, t, :], None, table,
                                    bass.IndirectOffsetOnAxis(ap=index[:, s, t:t + 1], axis=0)
                                ).then_inc(self.rows_in[s], 16)
                        pipelined(pool, [(gather, 0)])

                def rows_landed(eng, i, s):
                    if not attributes:
                        eng.wait_ge(*self.landed(self.rows_in, i, s, TG))
                    else:
                        sem, value = self.landed(attributes_in, i, s)
                        last = isinstance(i, int) and i == NI - 1 and s == SLOTS - 1
                        eng.wait_ge(sem, value + 16 if last else value)

                def keep(eng, copy, first, tiles):
                    def stage(i, s):
                        if first == 0:
                            eng.wait_ge(ev["back"], self.ready(i, s))
                            eng.wait_ge(ev["placed"], self.freed(i, s, BUFS))
                        some = slice(first, first + tiles)
                        last = copy(by_edge[:, s % BUFS, some, :], ps_back[:, some, 0:nk * bw])
                        if first + tiles == TG:
                            last.then_inc(ev["kept"], 1)
                    return stage

                @block.scalar
                def _(act):
                    self.start_events(act, [ev["kept"] if attributes else ev["weighed"]] + stored)

                    def weigh(i, s, t):
                        if t == 0:
                            rows_landed(act, i, s)
                        w = self.weight[:, bass.ds(i * (SLOTS * TG) + (s * TG + t), 1)]
                        last = nc.scalar.activation(rows[:, s, t, :], rows[:, s, t, :], ACT.Copy, scale=w)
                        if t == TG - 1:
                            last.then_inc(ev["weighed"], 1)

                    held, bases = [], []

                    def store(i, s, t):
                        if t == 0:
                            bases[:] = self.bases(mybir.EngineType.Activation, i, s, held)
                            act.wait_ge(ev["placed"], self.ready(i, s))
                        self.after_tile_before(act, stored, i, s, t)
                        nc.scalar.copy(outT[:, :, bass.ds(bases[t], P)], ps_placed[s % 2][:, t, :, :]
                                       ).then_inc(stored[t], 1)

                    def of_tile(stage, t):
                        return lambda i, s: stage(i, s, t)
                    stages = []
                    for t in range(TG):
                        stages.append((of_tile(store, t), 0))
                        if not attributes:
                            stages.append((of_tile(weigh, t), 5))
                    if attributes:
                        stages.insert(1, (keep(act, nc.scalar.copy, 0, HALF), 2))
                        stages.insert(3, (keep(act, nc.scalar.copy, HALF, HALF), 2))
                    pipelined(act, stages)

                @block.vector
                def _(dve):
                    self.start_events(dve, [ev["ends"]] + ([] if attributes else [ev["kept"]]))
                    if first:
                        first[1](dve, banks)

                    def one_hots(i, s, half):
                        if half == 0:
                            dve.wait_ge(ev["placed"], self.freed(i, s, BUFS))
                        last = self.one_hots(ends[:, s % BUFS, :, :], self.place_end, i, s, half)
                        if half == 1:
                            last.then_inc(ev["ends"], 1)

                    def run_scan(i, s):
                        dve.wait_ge(*self.landed(self.line_in, i, s, groups=PAIR))
                        dve.wait_ge(ev["turned"], self.ready(i, s))
                        dve.wait_ge(ev["scanned"], self.freed(i, s, 1))
                        if attributes:
                            dve.wait_ge(*self.landed(carry_in, i, s, groups=PAIR))
                        for k in range(nk):
                            sums = attributes and k == 1
                            last = nc.vector.tensor_tensor_scan(
                                scan[:, s % 2, k, :], (carry if sums else line)[0:bw, s % BUFS, :],
                                ps_turned[s % turned_bufs][k % source_blocks][:],
                                scan[:, 1 - s % 2, k, GE - 1:GE], *((ALU.mult, ALU.add) if sums else (ALU.min, ALU.max)))
                        last.then_inc(ev["scanned"], 1)

                    def of_tile(stage, t):
                        return lambda i, s: stage(i, s, t)
                    hot = [of_tile(one_hots, half) for half in range(2)]
                    nc.vector.memset(scan[:, 1, :, GE - 1:GE], 0.0).then_inc(
                        ev["scanned"], self.credit(ev["scanned"]))
                    if attributes:
                        pipelined(dve, [(run_scan, 3), (hot[0], 2), (hot[1], 2)])
                    else:
                        pipelined(dve, [(run_scan, 3), (hot[0], 2), (hot[1], 2), (keep(dve, nc.vector.tensor_copy, 0, TG), 2)])

                @block.tensor
                def _(pe):
                    self.start_events(pe, [ev["turned"], ev["back"], ev["placed"]])
                    if first:
                        first[0](pe, banks)
                    if attributes:
                        pe.wait_ge(ones_made, 1)

                    def turn(i, s):
                        if attributes:
                            rows_landed(pe, i, s)
                        else:
                            pe.wait_ge(ev["weighed"], self.ready(i, s))
                        pe.wait_ge(ev["scanned"], self.freed(i, s, turned_bufs))
                        for k in range(source_blocks):
                            for t in range(TG):
                                last = nc.tensor.transpose(ps_turned[s % turned_bufs][k][:, t * P:(t + 1) * P],
                                                           rows[:, s, t, k * bw:(k + 1) * bw], self.ident[:])
                        last.then_inc(ev["turned"], 1)

                    def turn_back(i, s):
                        hold(pe, ev["scanned"], self.ready(i, s))
                        hold(pe, ev["kept"], self.freed(i, s, 1))
                        for t in range(TG):
                            for k in range(nk):
                                last = nc.tensor.transpose(ps_back[:, t, k * bw:(k + 1) * bw],
                                                           scan[:, s % 2, k, t * P:(t + 1) * P],
                                                           self.ident[0:bw, 0:bw])
                        last.then_inc(ev["back"], 1)

                    def put(i, s):
                        pe.wait_ge(ev["kept"], self.ready(i, s))
                        pe.wait_ge(ev["ends"], self.ready(i, s))
                        pe.wait_ge(stored[TG - 1], self.freed(i, s, 2))
                        for t in range(TG):
                            for k in range(nk):
                                last = nc.tensor.matmul(ps_placed[s % 2][:, t, k, :],
                                                        by_edge[:, s % BUFS, t, k * bw:(k + 1) * bw],
                                                        ends[:, s % BUFS, t, :], start=True, stop=True)
                        last.then_inc(ev["placed"], 1)
                    pipelined(pe, [(turn_back, 2), (put, 1), (turn, 4)])
        self.pass_over(self.line_in, groups=PAIR)
        if attributes:
            self.pass_over(carry_in, groups=PAIR)
        else:
            self.pass_over(self.index_in, groups=PAIR)
            self.pass_over(self.rows_in, TG)
        self.count += CREDIT + NG

    def logit_pass(self, largestT):
        nc = self.nc
        LH = LB * H
        names = ["hot", "looked", "masked", "picked", "scanned", "back", "kept", "ends", "placed"]
        ev = dict(zip(names, self.events(*names)))
        stored = self.events(*(f"stored{t}" for t in range(TG)))
        marks, made, chain, parted = (self.sem(f"logit_{k}") for k in ("marks", "made", "chain", "parted"))
        within_in, block_in = self.window_in[0:2], self.window_in[2:4]
        with ExitStack() as ctx:
            within = self.sb("logit_within", [P, BUFS, GE], BF16, ctx)
            blocks = self.sb("logit_blocks", [P, BUFS, GE], BF16, ctx)
            line = self.sb("logit_line", [P, BUFS, GE], BF16, ctx)
            hot = self.sb("logit_hot", [P, 2, GE], BF16, ctx)
            rest = self.sb("logit_rest", [P, LH], ctx=ctx)
            lookup = self.sb("logit_lookup", [P, SPLIT, LH], BF16, ctx)
            masked = self.sb("logit_masked", [LH, 2, GE], ctx=ctx)
            scan = self.sb("logit_scan", [H, 2, GE], ctx=ctx)
            by_edge = self.sb("logit_by_edge", [P, BUFS, TG, H], ctx=ctx)
            ends = self.sb("logit_ends", [P, BUFS, TG, P], ctx=ctx)
            row_i, row_block_i, row_head_i = (self.sb(f"logit_{k}", [LH, 1], I32, ctx) for k in (
                "row_i", "row_block_i", "row_head_i"))
            row_block, row_head = (self.sb(f"logit_{k}", [LH, 1], ctx=ctx) for k in ("row_block", "row_head"))
            own = self.sb("logit_own", [LH, H], ctx=ctx)
            ps_looked = [self.ps(f"logit_ps_looked{b}", [LH, GE], ctx) for b in range(2)]
            ps_picked = [self.ps(f"logit_ps_picked{b}", [H, GE], ctx) for b in range(2)]
            ps_back = [self.ps(f"logit_ps_back{b}", [P, TG, H], ctx) for b in range(2)]
            ps_placed = [self.ps(f"logit_ps_placed{b}", [H, TG, P], ctx) for b in range(2)]
            with nc.Block() as block:
                @block.sync
                def _(sp):
                    def fetch_pair(tile, row, semaphores, used):
                        def stage(i, s):
                            if s % PAIR == 0:
                                hold(sp, used, self.freed(i, s + PAIR - 1, BUFS))
                                self.fetch_line(sp, tile, row, i, s, semaphores)
                        return stage
                    pipelined(sp, [(fetch_pair(within, self.within_line, within_in, ev["hot"]), 4),
                                   (fetch_pair(blocks, self.block_line, block_in, ev["masked"]), 2),
                                   (fetch_pair(line, self.mask_line, self.line_in, ev["scanned"]), 0)])

                @block.gpsimd
                def _(pool):
                    nc.gpsimd.iota(row_i[:], pattern=[[0, 1]], base=0, channel_multiplier=1).then_inc(marks, 1)

                @block.vector
                def _(dve):
                    self.start_events(dve, [ev[k] for k in ("hot", "masked", "scanned", "ends")])
                    dve.wait_ge(marks, 1)
                    nc.vector.tensor_scalar(row_block_i[:], row_i[:], H_BITS, None, ALU.logical_shift_right
                                            ).then_inc(chain, 1)
                    nc.vector.tensor_scalar(row_head_i[:], row_i[:], H - 1, None, ALU.bitwise_and).then_inc(chain, 1)
                    dve.wait_ge(chain, 2)
                    nc.vector.tensor_copy(row_block[:], row_block_i[:]).then_inc(chain, 1)
                    nc.vector.tensor_copy(row_head[:], row_head_i[:]).then_inc(chain, 1)
                    dve.wait_ge(chain, 4)
                    nc.vector.tensor_scalar(own[:], self.columns[0:LH, 0:H], row_head[:, 0:1], None, ALU.is_equal
                                            ).then_inc(made, 1)
                    nc.vector.memset(scan[:, 1, GE - 1:GE], 0.0).then_inc(chain, 1)
                    dve.wait_ge(chain, 5)
                    self.split(dve, parted, self.lookup[:].rearrange("p b h -> p (b h)"), rest[:],
                               [lookup[:, k, :] for k in range(SPLIT)])

                    def place_within(i, s):
                        dve.wait_ge(*self.landed(within_in, i, s, groups=PAIR))
                        nc.vector.tensor_scalar(hot[:, s % 2, :], within[:, s % BUFS, :], self.partition[:, 0:1],
                                                None, ALU.is_equal).then_inc(ev["hot"], 1)

                    def mask(i, s):
                        dve.wait_ge(*self.landed(block_in, i, s, groups=PAIR))
                        dve.wait_ge(ev["looked"], self.ready(i, s))
                        dve.wait_ge(ev["picked"], self.freed(i, s, 2))
                        nc.vector.scalar_tensor_tensor(out=masked[:, s % 2, :], in0=blocks[0:LH, s % BUFS, :],
                                                       scalar=row_block[:, 0:1], in1=ps_looked[s % 2][:],
                                                       op0=ALU.is_equal, op1=ALU.mult).then_inc(ev["masked"], 1)

                    def run_scan(i, s):
                        dve.wait_ge(*self.landed(self.line_in, i, s, groups=PAIR))
                        dve.wait_ge(ev["picked"], self.ready(i, s))
                        dve.wait_ge(ev["scanned"], self.freed(i, s, 1))
                        nc.vector.tensor_tensor_scan(scan[:, s % 2, :], line[0:H, s % BUFS, :], ps_picked[s % 2][:],
                                                     scan[:, 1 - s % 2, GE - 1:GE], ALU.min, ALU.max
                                                     ).then_inc(ev["scanned"], 1)

                    def last_edges(i, s, half):
                        if half == 0:
                            dve.wait_ge(ev["placed"], self.freed(i, s, BUFS))
                        last = self.one_hots(ends[:, s % BUFS, :, :], self.place_end, i, s, half)
                        if half == 1:
                            last.then_inc(ev["ends"], 1)
                    pipelined(dve, [(run_scan, 3), (lambda i, s: last_edges(i, s, 0), 2), (mask, 5),
                                    (lambda i, s: last_edges(i, s, 1), 2), (place_within, 7)])

                @block.scalar
                def _(act):
                    self.start_events(act, [ev["kept"]] + stored)
                    held, bases = [], []

                    def keep(i, s):
                        act.wait_ge(ev["back"], self.ready(i, s))
                        act.wait_ge(ev["placed"], self.freed(i, s, BUFS))
                        nc.scalar.copy(by_edge[:, s % BUFS, :, :], ps_back[s % 2][:]).then_inc(ev["kept"], 1)

                    def store(t):
                        def stage(i, s):
                            if t == 0:
                                bases[:] = self.bases(mybir.EngineType.Activation, i, s, held)
                                act.wait_ge(ev["placed"], self.ready(i, s))
                            self.after_tile_before(act, stored, i, s, t)
                            nc.scalar.copy(largestT[:, 0, bass.ds(bases[t], P)], ps_placed[s % 2][:, t, :]
                                           ).then_inc(stored[t], 1)
                        return stage
                    pipelined(act, [(store(0), 0), (keep, 2), (store(1), 0), (store(2), 0), (store(3), 0)])

                @block.tensor
                def _(pe):
                    self.start_events(pe, [ev[k] for k in ("looked", "picked", "back", "placed")])
                    pe.wait_ge(made, 1)
                    pe.wait_ge(parted, 2 * SPLIT - 1)

                    def look(i, s):
                        pe.wait_ge(ev["hot"], self.ready(i, s))
                        pe.wait_ge(ev["masked"], self.freed(i, s, 2))
                        for k in range(SPLIT):
                            last = nc.tensor.matmul(ps_looked[s % 2][:], lookup[:, k, :], hot[:, s % 2, :],
                                                    start=k == 0, stop=k == SPLIT - 1)
                        last.then_inc(ev["looked"], 1)

                    def pick(i, s):
                        pe.wait_ge(ev["masked"], self.ready(i, s))
                        pe.wait_ge(ev["scanned"], self.freed(i, s, 2))
                        nc.tensor.matmul(ps_picked[s % 2][:], own[:], masked[:, s % 2, :], start=True, stop=True
                                         ).then_inc(ev["picked"], 1)

                    def turn_back(i, s):
                        hold(pe, ev["scanned"], self.ready(i, s))
                        hold(pe, ev["kept"], self.freed(i, s, 2))
                        for t in range(TG):
                            last = nc.tensor.transpose(ps_back[s % 2][:, t, :], scan[:, s % 2, t * P:(t + 1) * P],
                                                       self.ident[0:H, 0:H])
                        last.then_inc(ev["back"], 1)

                    def put(i, s):
                        pe.wait_ge(ev["kept"], self.ready(i, s))
                        pe.wait_ge(ev["ends"], self.ready(i, s))
                        pe.wait_ge(stored[TG - 1], self.freed(i, s, 2))
                        for t in range(TG):
                            last = nc.tensor.matmul(ps_placed[s % 2][:, t, :], by_edge[:, s % BUFS, t, :],
                                                    ends[:, s % BUFS, t, :], start=True, stop=True)
                        last.then_inc(ev["placed"], 1)
                    pipelined(pe, [(turn_back, 2), (put, 1), (pick, 4), (look, 6)])
        for semaphores in (self.line_in, within_in, block_in):
            self.pass_over(semaphores, groups=PAIR)
        self.count += CREDIT + NG

    def row(self, vector, parts=NT):
        return vector.partition_broadcast(parts)

    def message_tables(self, flags, turn, store):
        nc, a = self.nc, self.a
        self.source_table = nc.dram_tensor("message_source_table", [N, D], F32).ap()
        self.window_table = nc.dram_tensor("message_window_table", [WN, D], F32).ap()
        loads, made, copied, biased, stores, clear = (self.sem(f"msg_{k}") for k in (
            "loads", "made", "copied", "biased", "stores", "clear"))
        with ExitStack() as ctx:
            w = self.sb("msg_w", [P, 2, 2 * D], ctx=ctx)
            bias = self.sb("msg_bias", [NT, D], ctx=ctx)
            out = self.sb("msg_out", [NT, NB, 2 * D], ctx=ctx)
            zero = self.sb("msg_zero", [P, D], ctx=ctx)
            ps_source = [self.ps(f"msg_table_ps_s{k}", [NT, D], ctx) for k in range(2)]
            ps_window = [self.ps(f"msg_table_ps_w{k}", [NT, D], ctx) for k in range(2)]
            with nc.Block() as block:
                @block.sync
                def _(sp):
                    for half in range(2):
                        sp.dma_start(w[:, :, half * D:(half + 1) * D],
                                     a["L0_gnn_W_msg"][half * D:(half + 1) * D, :].rearrange("(k p) n -> p k n", p=P)
                                     ).then_inc(loads, 16)
                    sp.dma_start(bias[:], self.row(a["L0_gnn_b_msg"])).then_inc(loads, 16)
                    sp.wait_ge(clear, 1)
                    sp.dma_start(self.window_table[N:WN, :], zero[:]).then_inc(stores, 16)
                    for b in range(NB):
                        sp.wait_ge(copied, b + 1)
                        sp.dma_start(self.source_table[b * NT:(b + 1) * NT, :], out[:, b, 0:D]).then_inc(stores, 16)
                        sp.wait_ge(biased, b + 1)
                        sp.dma_start(self.window_table[b * NT:(b + 1) * NT, :], out[:, b, D:2 * D]).then_inc(stores, 16)
                    store(sp)
                    sp.wait_ge(stores, 16 * (2 * NB + 1))

                @block.gpsimd
                def _(pool):
                    nc.gpsimd.memset(zero[:], 0.0).then_inc(clear, 1)
                    nc.gpsimd.memset(self.aggT[:], 0.0)

                @block.tensor
                def _(pe):
                    pe.wait_ge(loads, 48)
                    for b in range(NB):
                        if b >= 2:
                            pe.wait_ge(copied, b - 1)
                            pe.wait_ge(biased, b - 1)
                        for half, ps in enumerate((ps_source, ps_window)):
                            for k in range(2):
                                last = nc.tensor.matmul(ps[b % 2][:], self.hT[:, k, b * NT:(b + 1) * NT],
                                                        w[:, k, half * D:(half + 1) * D], start=k == 0, stop=k == 1)
                        last.then_inc(made, 1)
                        if b == NB - 3:
                            turn(pe)

                @block.scalar
                def _(act):
                    for b in range(NB):
                        act.wait_ge(made, b + 1)
                        nc.scalar.copy(out[:, b, 0:D], ps_source[b % 2][:]).then_inc(copied, 1)

                @block.vector
                def _(dve):
                    dve.wait_ge(loads, 48)
                    b = 0

                    def add_bias():
                        nonlocal b
                        if b < NB:
                            dve.wait_ge(made, b + 1)
                            nc.vector.tensor_tensor(out[:, b, D:2 * D], ps_window[b % 2][:], bias[:],
                                                    ALU.add).then_inc(biased, 1)
                            b += 1
                    flags(dve, add_bias)
                    while b < NB:
                        add_bias()

    def update_weights(self, layer):
        a = self.a
        w = self.sb("upd_w", [P, 4, D], ctx=layer)
        bias, gamma, beta = (self.sb(f"upd_{k}", [NT, D], ctx=layer) for k in ("bias", "gamma", "beta"))
        transfers = [(w[:], a["L0_gnn_W_upd"].rearrange("(k p) n -> p k n", p=P))] + [
            (tile[:], self.row(a[f"L0_gnn_{k}"])) for tile, k in ((bias, "b_upd"), (gamma, "gamma"), (beta, "beta"))]
        return (w, bias, gamma, beta), (transfers, self.sem("upd_loads"))

    def message_update(self, weights, transfers, loads):
        nc = self.nc
        w, bias, gamma, beta = weights
        loaded = 16 * len(transfers)
        made, biased, relued, stats, aggregated, shifted, root, inverted, moved, scaled, based, gained, added = (
            self.sem(f"upd_{k}") for k in (
                "made", "biased", "relued", "stats", "aggregated", "shifted", "root", "inverted", "moved",
                "scaled", "based", "gained", "added"))
        parts = [range(b, b + PART) for b in range(0, NB, PART)]
        bufs = 6
        u = self.h
        with ExitStack() as ctx:
            st = self.sb("upd_st", [NT, NB, 6], ctx=ctx)
            mv = self.sb("upd_mv", [NT, NB, 2], ctx=ctx)
            sd, rs, nm = (self.sb(f"upd_{k}", [NT, NB], ctx=ctx) for k in ("sd", "rs", "nm"))
            ps = [self.ps(f"upd_ps{k}", [NT, D], ctx) for k in range(bufs)]
            with nc.Block() as block:
                @block.tensor
                def _(pe):
                    pe.wait_ge(loads, loaded)
                    for b in range(NB):
                        if b >= bufs:
                            pe.wait_ge(biased, b + 1 - bufs)
                        for k in range(4):
                            src = self.hT if k < 2 else self.aggT
                            last = nc.tensor.matmul(ps[b % bufs][:], src[:, k % 2, b * NT:(b + 1) * NT], w[:, k, :],
                                                    start=k == 0, stop=k == 3)
                        last.then_inc(made, 1)

                @block.scalar
                def _(act):
                    for c in range(len(parts) + 1):
                        if c < len(parts):
                            for b in parts[c]:
                                act.wait_ge(biased, b + 1)
                                nc.scalar.activation(u[:, b, :], u[:, b, :], ACT.Relu).then_inc(relued, 1)
                        if c > 0:
                            act.wait_ge(shifted, c)
                            of = slice(parts[c - 1].start, parts[c - 1].stop)
                            nc.scalar.activation(sd[:, of], sd[:, of], ACT.Sqrt).then_inc(root, 1)
                            act.wait_ge(moved, c)
                            for b in parts[c - 1]:
                                nc.scalar.activation(u[:, b, :], u[:, b, :], ACT.Identity, scale=rs[:, b:b + 1],
                                                     bias=nm[:, b:b + 1]).then_inc(scaled, 1)

                @block.gpsimd
                def _(pool):
                    pool.wait_ge(loads, loaded)
                    for of in parts:
                        rows = slice(of.start, of.stop)
                        nc.gpsimd.tensor_tensor(self.x[:, rows, :], self.x[:, rows, :],
                                                beta[:].unsqueeze(1).to_broadcast([NT, PART, D]),
                                                ALU.add).then_inc(based, 1)
                    for b in range(NB):
                        pool.wait_ge(scaled, b + 1)
                        nc.gpsimd.tensor_tensor(u[:, b, :], u[:, b, :], gamma[:], ALU.mult).then_inc(gained, 1)

                @block.vector
                def _(dve):
                    dve.wait_ge(loads, loaded)

                    def activations(b):
                        if b < NB:
                            dve.wait_ge(made, b + 1)
                            nc.vector.tensor_tensor(u[:, b, :], ps[b % bufs][:], bias[:], ALU.add).then_inc(biased, 1)
                        if b > 0:
                            dve.wait_ge(relued, b)
                            nc.vector.bn_stats(st[:, b - 1, :], u[:, b - 1, :]).then_inc(stats, 1)

                    def variances(c):
                        of = slice(parts[c].start, parts[c].stop)
                        for b in parts[c]:
                            dve.wait_ge(stats, b + 1)
                            nc.vector.bn_aggr(mv[:, b, :], st[:, b, :]).then_inc(aggregated, 1)
                        dve.wait_ge(aggregated, of.stop)
                        nc.vector.tensor_scalar(sd[:, of], mv[:, of, 1], EPS, None, ALU.add).then_inc(shifted, 1)

                    def scales(c):
                        of = slice(parts[c].start, parts[c].stop)
                        dve.wait_ge(root, c + 1)
                        nc.vector.reciprocal(rs[:, of], sd[:, of]).then_inc(inverted, 1)
                        dve.wait_ge(inverted, c + 1)
                        nc.vector.scalar_tensor_tensor(out=nm[:, of], in0=mv[:, of, 0], scalar=-1.0, in1=rs[:, of],
                                                       op0=ALU.mult, op1=ALU.mult).then_inc(moved, 1)

                    def residual(c):
                        for b in parts[c]:
                            dve.wait_ge(based, c + 1)
                            dve.wait_ge(gained, b + 1)
                            nc.vector.tensor_tensor(self.x[:, b, :], self.x[:, b, :], u[:, b, :], ALU.add
                                                    ).then_inc(added, 1)
                            if b > 0:
                                self.tile_stats(dve, b - 1, added, b)
                    for c in range(len(parts) + 2):
                        if c < len(parts):
                            for b in parts[c]:
                                activations(b)
                        if c == len(parts):
                            activations(NB)
                        if 0 < c <= len(parts):
                            variances(c - 1)
                            scales(c - 1)
                        if c > 1:
                            residual(c - 2)
                    self.tile_stats(dve, NB - 1, added, NB)

    def mlp_weights(self, layer):
        a = self.a
        w1 = self.sb("mlp_w1", [P, 6, HID], ctx=layer)
        w2 = self.sb("mlp_w2", [P, HID // P, D], ctx=layer)
        b1 = self.sb("mlp_b1", [P, HID // P], ctx=layer)
        b2 = self.sb("mlp_b2", [NT, D], ctx=layer)
        u0 = self.sb("mlp_u0", [U, 1], ctx=layer)
        parts = [(0, P), (P, P), (D, AF), (D + AF, AF), (D + 2 * AF, AF), (D + 3 * AF, U)]
        transfers = [(w1[0:n, k, :], a["L1_gnn_W1"][r:r + n, :]) for k, (r, n) in enumerate(parts)]
        transfers += [(w2[:], a["L1_gnn_W2"].rearrange("(k p) n -> p k n", p=P)),
                      (b1[:], a["L1_gnn_b1"].rearrange("(k p) -> p k", p=P)),
                      (b2[:], self.row(a["L1_gnn_b2"])), (u0[:], a["L1_gnn_u"][0:1, :].rearrange("o f -> f o"))]
        return (w1, w2, b1, b2, u0, parts), (transfers, self.sem("mlp_loads"))

    def mlp(self, edgesT, weights, transfers, loads):
        w1, w2, b1, b2, u0, parts = weights
        loaded = 16 * len(transfers)
        nc, a = self.nc, self.a
        maxT, sums = edgesT[0:AF, 0, :], edgesT[:, 1, :]
        chain, spread, graph, b1_made, hidden, relued, outer, added, based = (self.sem(f"mlp_{k}") for k in (
            "chain", "spread", "graph", "b1_made", "hidden", "relued", "outer", "added", "based"))
        HB = HID // P
        with ExitStack() as ctx:
            hid = self.sb("mlp_hid", [P, HB, CH], ctx=ctx)
            mean = self.sb("mlp_mean", [AF, N], ctx=ctx)
            pick = self.sb("mlp_pick", [AF + 1, AF], ctx=ctx)
            ps_g = self.ps("mlp_ps_g", [P, HB], ctx)
            ps_h = [self.ps(f"mlp_ps_h{k}", [P, 512], ctx) for k in range(3)]
            ps_o = [self.ps(f"mlp_ps_o{k}", [NT, D], ctx) for k in range(2)]
            ps_c = [self.ps(f"mlp_ps_c{k}", [AF, 512], ctx) for k in range(2)]
            with nc.Block() as block:
                @block.gpsimd
                def _(pool):
                    nc.gpsimd.tensor_tensor(self.x[:], self.x[:], self.h[:], ALU.add).then_inc(based, 1)
                    pool.wait_ge(loads, loaded)
                    pool.wait_ge(based, 1)
                    nc.gpsimd.tensor_tensor(self.x[:], self.x[:], b2[:].unsqueeze(1).to_broadcast([NT, NB, D]),
                                            ALU.add).then_inc(based, 1)

                @block.vector
                def _(dve):
                    nc.vector.tensor_scalar(pick[:], self.ones[0:AF + 1, 0:AF], self.partition[0:AF + 1, 0:1],
                                            float(AF), ALU.mult, ALU.is_equal).then_inc(chain, 1)
                    def means(c):
                        c0, cn = CHUNKS[c]
                        cnt = mean[:, c0:c0 + cn]
                        dve.wait_ge(spread, c + 1)
                        nc.vector.tensor_scalar(cnt, ps_c[c % 2][:, 0:cn], 1.0, None, ALU.max).then_inc(chain, 1)
                        dve.wait_ge(chain, 3 * c + 2)
                        nc.vector.reciprocal(cnt, cnt).then_inc(chain, 1)
                        dve.wait_ge(chain, 3 * c + 3)
                        nc.vector.tensor_tensor(cnt, cnt, sums[0:AF, c0:c0 + cn], ALU.mult).then_inc(chain, 1)
                    means(0)
                    dve.wait_ge(graph, 1)
                    nc.vector.tensor_tensor(b1[:], b1[:], ps_g[:], ALU.add).then_inc(b1_made, 1)
                    dve.wait_ge(based, 2)
                    for c, (c0, cn) in enumerate(CHUNKS):
                        if c + 1 < len(CHUNKS):
                            means(c + 1)
                        for b in range(c0 // NT, (c0 + cn) // NT):
                            dve.wait_ge(outer, b + 1)
                            nc.vector.tensor_tensor(self.x[:, b, :], self.x[:, b, :], ps_o[b % 2][:], ALU.add
                                                    ).then_inc(added, 1)
                            if b > 0:
                                self.tile_stats(dve, b - 1, added, b)
                    self.tile_stats(dve, NB - 1, added, NB)

                @block.scalar
                def _(act):
                    act.wait_ge(b1_made, 1)
                    n = 0
                    for c, (c0, cn) in enumerate(CHUNKS):
                        for k in range(HB):
                            act.wait_ge(hidden, n + 1)
                            if c > 0 and k == 0:
                                act.wait_ge(outer, CH // NT * c)
                            nc.scalar.activation(hid[:, k, 0:cn], ps_h[n % 3][:, 0:cn], ACT.Relu,
                                                 bias=b1[:, k:k + 1]).then_inc(relued, 1)
                            n += 1

                @block.tensor
                def _(pe):
                    pe.wait_ge(loads, loaded)
                    for k in range(HB):
                        last = nc.tensor.matmul(ps_g[:, k:k + 1], w1[0:U, 5, k * P:(k + 1) * P], u0[:],
                                                start=True, stop=True)
                    last.then_inc(graph, 1)
                    pe.wait_ge(chain, 1)
                    def spread_counts(c):
                        c0, cn = CHUNKS[c]
                        if c >= 2:
                            pe.wait_ge(chain, 3 * (c - 2) + 2)
                        nc.tensor.matmul(ps_c[c % 2][:, 0:cn], pick[:], sums[:, c0:c0 + cn],
                                         start=True, stop=True).then_inc(spread, 1)
                    spread_counts(0)
                    n = b = 0
                    for c, (c0, cn) in enumerate(CHUNKS):
                        if c + 1 < len(CHUNKS):
                            spread_counts(c + 1)
                        moving = [self.hT[:, 0, c0:c0 + cn], self.hT[:, 1, c0:c0 + cn], sums[0:AF, c0:c0 + cn],
                                  maxT[:, c0:c0 + cn], mean[:, c0:c0 + cn]]
                        for k in range(HB):
                            if n >= 3:
                                pe.wait_ge(relued, n - 2)
                            for j, m in enumerate(moving):
                                if k == 0 and j == len(moving) - 1:
                                    pe.wait_ge(chain, 3 * c + 4)
                                last = nc.tensor.matmul(ps_h[n % 3][:, 0:cn], w1[0:parts[j][1], j, k * P:(k + 1) * P],
                                                        m, start=j == 0, stop=j == len(moving) - 1)
                            last.then_inc(hidden, 1)
                            n += 1
                        pe.wait_ge(relued, n)
                        for t in range(cn // NT):
                            if b >= 2:
                                pe.wait_ge(added, b - 1)
                            for k in range(HB):
                                last = nc.tensor.matmul(ps_o[b % 2][:], hid[:, k, t * NT:(t + 1) * NT], w2[:, k, :],
                                                        start=k == 0, stop=k == HB - 1)
                            last.then_inc(outer, 1)
                            b += 1

    def attention_tables(self):
        nc, a = self.nc, self.a
        AW = D + H
        folds_made = 0
        self.attention_table = nc.dram_tensor("att_table", [N, AW], F32).ap()
        loads, clears, marks, chain, turned, folded, rhs, made, kept, dmade, dkept, lmade, stores = (
            self.sem(f"att_{k}") for k in ("loads", "clears", "marks", "chain", "turned", "folded", "rhs", "made",
                                           "kept", "dmade", "dkept", "lmade", "stores"))
        with ExitStack() as ctx:
            wc = self.sb("att_wc", [P, 2, D], ctx=ctx)
            wp = self.sb("att_wp", [U, P], ctx=ctx)
            av = self.sb("att_av", [P, 2, 2], ctx=ctx)
            ap = self.sb("att_ap", [U, 2], ctx=ctx)
            comb = self.sb("att_comb", [P, H, 2], ctx=ctx)
            own = self.sb("att_own", [P, 2, H], ctx=ctx)
            own_b = self.sb("att_own_b", [P, 2, H], ctx=ctx)
            own_p = self.sb("att_own_p", [U, H], ctx=ctx)
            own_pb = self.sb("att_own_pb", [U, H], ctx=ctx)
            fold = self.sb("att_fold", [P, 2, 2, H], ctx=ctx)
            fold_p = self.sb("att_fold_p", [U, 2, H], ctx=ctx)
            w = self.sb("att_w", [P, 2, D + 2 * H], ctx=ctx)
            out = self.sb("att_out", [NT, NB, AW], ctx=ctx)
            ps_t = self.ps("att_ps_t", [P, 2, 2, P], ctx)
            ps_v = self.ps("att_ps_v", [P, 2, 2 * H], ctx)
            ps = [self.ps(f"att_ps{k}", [NT, D + 2 * H], ctx) for k in range(2)]
            ps_d = [self.ps(f"att_ps_d{k}", [H, 512], ctx) for k in range(2)]
            ps_l = self.ps("att_ps_l", [P, LB, H], ctx)
            with nc.Block() as block:
                @block.sync
                def _(sp):
                    sp.wait_ge(clears, 2)
                    sp.dma_start(wc[:, :, 0:CD], a["L2_gnn_Wc"].rearrange("(k p) n -> p k n", p=P)).then_inc(loads, 16)
                    sp.dma_start(wp[:, P - POS:P], a["L2_gnn_Wp"]).then_inc(loads, 16)
                    for k, name in enumerate(("src", "dst")):
                        sp.dma_start(av[:, :, k:k + 1], a[f"L2_gnn_attn_{name}"].rearrange(
                            "o (k g) d -> (g d) k o", k=2), allow_slow_non_contiguous=True).then_inc(loads, 16)
                        sp.dma_start(ap[:, k:k + 1], a[f"L2_gnn_pos_attn_{name}"].rearrange("o h d -> (h d) o"),
                                     allow_slow_non_contiguous=True).then_inc(loads, 16)
                    sp.dma_start(comb[:], a["L2_gnn_att_comb"].partition_broadcast(P)).then_inc(loads, 16)
                    for b in range(NB):
                        sp.wait_ge(kept, b + 1)
                        sp.dma_start(self.attention_table[b * NT:(b + 1) * NT, :], out[:, b, :]).then_inc(stores, 16)
                    sp.wait_ge(stores, 16 * NB)

                @block.gpsimd
                def _(pool):
                    nc.gpsimd.memset(wc[:], 0.0).then_inc(clears, 1)
                    nc.gpsimd.memset(wp[:], 0.0).then_inc(clears, 1)
                    nc.gpsimd.memset(self.lookup[:], 0.0).then_inc(clears, 1)
                    nc.gpsimd.iota(own[:], pattern=[[P, 2], [-HD, H]], base=0, channel_multiplier=1,
                                   allow_small_or_imprecise_dtypes=True).then_inc(marks, 1)
                    nc.gpsimd.iota(own_p[:], pattern=[[-POS, H]], base=0, channel_multiplier=1,
                                   allow_small_or_imprecise_dtypes=True).then_inc(marks, 1)
                    nc.gpsimd.memset(self.aggT[:], 0.0)

                @block.vector
                def _(dve):
                    nonlocal folds_made
                    steps = 0

                    def link(ins):
                        nonlocal steps
                        steps += 1
                        ins.then_inc(chain, 1)
                        dve.wait_ge(chain, steps)
                    dve.wait_ge(marks, 2)
                    for dist, less, size in ((own, own_b, HD), (own_p, own_pb, POS)):
                        link(nc.vector.tensor_scalar(less[:], dist[:], float(size), None, ALU.is_lt))
                        link(nc.vector.tensor_scalar(dist[:], dist[:], 0.0, None, ALU.is_ge))
                        link(nc.vector.tensor_tensor(dist[:], dist[:], less[:], ALU.mult))
                    dve.wait_ge(loads, 16 * 7)
                    for blk in range(2):
                        link(nc.vector.tensor_tensor(own_b[:, blk, :], own[:, blk, :], comb[:, :, 0], ALU.mult))
                        for k in range(2):
                            link(nc.vector.tensor_scalar(fold[:, blk, k, :], own_b[:, blk, :], av[:, blk, k:k + 1],
                                                         None, ALU.mult))
                    link(nc.vector.tensor_tensor(own_pb[:], own_p[:], comb[0:U, :, 1], ALU.mult))
                    for k in range(2):
                        link(nc.vector.tensor_scalar(fold_p[:, k, :], own_pb[:], ap[:, k:k + 1], None, ALU.mult))
                    folds_made = steps
                    dve.wait_ge(turned, 1)
                    nc.vector.tensor_copy(w[:, :, 0:D], ps_t[:].rearrange("p i f n -> p i (f n)")).then_inc(rhs, 1)
                    dve.wait_ge(folded, 1)
                    nc.vector.tensor_copy(w[:, :, D:D + 2 * H], ps_v[:]).then_inc(rhs, 1)
                    for c, (c0, cn) in enumerate(CHUNKS):
                        dve.wait_ge(dmade, c + 1)
                        nc.vector.tensor_copy(self.dstT[:, c0:c0 + cn], ps_d[c % 2][:, 0:cn]).then_inc(dkept, 1)
                    dve.wait_ge(clears, 3)
                    dve.wait_ge(lmade, 1)
                    whole = N // P
                    nc.vector.tensor_copy(self.lookup[:, 0:whole, :], ps_l[:, 0:whole, :])
                    nc.vector.tensor_copy(self.lookup[0:N - whole * P, whole, :], ps_l[0:N - whole * P, whole, :])

                @block.tensor
                def _(pe):
                    pe.wait_ge(loads, 16 * 7)
                    for i in range(2):
                        for f in range(2):
                            last = nc.tensor.transpose(ps_t[:, i, f, :], wc[:, f, i * P:(i + 1) * P], self.ident[:])
                    last.then_inc(turned, 1)
                    pe.wait_ge(chain, folds_made)
                    for i in range(2):
                        for f in range(2):
                            last = nc.tensor.matmul(ps_v[:, i, :], wc[:, f, i * P:(i + 1) * P],
                                                    fold[:, f, :, :].rearrange("p k h -> p (k h)"),
                                                    start=f == 0, stop=i == 0 and f == 1)
                    nc.tensor.matmul(ps_v[:, 1, :], wp[:], fold_p[:].rearrange("p k h -> p (k h)"),
                                     start=False, stop=True).then_inc(folded, 1)
                    pe.wait_ge(rhs, 2)
                    for b in range(NB):
                        if b >= 2:
                            pe.wait_ge(kept, b - 1)
                        for k in range(2):
                            last = nc.tensor.matmul(ps[b % 2][:], self.hT[:, k, b * NT:(b + 1) * NT], w[:, k, :],
                                                    start=k == 0, stop=k == 1)
                        last.then_inc(made, 1)
                    for c, (c0, cn) in enumerate(CHUNKS):
                        if c >= 2:
                            pe.wait_ge(dkept, c - 1)
                        for k in range(2):
                            last = nc.tensor.matmul(ps_d[c % 2][:, 0:cn], w[:, k, D + H:D + 2 * H],
                                                    self.hT[:, k, c0:c0 + cn], start=k == 0, stop=k == 1)
                        last.then_inc(dmade, 1)
                    for b in range(LB):
                        n = min(P, N - b * P)
                        for k in range(2):
                            last = nc.tensor.matmul(ps_l[0:n, b, :], self.hT[:, k, b * P:b * P + n], w[:, k, D:D + H],
                                                    start=k == 0, stop=k == 1)
                    last.then_inc(lmade, 1)

                @block.scalar
                def _(act):
                    for b in range(NB):
                        act.wait_ge(made, b + 1)
                        nc.scalar.copy(out[:, b, :], ps[b % 2][:, 0:AW]).then_inc(kept, 1)

    def logit_table(self, largestT):
        nc = self.nc
        self.logit_rows = nc.dram_tensor("logit_window_table", [WN, SPLIT * 2 * H], BF16).ap()
        chain, made, parted, kept, clear, stores = (self.sem(f"log_{k}") for k in (
            "chain", "made", "parted", "kept", "clear", "stores"))
        with ExitStack() as ctx:
            value = self.sb("log_value", [NT, NB, 2 * H], ctx=ctx)
            rest = self.sb("log_rest", [NT, NB, 2 * H], ctx=ctx)
            out = self.sb("log_out", [NT, NB, SPLIT, 2 * H], BF16, ctx)
            zero = self.sb("log_zero", [P, SPLIT * 2 * H], BF16, ctx)
            ps = self.ps("log_ps", [NT, NB, 2 * H], ctx)
            with nc.Block() as block:
                @block.gpsimd
                def _(pool):
                    nc.gpsimd.memset(zero[:], 0.0).then_inc(clear, 1)

                @block.vector
                def _(dve):
                    m, d = largestT[:, 0, 0:N], self.dstT[:, 0:N]
                    nc.vector.tensor_tensor(m, m, d, ALU.add).then_inc(chain, 1)
                    dve.wait_ge(chain, 1)
                    nc.vector.scalar_tensor_tensor(out=m, in0=m, scalar=0.2, in1=m, op0=ALU.mult,
                                                   op1=ALU.max).then_inc(chain, 1)
                    dve.wait_ge(made, 1)
                    nc.vector.tensor_copy(value[:], ps[:]).then_inc(kept, 1)
                    dve.wait_ge(kept, 1)
                    self.split(dve, parted, value[:], rest[:], [out[:, :, k, :] for k in range(SPLIT)])

                @block.tensor
                def _(pe):
                    pe.wait_ge(chain, 2)
                    for b in range(NB):
                        nodes = slice(b * NT, (b + 1) * NT)
                        nc.tensor.transpose(ps[:, b, 0:H], self.dstT[:, nodes], self.ident[0:H, 0:H])
                        last = nc.tensor.transpose(ps[:, b, H:2 * H], largestT[:, 0, nodes], self.ident[0:H, 0:H])
                    last.then_inc(made, 1)

                @block.sync
                def _(sp):
                    sp.wait_ge(clear, 1)
                    sp.dma_start(self.logit_rows[N:WN, :], zero[:]).then_inc(stores, 16)
                    sp.wait_ge(parted, 2 * SPLIT - 1)
                    sp.dma_start(self.logit_rows[0:N, :].rearrange("(b p) k -> p b k", p=NT),
                                 out[:].rearrange("p b k h -> p b (k h)")).then_inc(stores, 16)
                    sp.wait_ge(stores, 32)

    def attention_update(self):
        nc = self.nc
        inverted, turned_den, turned, divided, added, based = (self.sem(f"fin_{k}") for k in (
            "inverted", "turned_den", "turned", "divided", "added", "based"))
        with ExitStack() as ctx:
            inv = self.sb("fin_inv", [NT, NB, H], ctx=ctx)
            share = self.sb("fin_share", [NT, 2, D], ctx=ctx)
            ps_den = self.ps("fin_ps_den", [NT, NB, H], ctx)
            ps = [self.ps(f"fin_ps{k}", [NT, D], ctx) for k in range(4)]
            with nc.Block() as block:
                @block.gpsimd
                def _(pool):
                    for b in range(0, NB, PART):
                        nc.gpsimd.tensor_tensor(self.x[:, b:b + PART, :], self.x[:, b:b + PART, :],
                                                self.h[:, b:b + PART, :], ALU.add).then_inc(based, 1)

                @block.vector
                def _(dve):
                    dve.wait_ge(turned_den, 1)
                    nc.vector.tensor_scalar(inv[:], ps_den[:], 1e-30, None, ALU.max).then_inc(inverted, 1)
                    dve.wait_ge(inverted, 1)
                    nc.vector.reciprocal(inv[:], inv[:]).then_inc(inverted, 1)
                    dve.wait_ge(inverted, 2)
                    for b in range(NB + 1):
                        if b < NB:
                            dve.wait_ge(turned, b + 1)
                            if b >= 2:
                                dve.wait_ge(added, b - 1)
                            nc.vector.tensor_tensor(share[:, b % 2, :].rearrange("p (h d) -> p h d", h=H),
                                                    ps[b % 4][:].rearrange("p (h d) -> p h d", h=H),
                                                    inv[:, b, :].unsqueeze(2).to_broadcast([NT, H, HD]),
                                                    ALU.mult).then_inc(divided, 1)
                        if b > 0:
                            dve.wait_ge(divided, b)
                            dve.wait_ge(based, (b - 1) // PART + 1)
                            nc.vector.tensor_tensor(self.x[:, b - 1, :], self.x[:, b - 1, :], share[:, (b - 1) % 2, :],
                                                    ALU.add).then_inc(added, 1)
                        if b > 1:
                            self.tile_stats(dve, b - 2, added, b - 1)
                    self.tile_stats(dve, NB - 1, added, NB)

                @block.tensor
                def _(pe):
                    for b in range(NB):
                        last = nc.tensor.transpose(ps_den[:, b, :], self.denomT[:, b * NT:(b + 1) * NT],
                                                   self.ident[0:H, 0:H])
                    last.then_inc(turned_den, 1)
                    for b in range(NB):
                        if b >= 4:
                            pe.wait_ge(divided, b - 3)
                        for k in range(2):
                            last = nc.tensor.transpose(ps[b % 4][:, k * P:(k + 1) * P],
                                                       self.aggT[:, k, b * NT:(b + 1) * NT], self.ident[:])
                        last.then_inc(turned, 1)

    def pool_table(self):
        nc, a = self.nc, self.a
        loads, turned, kept, made, added, relued, stores = (self.sem(f"pool_{k}") for k in (
            "loads", "turned", "kept", "made", "added", "relued", "stores"))
        self.pool_kept = kept
        names = ("pool", "self", "neigh")
        self.wT = {k: self.sb(f"w_{k}T", [P, 2, D]) for k in names}
        with ExitStack() as ctx:
            raw = self.sb("pool_raw", [P, 3, 2, D], ctx=ctx)
            bias = self.sb("pool_bias", [NT, D], ctx=ctx)
            out = self.sb("pool_out", [NT, NB, D], ctx=ctx)
            ps_t = [self.ps(f"pool_ps_t{k}", [P, 2, 2, P], ctx) for k in range(3)]
            ps = [self.ps(f"pool_ps{k}", [NT, D], ctx) for k in range(2)]
            with nc.Block() as block:
                @block.sync
                def _(sp):
                    for k, name in enumerate(names):
                        sp.dma_start(raw[:, k, :, :], a[f"L3_gnn_W_{name}"].rearrange("(k p) n -> p k n", p=P)
                                     ).then_inc(loads, 16)
                    sp.dma_start(bias[:], self.row(a["L3_gnn_b_pool"])).then_inc(loads, 16)
                    for b in range(NB):
                        sp.wait_ge(relued, b + 1)
                        sp.dma_start(self.source_table[b * NT:(b + 1) * NT, :], out[:, b, :]).then_inc(stores, 16)
                    sp.wait_ge(stores, 16 * NB)

                @block.tensor
                def _(pe):
                    pe.wait_ge(loads, 64)
                    for k in range(3):
                        for i in range(2):
                            for o in range(2):
                                last = nc.tensor.transpose(ps_t[k][:, i, o, :], raw[:, k, o, i * P:(i + 1) * P],
                                                           self.ident[:])
                        last.then_inc(turned, 1)
                    pe.wait_ge(kept, 1)
                    for b in range(NB):
                        if b >= 2:
                            pe.wait_ge(added, b - 1)
                        for k in range(2):
                            last = nc.tensor.matmul(ps[b % 2][:], self.hT[:, k, b * NT:(b + 1) * NT],
                                                    self.wT["pool"][:, k, :], start=k == 0, stop=k == 1)
                        last.then_inc(made, 1)

                @block.vector
                def _(dve):
                    for k, name in enumerate(names):
                        dve.wait_ge(turned, k + 1)
                        nc.vector.tensor_copy(self.wT[name][:], ps_t[k][:].rearrange("p i o n -> p i (o n)")
                                              ).then_inc(kept, 1)
                    dve.wait_ge(loads, 64)
                    for b in range(NB):
                        dve.wait_ge(made, b + 1)
                        nc.vector.tensor_tensor(out[:, b, :], ps[b % 2][:], bias[:], ALU.add).then_inc(added, 1)

                @block.scalar
                def _(act):
                    for b in range(NB):
                        act.wait_ge(added, b + 1)
                        nc.scalar.activation(out[:, b, :], out[:, b, :], ACT.Relu).then_inc(relued, 1)

    def pool_update(self):
        nc, a = self.nc, self.a
        loads, made, biased, added, stores = (self.sem(f"out_{k}") for k in (
            "loads", "made", "biased", "added", "stores"))
        with ExitStack() as ctx:
            b_self, b_neigh = (self.sb(f"out_{k}", [NT, D], ctx=ctx) for k in ("b_self", "b_neigh"))
            ps = [self.ps(f"out_ps{k}", [NT, D], ctx) for k in range(6)]
            with nc.Block() as block:
                @block.sync
                def _(sp):
                    sp.dma_start(b_self[:], self.row(a["L3_gnn_b_self"])).then_inc(loads, 16)
                    sp.dma_start(b_neigh[:], self.row(a["L3_gnn_b_neigh"])).then_inc(loads, 16)
                    for b in range(NB):
                        sp.wait_ge(added, b + 1)
                        sp.dma_start(self.out[b * NT:(b + 1) * NT, :], self.x[:, b, :]).then_inc(stores, 16)
                    sp.wait_ge(stores, 16 * NB)

                @block.gpsimd
                def _(pool):
                    pool.wait_ge(loads, 32)
                    nc.gpsimd.tensor_tensor(b_self[:], b_self[:], b_neigh[:], ALU.add).then_inc(biased, 1)
                    pool.wait_ge(biased, 1)
                    for b in range(0, NB, PART):
                        nc.gpsimd.tensor_tensor(self.x[:, b:b + PART, :], self.x[:, b:b + PART, :],
                                                b_self[:].unsqueeze(1).to_broadcast([NT, PART, D]),
                                                ALU.add).then_inc(biased, 1)

                @block.tensor
                def _(pe):
                    for b in range(NB):
                        if b >= 6:
                            pe.wait_ge(added, b - 5)
                        for k in range(2):
                            last = nc.tensor.matmul(ps[b % 6][:], self.aggT[:, k, b * NT:(b + 1) * NT],
                                                    self.wT["neigh"][:, k, :], start=k == 0, stop=k == 1)
                        last.then_inc(made, 1)

                @block.vector
                def _(dve):
                    for b in range(NB):
                        dve.wait_ge(biased, b // PART + 2)
                        dve.wait_ge(made, b + 1)
                        nc.vector.tensor_tensor(self.x[:, b, :], self.x[:, b, :], ps[b % 6][:], ALU.add
                                                ).then_inc(added, 1)


def build(nc, a, out):
    with ExitStack() as ctx:
        k = Kernel(nc, ctx, a, out)
        with ExitStack() as edges:
            parts = k.prepare(edges)
            k.normalize("norm0")
            k.message_tables(*parts)
        with ExitStack() as layer:
            weights, ahead = k.update_weights(layer)
            k.sum_pass("msg", k.source_table, D, k.window_table, D, attention=False, ahead=ahead)
            k.message_update(weights, *ahead)
        k.normalize("norm1")
        with ExitStack() as layer:
            edgesT = k.aggT[0:AF + 1, 0:2, :]
            weights, ahead = k.mlp_weights(layer)
            k.max_pass("attr", edgesT, ahead=ahead)
            k.mlp(edgesT, weights, *ahead)
        k.normalize("norm2")
        with ExitStack() as layer:
            k.dstT = k.sb("dstT", [H, N], ctx=layer)
            largestT = k.sb("largestT", [H, 1, WN], ctx=layer)
            k.lookup = k.sb("lookup", [P, LB, H], ctx=layer)
            k.attention_tables()
            k.logit_pass(largestT)
            k.logit_table(largestT)
            k.sum_pass("att", k.attention_table, D + H, k.logit_rows, 2 * H, attention=True)
            k.attention_update()
        k.normalize("norm3")
        k.pool_table()
        first = k.self_products("pool", k.wT["self"], k.pool_kept, 3, k.x, lambda b: k.x[:, b, :])
        k.max_pass("pool_max", k.aggT[:, 0:2, :], table=k.source_table, first=first)
        k.pool_update()


_INS = ["x", "src", "dst", "edge_attr_96", "edge_weight1",
        "L0_gnn_W_msg", "L0_gnn_b_msg", "L0_gnn_W_upd", "L0_gnn_b_upd", "L0_gnn_gamma", "L0_gnn_beta",
        "L1_gnn_u", "L1_gnn_W1", "L1_gnn_b1", "L1_gnn_W2", "L1_gnn_b2",
        "L2_gnn_Wc", "L2_gnn_Wp", "L2_gnn_attn_src", "L2_gnn_attn_dst", "L2_gnn_pos_attn_src",
        "L2_gnn_pos_attn_dst", "L2_gnn_att_comb",
        "L3_gnn_W_pool", "L3_gnn_b_pool", "L3_gnn_W_self", "L3_gnn_b_self", "L3_gnn_W_neigh", "L3_gnn_b_neigh"]


def kernel(**inputs):
    import numpy as _np
    import concourse.bacc as _bacc
    from concourse import mybir as _mybir
    from concourse.bass_utils import run_bass_kernel_spmd as _run

    nc = _bacc.Bacc("TRN2", target_bir_lowering=False, num_devices=1)
    arrays, aps = {}, {}
    for name in _INS:
        arr = _np.ascontiguousarray(inputs[name])
        arrays[f"in_{name}"] = arr
        aps[name] = nc.dram_tensor(f"in_{name}", arr.shape, _mybir.dt.from_np(arr.dtype), kind="ExternalInput").ap()
    out = nc.dram_tensor("out_x", (N, D), F32, kind="ExternalOutput").ap()
    build(nc, aps, out)
    r = _run(nc, [arrays], core_ids=[0])
    return r.results[0]["out_x"]
```
